# Optimizing a Trainium2 kernel written in Bass

```python
import numpy as np
import jax
import jax.numpy as jnp

def _softmax(x, axis=-1):
    return jax.nn.softmax(x, axis=axis)

def _gelu(x):
    return jax.nn.gelu(x, approximate=True)

def _silu(x):
    return jax.nn.silu(x)

def _sigmoid(x):
    return jax.nn.sigmoid(x)

def _layernorm(x, axis=-1, eps=1e-05):
    m = jnp.mean(x, axis=axis, keepdims=True)
    v = jnp.var(x, axis=axis, keepdims=True)
    return (x - m) / jnp.sqrt(v + eps)

def _scatter_add(tgt, idx, src, axis=0):
    return tgt.at[idx].add(src)

def _segment_sum(src, seg, n):
    return jax.ops.segment_sum(src, seg, n)
kernel_name = 'mk_audio_tower_d2_tok_aud1d256_r4_25022c'

def setup_inputs(seed: int=0):
    np.random.seed(seed)
    _w = jnp.asarray

    def _rec_inputs():
        import jax
        import jax.numpy as jnp
        _rk = jax.random.key(seed)
        x = -0.000292821 + 1.00034 * jax.random.normal(jax.random.fold_in(_rk, 1), (64, 8192), jnp.float32)
        return x
    x = _rec_inputs()

    def _L0_tok_setup():
        import jax, jax.numpy as jnp
        import numpy as np
        EPS = 1e-05

        def _conv1d(x, W, b, stride, pad):
            y = jax.lax.conv_general_dilated(x, W, (stride,), [(pad, pad)], dimension_numbers=('NCH', 'OIH', 'NCH'))
            return y + b[None, :, None]

        def _bn(x, g, b, m, v):
            return (x - m[None, :, None]) * (g * jax.lax.rsqrt(v + EPS))[None, :, None] + b[None, :, None]

        def _maxpool(x, k):
            B, C, L = x.shape
            return x.reshape(B, C, L // k, k).max(axis=-1)

        def _self_attn(x, Wq, bq, Wk, bk, Wv, bv, gamma):
            q = jnp.einsum('oc,bcl->bol', Wq, x) + bq[None, :, None]
            k = jnp.einsum('oc,bcl->bol', Wk, x) + bk[None, :, None]
            v = jnp.einsum('oc,bcl->bol', Wv, x) + bv[None, :, None]
            energy = jnp.einsum('bci,bcj->bij', q, k)
            attn = jax.nn.softmax(energy, axis=-1)
            out = jnp.einsum('bcj,bij->bci', v, attn)
            return gamma * out + x
        key = jax.random.key(seed)
        ks = jax.random.split(key, 32)
        B, D = (128, 8192)
        r = lambda i, shape, s=0.1: jax.random.normal(ks[i], shape, jnp.float32) * s
        return {'x': jax.random.normal(ks[0], (B, D), jnp.float32), 'w1': r(1, (16, 2, 3)), 'b1': r(2, (16,)), 'g1': 1.0 + r(3, (16,)), 'be1': r(4, (16,)), 'm1': r(5, (16,)), 'v1': 0.5 + jax.random.uniform(ks[6], (16,), jnp.float32), 'w2': r(7, (64, 16, 3)), 'b2': r(8, (64,)), 'g2': 1.0 + r(9, (64,)), 'be2': r(10, (64,)), 'm2': r(11, (64,)), 'v2': 0.5 + jax.random.uniform(ks[12], (64,), jnp.float32), 'wq': r(13, (8, 64)), 'bq': r(14, (8,)), 'wk': r(15, (8, 64)), 'bk': r(16, (8,)), 'wv': r(17, (64, 64)), 'bv': r(18, (64,)), 'gamma': jnp.float32(0.7), 'w3': r(19, (128, 64, 4)), 'b3': r(20, (128,)), 'g3': 1.0 + r(21, (128,)), 'be3': r(22, (128,)), 'm3': r(23, (128,)), 'v3': 0.5 + jax.random.uniform(ks[24], (128,), jnp.float32)}
    _L0_tok_all = _L0_tok_setup()
    _L0_tok_in = {k: v for k, v in _L0_tok_all.items() if k in ('w1', 'b1', 'g1', 'be1', 'm1', 'v1', 'w2', 'b2', 'g2', 'be2', 'm2', 'v2', 'wq', 'bq', 'wk', 'bk', 'wv', 'bv', 'gamma', 'w3', 'b3', 'g3', 'be3', 'm3', 'v3')}
    del _L0_tok_all

    def _L0_attn_setup():
        import jax, jax.numpy as jnp
        import numpy as np
        B, N, DIM = (8, 2048, 64)
        HEADS, LOCAL_HEADS, WINDOW = (8, 1, 64)
        HD = DIM // HEADS
        MLP_HIDDEN = 256
        EPS = 1e-05

        def layer_norm(x, g, b):
            mu = jnp.mean(x, axis=-1, keepdims=True)
            var = jnp.var(x, axis=-1, keepdims=True)
            return (x - mu) * jax.lax.rsqrt(var + EPS) * g + b

        def look_around(t, pad_value=0.0):
            nw = t.shape[1]
            pads = [(0, 0), (1, 1)] + [(0, 0)] * (t.ndim - 2)
            p = jnp.pad(t, pads, constant_values=pad_value)
            return jnp.concatenate([p[:, i:i + nw] for i in range(3)], axis=2)

        def local_attn(q, k, v):
            b, n, d = q.shape
            nw = n // WINDOW
            scale = d ** (-0.5)
            bq = q.reshape(b, nw, WINDOW, d) * scale
            bk = look_around(k.reshape(b, nw, WINDOW, d))
            bv = look_around(v.reshape(b, nw, WINDOW, d))
            ticker = jnp.arange(n).reshape(1, nw, WINDOW)
            bq_k = look_around(ticker, pad_value=-1)
            pad_mask = (bq_k == -1)[:, :, None, :]
            dots = jnp.einsum('bnie,bnje->bnij', bq, bk)
            dots = jnp.where(pad_mask, -1000000000.0, dots)
            attn = jax.nn.softmax(dots, axis=-1)
            out = jnp.einsum('bnij,bnje->bnie', attn, bv)
            return out.reshape(b, n, d)

        def linear_attn(q, k, v):
            d = q.shape[-1]
            qs = jax.nn.softmax(q, axis=-1) * d ** (-0.5)
            ks = jax.nn.softmax(k, axis=-2)
            ctx = jnp.einsum('bhnd,bhne->bhde', ks, v)
            return jnp.einsum('bhnd,bhde->bhne', qs, ctx)
        key = jax.random.key(seed)
        ks = jax.random.split(key, 8)
        s = 0.02
        return {'x': jax.random.normal(ks[0], (B, N, DIM), jnp.float32), 'norm1_g': jnp.ones((DIM,), jnp.float32), 'norm1_b': jnp.zeros((DIM,), jnp.float32), 'Wq': jax.random.normal(ks[1], (DIM, DIM), jnp.float32) * s, 'Wkv': jax.random.normal(ks[2], (DIM, DIM), jnp.float32) * s, 'Wproj': jax.random.normal(ks[3], (DIM, DIM), jnp.float32) * s, 'bproj': jnp.zeros((DIM,), jnp.float32), 'norm2_g': jnp.ones((DIM,), jnp.float32), 'norm2_b': jnp.zeros((DIM,), jnp.float32), 'W1': jax.random.normal(ks[4], (MLP_HIDDEN, DIM), jnp.float32) * s, 'b1': jnp.zeros((MLP_HIDDEN,), jnp.float32), 'W2': jax.random.normal(ks[5], (DIM, MLP_HIDDEN), jnp.float32) * s, 'b2': jnp.zeros((DIM,), jnp.float32)}
    _L0_attn_all = _L0_attn_setup()
    _L0_attn_in = {k: v for k, v in _L0_attn_all.items() if k in ('norm1_g', 'norm1_b', 'Wq', 'Wkv', 'Wproj', 'bproj', 'norm2_g', 'norm2_b', 'W1', 'b1', 'W2', 'b2')}
    del _L0_attn_all

    def _L0_ffn_setup():
        import jax, jax.numpy as jnp
        import numpy as np
        B, S, H, F, E, K = (8, 1024, 64, 128, 16, 2)
        EPS = 1e-05
        key = jax.random.key(seed)
        ks = jax.random.split(key, 9)
        sc = 0.02
        return {'x': jax.random.normal(ks[0], (B, S, H), dtype=jnp.float32), 'gate_w': jax.random.normal(ks[1], (H, E), dtype=jnp.float32) * sc, 'gate_b': jnp.zeros((E,), dtype=jnp.float32), 'w1': jax.random.normal(ks[2], (E, H, F), dtype=jnp.float32) * sc, 'b1': jnp.zeros((E, F), dtype=jnp.float32), 'w2': jax.random.normal(ks[3], (E, F, H), dtype=jnp.float32) * sc, 'b2': jnp.zeros((E, H), dtype=jnp.float32), 'gamma': jnp.ones((H,), dtype=jnp.float32), 'beta': jnp.zeros((H,), dtype=jnp.float32)}
    _L0_ffn_all = _L0_ffn_setup()
    _L0_ffn_in = {k: v for k, v in _L0_ffn_all.items() if k in ('gate_w', 'gate_b', 'w1', 'b1', 'w2', 'b2', 'gamma', 'beta')}
    del _L0_ffn_all

    def _L1_attn_setup():
        import jax, jax.numpy as jnp
        import numpy as np
        IN_C = 64
        HID_C = 64
        HEADS = 8
        SCALE = 1.0 / np.sqrt(HID_C / HEADS).astype(np.float32)
        key = jax.random.key(seed)
        k_v, k_q, k_k, k_w, k_o, k_b = jax.random.split(key, 6)
        B, S = (4, 512)
        lim_in = 1.0 / np.sqrt(IN_C)
        lim_out = 1.0 / np.sqrt(IN_C * HEADS)
        v = jax.random.normal(k_v, (B, S, IN_C), dtype=jnp.float32)
        WQ = jax.random.uniform(k_q, (IN_C, IN_C * HEADS), jnp.float32, -lim_in, lim_in)
        WK = jax.random.uniform(k_k, (IN_C, IN_C * HEADS), jnp.float32, -lim_in, lim_in)
        WV = jax.random.uniform(k_w, (IN_C, IN_C * HEADS), jnp.float32, -lim_in, lim_in)
        Wout = jax.random.uniform(k_o, (IN_C * HEADS, HID_C), jnp.float32, -lim_out, lim_out)
        bout = jax.random.uniform(k_b, (HID_C,), jnp.float32, -lim_out, lim_out)
        return {'v': v, 'WQ': WQ, 'WK': WK, 'WV': WV, 'Wout': Wout, 'bout': bout}
    _L1_attn_all = _L1_attn_setup()
    _L1_attn_in = {k: v for k, v in _L1_attn_all.items() if k in ('WQ', 'WK', 'WV', 'Wout', 'bout')}
    del _L1_attn_all

    def _L1_ffn_setup():
        import jax, jax.numpy as jnp
        import numpy as np
        B, K, D = (128, 16, 64)
        E = 32
        H = int(D * 0.25)
        key = jax.random.key(seed)
        ks = jax.random.split(key, 7)
        d_rs = D ** (-0.5)
        h_rs = H ** (-0.5)
        x = jax.random.normal(ks[0], (B, K, D), dtype=jnp.float32)
        router_w = jax.random.uniform(ks[1], (E, D), jnp.float32, -d_rs, d_rs)
        router_b = jax.random.uniform(ks[2], (E,), jnp.float32, -d_rs, d_rs)
        W1 = jax.random.uniform(ks[3], (E, D, H), jnp.float32, -h_rs, h_rs)
        b1 = jax.random.uniform(ks[4], (E, H), jnp.float32, -h_rs, h_rs)
        W2 = jax.random.uniform(ks[5], (E, H, D), jnp.float32, -d_rs, d_rs)
        b2 = jax.random.uniform(ks[6], (E, D), jnp.float32, -d_rs, d_rs)
        return {'x': x, 'router_w': router_w, 'router_b': router_b, 'W1': W1, 'b1': b1, 'W2': W2, 'b2': b2}
    _L1_ffn_all = _L1_ffn_setup()
    _L1_ffn_in = {k: v for k, v in _L1_ffn_all.items() if k in ('router_w', 'router_b', 'W1', 'b1', 'W2', 'b2')}
    del _L1_ffn_all
    return {'x': x, 'L0_tok_w1': _L0_tok_in['w1'], 'L0_tok_b1': _L0_tok_in['b1'], 'L0_tok_g1': _L0_tok_in['g1'], 'L0_tok_be1': _L0_tok_in['be1'], 'L0_tok_m1': _L0_tok_in['m1'], 'L0_tok_v1': _L0_tok_in['v1'], 'L0_tok_w2': _L0_tok_in['w2'], 'L0_tok_b2': _L0_tok_in['b2'], 'L0_tok_g2': _L0_tok_in['g2'], 'L0_tok_be2': _L0_tok_in['be2'], 'L0_tok_m2': _L0_tok_in['m2'], 'L0_tok_v2': _L0_tok_in['v2'], 'L0_tok_wq': _L0_tok_in['wq'], 'L0_tok_bq': _L0_tok_in['bq'], 'L0_tok_wk': _L0_tok_in['wk'], 'L0_tok_bk': _L0_tok_in['bk'], 'L0_tok_wv': _L0_tok_in['wv'], 'L0_tok_bv': _L0_tok_in['bv'], 'L0_tok_gamma': _L0_tok_in['gamma'], 'L0_tok_w3': _L0_tok_in['w3'], 'L0_tok_b3': _L0_tok_in['b3'], 'L0_tok_g3': _L0_tok_in['g3'], 'L0_tok_be3': _L0_tok_in['be3'], 'L0_tok_m3': _L0_tok_in['m3'], 'L0_tok_v3': _L0_tok_in['v3'], 'L0_attn_norm1_g': _L0_attn_in['norm1_g'], 'L0_attn_norm1_b': _L0_attn_in['norm1_b'], 'L0_attn_Wq': _L0_attn_in['Wq'], 'L0_attn_Wkv': _L0_attn_in['Wkv'], 'L0_attn_Wproj': _L0_attn_in['Wproj'], 'L0_attn_bproj': _L0_attn_in['bproj'], 'L0_attn_norm2_g': _L0_attn_in['norm2_g'], 'L0_attn_norm2_b': _L0_attn_in['norm2_b'], 'L0_attn_W1': _L0_attn_in['W1'], 'L0_attn_b1': _L0_attn_in['b1'], 'L0_attn_W2': _L0_attn_in['W2'], 'L0_attn_b2': _L0_attn_in['b2'], 'L0_ffn_gate_w': _L0_ffn_in['gate_w'], 'L0_ffn_gate_b': _L0_ffn_in['gate_b'], 'L0_ffn_w1': _L0_ffn_in['w1'], 'L0_ffn_b1': _L0_ffn_in['b1'], 'L0_ffn_w2': _L0_ffn_in['w2'], 'L0_ffn_b2': _L0_ffn_in['b2'], 'L0_ffn_gamma': _L0_ffn_in['gamma'], 'L0_ffn_beta': _L0_ffn_in['beta'], 'L1_attn_WQ': _L1_attn_in['WQ'], 'L1_attn_WK': _L1_attn_in['WK'], 'L1_attn_WV': _L1_attn_in['WV'], 'L1_attn_Wout': _L1_attn_in['Wout'], 'L1_attn_bout': _L1_attn_in['bout'], 'L1_ffn_router_w': _L1_ffn_in['router_w'], 'L1_ffn_router_b': _L1_ffn_in['router_b'], 'L1_ffn_W1': _L1_ffn_in['W1'], 'L1_ffn_b1': _L1_ffn_in['b1'], 'L1_ffn_W2': _L1_ffn_in['W2'], 'L1_ffn_b2': _L1_ffn_in['b2']}

def reference(x, L0_tok_w1, L0_tok_b1, L0_tok_g1, L0_tok_be1, L0_tok_m1, L0_tok_v1, L0_tok_w2, L0_tok_b2, L0_tok_g2, L0_tok_be2, L0_tok_m2, L0_tok_v2, L0_tok_wq, L0_tok_bq, L0_tok_wk, L0_tok_bk, L0_tok_wv, L0_tok_bv, L0_tok_gamma, L0_tok_w3, L0_tok_b3, L0_tok_g3, L0_tok_be3, L0_tok_m3, L0_tok_v3, L0_attn_norm1_g, L0_attn_norm1_b, L0_attn_Wq, L0_attn_Wkv, L0_attn_Wproj, L0_attn_bproj, L0_attn_norm2_g, L0_attn_norm2_b, L0_attn_W1, L0_attn_b1, L0_attn_W2, L0_attn_b2, L0_ffn_gate_w, L0_ffn_gate_b, L0_ffn_w1, L0_ffn_b1, L0_ffn_w2, L0_ffn_b2, L0_ffn_gamma, L0_ffn_beta, L1_attn_WQ, L1_attn_WK, L1_attn_WV, L1_attn_Wout, L1_attn_bout, L1_ffn_router_w, L1_ffn_router_b, L1_ffn_W1, L1_ffn_b1, L1_ffn_W2, L1_ffn_b2):
    import jax
    import jax.numpy as jnp

    def _L0_tok_ref(x, w1, b1, g1, be1, m1, v1, w2, b2, g2, be2, m2, v2, wq, bq, wk, bk, wv, bv, gamma, w3, b3, g3, be3, m3, v3):
        import jax, jax.numpy as jnp
        import numpy as np
        EPS = 1e-05

        def _conv1d(x, W, b, stride, pad):
            y = jax.lax.conv_general_dilated(x, W, (stride,), [(pad, pad)], dimension_numbers=('NCH', 'OIH', 'NCH'))
            return y + b[None, :, None]

        def _bn(x, g, b, m, v):
            return (x - m[None, :, None]) * (g * jax.lax.rsqrt(v + EPS))[None, :, None] + b[None, :, None]

        def _maxpool(x, k):
            B, C, L = x.shape
            return x.reshape(B, C, L // k, k).max(axis=-1)

        def _self_attn(x, Wq, bq, Wk, bk, Wv, bv, gamma):
            q = jnp.einsum('oc,bcl->bol', Wq, x) + bq[None, :, None]
            k = jnp.einsum('oc,bcl->bol', Wk, x) + bk[None, :, None]
            v = jnp.einsum('oc,bcl->bol', Wv, x) + bv[None, :, None]
            energy = jnp.einsum('bci,bcj->bij', q, k)
            attn = jax.nn.softmax(energy, axis=-1)
            out = jnp.einsum('bcj,bij->bci', v, attn)
            return gamma * out + x
        B, D = x.shape
        emb_sample, emb_task = (x[:, :D // 2], x[:, D // 2:])
        h = jnp.stack([emb_sample, emb_task], axis=1)
        h = _maxpool(jax.nn.relu(_bn(_conv1d(h, w1, b1, 1, 1), g1, be1, m1, v1)), 8)
        h = _maxpool(jax.nn.relu(_bn(_conv1d(h, w2, b2, 1, 1), g2, be2, m2, v2)), 4)
        h = _self_attn(h, wq, bq, wk, bk, wv, bv, gamma)
        h = _bn(_conv1d(h, w3, b3, 2, 1), g3, be3, m3, v3)
        return h

    def _L0_attn_ref(x, norm1_g, norm1_b, Wq, Wkv, Wproj, bproj, norm2_g, norm2_b, W1, b1, W2, b2):
        import jax, jax.numpy as jnp
        import numpy as np
        B, N, DIM = (8, 2048, 64)
        HEADS, LOCAL_HEADS, WINDOW = (8, 1, 64)
        HD = DIM // HEADS
        MLP_HIDDEN = 256
        EPS = 1e-05

        def layer_norm(x, g, b):
            mu = jnp.mean(x, axis=-1, keepdims=True)
            var = jnp.var(x, axis=-1, keepdims=True)
            return (x - mu) * jax.lax.rsqrt(var + EPS) * g + b

        def look_around(t, pad_value=0.0):
            nw = t.shape[1]
            pads = [(0, 0), (1, 1)] + [(0, 0)] * (t.ndim - 2)
            p = jnp.pad(t, pads, constant_values=pad_value)
            return jnp.concatenate([p[:, i:i + nw] for i in range(3)], axis=2)

        def local_attn(q, k, v):
            b, n, d = q.shape
            nw = n // WINDOW
            scale = d ** (-0.5)
            bq = q.reshape(b, nw, WINDOW, d) * scale
            bk = look_around(k.reshape(b, nw, WINDOW, d))
            bv = look_around(v.reshape(b, nw, WINDOW, d))
            ticker = jnp.arange(n).reshape(1, nw, WINDOW)
            bq_k = look_around(ticker, pad_value=-1)
            pad_mask = (bq_k == -1)[:, :, None, :]
            dots = jnp.einsum('bnie,bnje->bnij', bq, bk)
            dots = jnp.where(pad_mask, -1000000000.0, dots)
            attn = jax.nn.softmax(dots, axis=-1)
            out = jnp.einsum('bnij,bnje->bnie', attn, bv)
            return out.reshape(b, n, d)

        def linear_attn(q, k, v):
            d = q.shape[-1]
            qs = jax.nn.softmax(q, axis=-1) * d ** (-0.5)
            ks = jax.nn.softmax(k, axis=-2)
            ctx = jnp.einsum('bhnd,bhne->bhde', ks, v)
            return jnp.einsum('bhnd,bhde->bhne', qs, ctx)
        b, n, c = x.shape
        h = layer_norm(x, norm1_g, norm1_b)
        q = h @ Wq.T
        kv = h @ Wkv.T
        split_heads = lambda t: t.reshape(b, n, HEADS, HD).transpose(0, 2, 1, 3)
        q, k, v = (split_heads(q), split_heads(kv), split_heads(kv))
        lq, gq = (q[:, :LOCAL_HEADS], q[:, LOCAL_HEADS:])
        lk, gk = (k[:, :LOCAL_HEADS], k[:, LOCAL_HEADS:])
        lv, gv = (v[:, :LOCAL_HEADS], v[:, LOCAL_HEADS:])
        lout = local_attn(lq.reshape(b * LOCAL_HEADS, n, HD), lk.reshape(b * LOCAL_HEADS, n, HD), lv.reshape(b * LOCAL_HEADS, n, HD)).reshape(b, LOCAL_HEADS, n, HD)
        gout = linear_attn(gq, gk, gv)
        attn = jnp.concatenate([lout, gout], axis=1)
        y = attn.transpose(0, 2, 1, 3).reshape(b, n, c) @ Wproj.T + bproj
        x = x + y
        h2 = layer_norm(x, norm2_g, norm2_b)
        m = jax.nn.gelu(h2 @ W1.T + b1, approximate=False) @ W2.T + b2
        return x + m

    def _L0_ffn_ref(x, gate_w, gate_b, w1, b1, w2, b2, gamma, beta):
        import jax, jax.numpy as jnp
        import numpy as np
        B, S, H, F, E, K = (8, 1024, 64, 128, 16, 2)
        EPS = 1e-05
        gate_logits = x @ gate_w + gate_b
        topk_vals, topk_idx = jax.lax.top_k(gate_logits, K)
        topk_w = jax.nn.softmax(topk_vals, axis=-1)
        h = jax.nn.relu(jnp.einsum('bsh,ehf->bsef', x, w1) + b1)
        expert_out = jnp.einsum('bsef,efh->bseh', h, w2) + b2
        sel = jnp.take_along_axis(expert_out, topk_idx[:, :, :, None], axis=2)
        moe = jnp.sum(topk_w[..., None] * sel, axis=2)
        y = x + moe
        mu = jnp.mean(y, axis=-1, keepdims=True)
        var = jnp.var(y, axis=-1, keepdims=True)
        return (y - mu) / jnp.sqrt(var + EPS) * gamma + beta

    def _L1_attn_ref(v, WQ, WK, WV, Wout, bout):
        import jax, jax.numpy as jnp
        import numpy as np
        IN_C = 64
        HID_C = 64
        HEADS = 8
        SCALE = 1.0 / np.sqrt(HID_C / HEADS).astype(np.float32)
        B, S, C = v.shape
        H = HEADS
        q = (v @ WQ).reshape(B, S, H, C)
        k = (v @ WK).reshape(B, S, H, C)
        val = (v @ WV).reshape(B, S, H, C)
        scores = jnp.einsum('bshc,bthc->bsth', q, k) * SCALE
        A = jax.nn.softmax(scores, axis=2)
        u = jnp.einsum('bsth,bthc->bshc', A, val).reshape(B, S, H * C)
        return u @ Wout + bout

    def _L1_ffn_ref(x, router_w, router_b, W1, b1, W2, b2):
        import jax, jax.numpy as jnp
        import numpy as np
        B, K, D = (128, 16, 64)
        E = 32
        H = int(D * 0.25)
        xf = x.reshape(-1, D)
        logits = xf @ router_w.T + router_b
        idx = jnp.argmax(logits, axis=-1)
        w1t = jnp.take(W1, idx, axis=0)
        h = jnp.einsum('nd,ndh->nh', xf, w1t) + jnp.take(b1, idx, axis=0)
        h = jax.nn.relu(h)
        w2t = jnp.take(W2, idx, axis=0)
        out = jnp.einsum('nh,nhd->nd', h, w2t) + jnp.take(b2, idx, axis=0)
        out = jax.nn.relu(out)
        return out.reshape(x.shape)
    h = _L0_tok_ref(x, L0_tok_w1, L0_tok_b1, L0_tok_g1, L0_tok_be1, L0_tok_m1, L0_tok_v1, L0_tok_w2, L0_tok_b2, L0_tok_g2, L0_tok_be2, L0_tok_m2, L0_tok_v2, L0_tok_wq, L0_tok_bq, L0_tok_wk, L0_tok_bk, L0_tok_wv, L0_tok_bv, L0_tok_gamma, L0_tok_w3, L0_tok_b3, L0_tok_g3, L0_tok_be3, L0_tok_m3, L0_tok_v3)
    h = h + _L0_attn_ref(_layernorm(h, axis=-1), L0_attn_norm1_g, L0_attn_norm1_b, L0_attn_Wq, L0_attn_Wkv, L0_attn_Wproj, L0_attn_bproj, L0_attn_norm2_g, L0_attn_norm2_b, L0_attn_W1, L0_attn_b1, L0_attn_W2, L0_attn_b2)
    h = h + _L0_ffn_ref(_layernorm(h, axis=-1), L0_ffn_gate_w, L0_ffn_gate_b, L0_ffn_w1, L0_ffn_b1, L0_ffn_w2, L0_ffn_b2, L0_ffn_gamma, L0_ffn_beta)
    h = h + _L1_attn_ref(_layernorm(h, axis=-1), L1_attn_WQ, L1_attn_WK, L1_attn_WV, L1_attn_Wout, L1_attn_bout)
    h = h + _L1_ffn_ref(_layernorm(h, axis=-1), L1_ffn_router_w, L1_ffn_router_b, L1_ffn_W1, L1_ffn_b1, L1_ffn_W2, L1_ffn_b2)
    return h

_drawn_inputs = setup_inputs


def setup_inputs(seed=0):
    import zlib

    import numpy as np

    out = dict(_drawn_inputs(seed))
    spreads = {'L0_attn_norm1_g': (1.0, 0.6),
     'L0_attn_norm1_b': (0.0, 0.8),
     'L0_attn_bproj': (0.0, 0.1),
     'L0_attn_norm2_g': (1.0, 0.6),
     'L0_attn_norm2_b': (0.0, 2.0),
     'L0_attn_b1': (0.0, 0.402),
     'L0_attn_b2': (0.0, 0.1),
     'L0_ffn_gate_b': (0.0, 0.1),
     'L0_ffn_b1': (0.0, 0.8),
     'L0_ffn_b2': (0.0, 0.272),
     'L0_ffn_gamma': (1.0, 0.2),
     'L0_ffn_beta': (0.0, 0.1)}
    factors = {'L0_tok_wq': 8.0,
     'L0_tok_bq': 8.0,
     'L0_tok_wk': 8.0,
     'L0_tok_bk': 64.0,
     'L0_attn_Wq': 8.0,
     'L0_attn_Wkv': 8.0,
     'L0_attn_Wproj': 8.0,
     'L0_ffn_w1': 5.615,
     'L0_ffn_w2': 4.355,
     'L1_attn_bout': 3.754,
     'L1_ffn_b1': 6.558,
     'L1_ffn_b2': 3.088}
    for name, (base, spread) in spreads.items():
        noise = np.random.default_rng([zlib.crc32(name.encode()), seed]).standard_normal(out[name].shape)
        drawn = base * np.exp(spread * noise) if base else spread * noise
        out[name] = jnp.asarray(drawn.astype(out[name].dtype))
    for name, factor in factors.items():
        out[name] = (out[name] * factor).astype(out[name].dtype)
    return out
```

```python
from contextlib import ExitStack

import concourse.bass as bass
from concourse import mybir

F32 = mybir.dt.float32
F32R = mybir.dt.float32r
BF16 = mybir.dt.bfloat16
U32 = mybir.dt.uint32
ACT = mybir.ActivationFunctionType
ALU = mybir.AluOpType
AX = mybir.AxisListType.X

P = 128
S = 64
C = 64
L = 4096
EPS = 1e-5
GS = 8
NG = S // GS
POOL1, POOL2 = 8, 4
L1 = L // POOL1
TS = 4
TG = S // TS
NT = TS * P
HEADS = 8
EXPERTS0, F0 = 16, 128
EXPERTS1, F1 = 32, 16
HID1 = EXPERTS1 * F1
MLP = 256

COLS = [("ident", P)]
COLS += [("g1r", P), ("v1r", P), ("w1", P), ("g2r", P), ("v2r", P), ("w2", P)]
COLS += [(n + str(i), 1) for i in (1, 2, 3) for n in ("b", "m", "g", "be", "v")]
COLS += [("gamma", 1), ("wq0", P), ("wq1", P), ("wk", P), ("bq0", 1), ("bq1", 1), ("bk", 1),
         ("wv", P), ("bvr", P), ("w3", 8 * P)]
TOK_END = sum(w for _, w in COLS)
COLS += [("n1g", 1), ("n1b", 1), ("wkv2", P), ("wq2", P), ("wtok", P), ("wproj", C), ("headmask", C),
         ("n2g", 1), ("n2b", 1), ("wm1", MLP), ("bm1", 2), ("wm2", 2 * C), ("bm2r", C)]
COLS += [("gatew", EXPERTS0), ("gatebr", EXPERTS0), ("iota16", EXPERTS0), ("eb1", EXPERTS0),
         ("eb2", C), ("gamr", C), ("betr", C)]
COLS += [("wqT", HEADS * C), ("wkT", HEADS * P), ("wvT", HEADS * P), ("wout", HEADS * C), ("boutr", C)]
COLS += [("routw", EXPERTS1), ("routbr", EXPERTS1), ("iota32", EXPERTS1), ("fw1", HID1), ("fb1", 4),
         ("fw2", 4 * C), ("fb2", C), ("sel32", HID1)]
NCOL = sum(w for _, w in COLS)
AT = {}
for _n, _w in COLS:
    AT[_n] = (sum(w for _, w in COLS[:[n for n, _ in COLS].index(_n)]), _w)


class Step:

    def __init__(self, nc, ctx, m, name, per=1):
        self.per = per
        fit = [f for f in m.ended if f.end >= 2 * per]
        if fit:
            m.ended.remove(fit[0])
            self.sem, self.start = fit[0].sem, fit[0].end
        else:
            self.sem, self.start = ctx.enter_context(nc.semaphore(name)), 2 * per
            m.raised.append(self)
        self.end = self.start + per * m.rounds
        m.steps.append(self)

    def at(self, r, k=None):
        return r * self.per + (self.start + (self.per if k is None else k))


def col(m, name, rows=slice(0, P)):
    a, w = AT[name]
    return m.cst[rows, a:a + w]


def settle(eng, m):
    eng.sem_inc(m.waited, 1)


class Memory:
    pass


def tokenizer(nc, ctx, m):
    def sb(name, shape, dt=F32):
        return m.mem.enter_context(nc.sbuf_tensor(name, shape, dt))

    def step(name, per=1):
        return Step(nc, ctx, m, name, per)

    m.rounds = NG
    NP = GS // 2
    K2 = 96
    x_in = [sb(f"x_in{b}", [K2, L]) for b in range(2)]
    c1_max = [sb(f"c1_max{b}", [P, L1]) for b in range(2)]
    c2_in = [sb(f"c2_in{b}", [K2, NP, L1]) for b in range(2)]
    c2_max = sb("c2_max", [P, NP * P])
    x2 = sb("x2", [P, NP * P])
    x3 = sb("x3", [P, NP, P + 2])
    qk = sb("qk", [P, 3, NP * P])
    v_tok = sb("v_tok", [P, NP, P])
    ex = sb("t_ex", [P, GS, P])
    prob = sb("t_prob", [P, GS, P])
    probT = sb("t_probT", [P, GS, P])
    row_max = sb("t_rmax", [P, GS])
    neg_max = sb("t_nmax", [P, GS])
    row_sum = sb("t_rsum", [P, GS])
    rec = sb("t_rec", [P, GS])
    row_scale = sb("t_rscale", [P, GS])
    w1s, w2s = sb("w1s", [P, P]), sb("w2s", [P, P])
    r1, r2 = sb("r1", [P, P]), sb("r2", [P, P])
    rr = sb("rr", [P, 3])
    sc = sb("sc", [P, 3])
    bi = sb("bi", [P, 3])

    x_sem = [ctx.enter_context(nc.semaphore(f"x_loaded{b}")) for b in range(2)]
    x_pad = ctx.enter_context(nc.semaphore("x_padded"))
    c2_pad = ctx.enter_context(nc.semaphore("c2_padded"))
    std = ctx.enter_context(nc.semaphore("norm_std"))
    prep = ctx.enter_context(nc.semaphore("norm_folded"))
    conv1_ps = step("conv1_ps", 4)
    conv1_max = step("conv1_max", 4)
    pooled1 = step("pooled1", 3 * NP)
    conv2_ps = step("conv2_ps", NP)
    conv2_max = step("conv2_max", NP)
    pooled2 = step("pooled2")
    qkv_ps = step("qkv_ps", 2)
    qk_sb = step("qk_sb", 3)
    v_sb = step("v_sb")
    energy_ps = step("energy_ps")
    negmax = step("negmax", 2)
    exp_sb = step("exp_sb", GS)
    scale_sb = step("scale_sb", 2)
    prob_sb = step("prob_sb")
    probT_ps = step("probT_ps")
    probT_sb = step("probT_sb")
    attn_ps = step("attn_ps")
    x3_sb = step("x3_sb")
    conv3_ps = step("conv3_ps")
    h_sb = step("h0_sb")
    h_stat = step("h0_stat", GS)
    m.stat_last = (h_stat.sem, h_stat.at(NG - 1))
    m.h_last, m.h_rounds = h_sb, NG - 1

    def sp(eng):
        def load(g, b, j):
            if j is not None:
                eng.wait_ge(conv1_ps.sem, conv1_ps.at(g - 2))
            for k in range(3):
                if k == 2 and j is None:
                    eng.wait_ge(x_pad, 4)
                rows = m.x[bass.ds(g * GS, GS), :, k:k + L].rearrange("s c l -> (s c) l")
                eng.dma_start(x_in[b][16 * k:16 * k + 16, :], rows).then_inc(x_sem[b], 16)
        load(0, 0, None)
        load(1, 1, None)
        with eng.Fori(1, NG // 2) as i:
            load(2 * i, 0, i)
            load(2 * i + 1, 1, i)

    def pool(eng):
        eng.wait_ge(m.eps_sem, 1)
        for b in range(2):
            for half in range(2):
                if b + half > 0:
                    eng.wait_ge(x_pad, 2 * b + half)
                r = 32 + 32 * half
                eng.memset(x_in[b][r:r + 32, :], 0.0).then_inc(x_pad, 1)
        eng.wait_ge(x_pad, 4)
        for b in range(2):
            if b:
                eng.wait_ge(c2_pad, 2)
            eng.memset(c2_in[b][0:32, :, 0:1], 0.0).then_inc(c2_pad, 1)
            eng.wait_ge(c2_pad, 2 * b + 1)
            eng.memset(c2_in[b][64:96, :, L1 - 1:L1], 0.0).then_inc(c2_pad, 1)
        eng.wait_ge(c2_pad, 4)
        eng.memset(x3[:, :, 0:1], 0.0).then_inc(c2_pad, 1)
        eng.memset(x3[:, :, P + 1:P + 2], 0.0).then_inc(c2_pad, 1)
        eng.wait_ge(c2_pad, 6)
        with eng.Fori(0, NG) as g:
            eng.wait_ge(scale_sb.sem, scale_sb.at(g))
            eng.wait_ge(exp_sb.sem, exp_sb.at(g))
            eng.wait_ge(probT_ps.sem, probT_ps.at(g - 1))
            eng.tensor_tensor(prob[:, :, :], ex[:, :, :],
                              row_scale[:, :].unsqueeze(2).broadcast_to([P, GS, P]),
                              ALU.mult).then_inc(prob_sb.sem, 1)

    def pe(eng):
        def conv1(g, b, j, h):
            if h == 0:
                eng.wait_ge(x_sem[b], (j + 1) * 48)
            if h < 2:
                eng.wait_ge(conv1_max.sem, conv1_max.at(g - 1, h + 3))
            else:
                eng.wait_ge(conv1_max.sem, conv1_max.at(g, h - 1))
            for t in range(2):
                mm = eng.matmul(m.ps[:, 2 * (h % 2) + t, :], w1s[0:K2, :],
                                x_in[b][:, (2 * h + t) * 512:(2 * h + t + 1) * 512],
                                start=True, stop=True)
            mm.then_inc(conv1_ps.sem, 1)

        def rest(g, b, ahead):
            eng.wait_ge(pooled1.sem, pooled1.at(g))
            eng.wait_ge(h_sb.sem, h_sb.at(g - 1))
            eng.wait_ge(x3_sb.sem, x3_sb.at(g - 1))
            for p in range(NP):
                eng.matmul(m.ps[:, 4 + p, :], w2s[0:K2, :], c2_in[b][:, p, :],
                           start=True, stop=True).then_inc(conv2_ps.sem, 1)
            ahead(0)
            eng.wait_ge(pooled2.sem, pooled2.at(g))
            for n, w in enumerate(("wq0", "wq1", "wk")):
                mm = eng.matmul(m.ps[:, 4 + n, :], col(m, w), x2[:, :], start=True, stop=True)
            mm.then_inc(qkv_ps.sem, 1)
            for p in range(NP):
                mm = eng.matmul(m.ps[:, 7, p * P:(p + 1) * P], x2[:, p * P:(p + 1) * P],
                                col(m, "wv"), start=True, stop=True)
            mm.then_inc(qkv_ps.sem, 1)
            ahead(1)
            eng.wait_ge(qk_sb.sem, qk_sb.at(g))
            for s in range(GS):
                p = s // 2
                mm = eng.matmul(m.ps[:, 4 + s // 4, (s % 4) * P:(s % 4 + 1) * P],
                                qk[:, s % 2, p * P:(p + 1) * P], qk[:, 2, p * P:(p + 1) * P],
                                start=True, stop=True)
            mm.then_inc(energy_ps.sem, 1)
            ahead(2)
            eng.wait_ge(prob_sb.sem, prob_sb.at(g))
            eng.wait_ge(v_sb.sem, v_sb.at(g))
            for s in range(GS):
                mm = eng.transpose(m.ps[:, 6 + s // 4, (s % 4) * P:(s % 4 + 1) * P], prob[:, s, :],
                                   col(m, "ident"))
            mm.then_inc(probT_ps.sem, 1)
            ahead(3)
            eng.wait_ge(probT_sb.sem, probT_sb.at(g))
            for s in range(GS):
                r = 64 * (s % 2)
                mm = eng.matmul(m.ps[r:r + 64, 4, (s // 2) * P:(s // 2 + 1) * P],
                                v_tok[:, s // 2, r:r + 64], probT[:, s, :], start=True, stop=True)
            mm.then_inc(attn_ps.sem, 1)
            eng.wait_ge(x3_sb.sem, x3_sb.at(g))
            for s in range(2):
                for k in range(4):
                    a = AT["w3"][0] + (4 * s + k) * P
                    mm = eng.matmul(m.ps[:, 5, s * 256:(s + 1) * 256], m.cst[:, a:a + P],
                                    x3[:, :, k:k + P - 1:2], start=(k == 0), stop=(k == 3))
            mm.then_inc(conv3_ps.sem, 1)

        eng.wait_ge(prep, 6)
        eng.wait_ge(x_pad, 4)
        eng.wait_ge(c2_pad, 6)
        for h in range(4):
            conv1(0, 0, 0, h)
        with eng.Fori(0, NG // 2 - 1) as i:
            rest(2 * i, 0, lambda h: conv1(2 * i + 1, 1, i, h))
            rest(2 * i + 1, 1, lambda h: conv1(2 * i + 2, 0, i + 1, h))
        rest(NG - 2, 0, lambda h: conv1(NG - 1, 1, NG // 2 - 1, h))
        rest(NG - 1, 1, lambda h: None)

    def dve(eng):
        eng.wait_ge(std, 3)
        eng.reciprocal(r1[:, :], r1[:, :]).then_inc(m.dve_pre, 1)
        eng.reciprocal(r2[:, :], r2[:, :]).then_inc(m.dve_pre, 1)
        eng.reciprocal(rr[:, :], rr[:, :]).then_inc(m.dve_pre, 1)
        eng.wait_ge(m.dve_pre, 3)
        eng.tensor_tensor(r1[:, :], r1[:, :], col(m, "g1r"), ALU.mult).then_inc(m.dve_pre, 1)
        eng.tensor_tensor(r2[:, :], r2[:, :], col(m, "g2r"), ALU.mult).then_inc(m.dve_pre, 1)
        for n in range(3):
            eng.tensor_tensor(sc[:, n:n + 1], rr[:, n:n + 1], col(m, f"g{n + 1}"), ALU.mult).then_inc(m.dve_pre, 1)
            eng.tensor_tensor(bi[:, n:n + 1], col(m, f"b{n + 1}"), col(m, f"m{n + 1}"), ALU.subtract).then_inc(m.dve_pre, 1)
        eng.wait_ge(m.dve_pre, 11)
        eng.tensor_tensor(w1s[:, :], r1[:, :], col(m, "w1"), ALU.mult).then_inc(prep, 1)
        eng.tensor_tensor(w2s[:, :], r2[:, :], col(m, "w2"), ALU.mult).then_inc(prep, 1)
        eng.tensor_tensor(bi[:, :], bi[:, :], sc[:, :], ALU.mult).then_inc(prep, 1)
        eng.wait_ge(prep, 3)
        for n in range(3):
            eng.tensor_tensor(bi[:, n:n + 1], bi[:, n:n + 1], col(m, f"be{n + 1}"), ALU.add).then_inc(prep, 1)

        def reduce1(g, b, h):
            eng.wait_ge(conv1_ps.sem, conv1_ps.at(g, h + 1))
            if h == 0:
                eng.wait_ge(pooled1.sem, pooled1.at(g - 2))
            src = m.ps[:, 2 * (h % 2):2 * (h % 2) + 2, :].rearrange("p a (l k) -> p (a l) k", k=POOL1)
            eng.tensor_reduce(c1_max[b][:, h * P:(h + 1) * P], src, AX, ALU.max).then_inc(conv1_max.sem, 1)

        def rest(g, b, ahead):
            for p in range(NP):
                eng.wait_ge(conv2_ps.sem, conv2_ps.at(g, p + 1))
                if p == 0:
                    eng.wait_ge(pooled2.sem, pooled2.at(g - 1))
                src = m.ps[:, 4 + p, :].rearrange("p (l k) -> p l k", k=POOL2)
                eng.tensor_reduce(c2_max[:, p * P:(p + 1) * P], src, AX, ALU.max).then_inc(conv2_max.sem, 1)
            ahead(0)
            eng.wait_ge(qkv_ps.sem, qkv_ps.at(g))
            eng.tensor_tensor(v_tok[:, :, :], m.ps[:, 7, :].rearrange("p (n c) -> p n c", n=NP),
                              col(m, "bvr").unsqueeze(1).broadcast_to([P, NP, P]),
                              ALU.add).then_inc(v_sb.sem, 1)
            ahead(1)
            eng.wait_ge(energy_ps.sem, energy_ps.at(g))
            eng.tensor_reduce(row_max[:, :], m.ps[:, 4:6, :].rearrange("p a (s j) -> p (a s) j", j=P), AX,
                              ALU.max).then_inc(negmax.sem, 1)
            eng.wait_ge(negmax.sem, negmax.at(g, 1))
            eng.wait_ge(exp_sb.sem, exp_sb.at(g - 1))
            eng.tensor_scalar(neg_max[:, :], row_max[:, :], -1.0, None, ALU.mult).then_inc(negmax.sem, 1)
            ahead(2)
            eng.wait_ge(exp_sb.sem, exp_sb.at(g))
            eng.reciprocal(rec[:, :], row_sum[:, :]).then_inc(scale_sb.sem, 1)
            eng.wait_ge(scale_sb.sem, scale_sb.at(g, 1))
            eng.wait_ge(prob_sb.sem, prob_sb.at(g - 1))
            eng.tensor_scalar(row_scale[:, :], rec[:, :], col(m, "gamma"), None, ALU.mult).then_inc(scale_sb.sem, 1)
            ahead(3)
            eng.wait_ge(attn_ps.sem, attn_ps.at(g))
            eng.wait_ge(conv3_ps.sem, conv3_ps.at(g - 1))
            eng.tensor_tensor(x3[:, :, 1:P + 1], m.ps[:, 4, :].rearrange("p (n l) -> p n l", n=NP),
                              x2[:, :].rearrange("p (n l) -> p n l", n=NP), ALU.add).then_inc(x3_sb.sem, 1)
            eng.wait_ge(h_sb.sem, h_sb.at(g))
            stats(eng, m, m.h, g, GS, h_stat.sem)

        eng.wait_ge(c2_pad, 6)
        for h in range(4):
            reduce1(0, 0, h)
        with eng.Fori(0, NG // 2 - 1) as i:
            rest(2 * i, 0, lambda h: reduce1(2 * i + 1, 1, h))
            rest(2 * i + 1, 1, lambda h: reduce1(2 * i + 2, 0, h))
        rest(NG - 2, 0, lambda h: reduce1(NG - 1, 1, h))
        rest(NG - 1, 1, lambda h: None)

    def act(eng):
        nc.scalar.activation(r1[:, :], col(m, "v1r"), ACT.Sqrt, bias=m.eps[:, :]).then_inc(std, 1)
        nc.scalar.activation(r2[:, :], col(m, "v2r"), ACT.Sqrt, bias=m.eps[:, :]).then_inc(std, 1)
        a = AT["v1"][0]
        d = AT["v2"][0] - a
        nc.scalar.activation(rr[:, :], m.cst[:, a:a + 2 * d + 1:d], ACT.Sqrt, bias=m.eps[:, :]).then_inc(std, 1)
        eng.preload_act_table(ACT.Exp)

        def relu1(g, b):
            eng.wait_ge(conv1_max.sem, conv1_max.at(g))
            eng.wait_ge(conv2_ps.sem, conv2_ps.at(g - 2))
            for p in range(NP):
                q = 32 * p
                for k, (to, of, n) in enumerate(((1, 0, L1 - 1), (0, 0, L1), (0, 1, L1 - 1))):
                    nc.scalar.activation(c2_in[b][32 * k:32 * k + 32, p, to:to + n],
                                         c1_max[b][q:q + 32, of:of + n], ACT.Relu,
                                         bias=bi[q:q + 32, 0:1]).then_inc(pooled1.sem, 1)

        def rest(g, b, ahead):
            eng.wait_ge(conv2_max.sem, conv2_max.at(g))
            nc.scalar.activation(x2[:, :], c2_max[:, :], ACT.Relu, bias=bi[:, 1:2]).then_inc(pooled2.sem, 1)
            eng.wait_ge(qkv_ps.sem, qkv_ps.at(g, 1))
            for n, w in enumerate(("bq0", "bq1", "bk")):
                nc.scalar.activation(qk[:, n, :], m.ps[:, 4 + n, :], ACT.Identity, bias=col(m, w)).then_inc(qk_sb.sem, 1)
            eng.wait_ge(negmax.sem, negmax.at(g))
            eng.wait_ge(prob_sb.sem, prob_sb.at(g - 1))
            for s in range(GS):
                nc.scalar.activation(ex[:, s, :], m.ps[:, 4 + s // 4, (s % 4) * P:(s % 4 + 1) * P], ACT.Exp,
                                     bias=neg_max[:, s:s + 1], accum_out=row_sum[:, s:s + 1]).then_inc(exp_sb.sem, 1)
            eng.wait_ge(probT_ps.sem, probT_ps.at(g))
            nc.scalar.activation(probT[:, :, :], m.ps[:, 6:8, :].rearrange("p a (s j) -> p (a s) j", j=P),
                                 ACT.Identity).then_inc(probT_sb.sem, 1)
            ahead()
            eng.wait_ge(conv3_ps.sem, conv3_ps.at(g))
            nc.scalar.activation(m.h[:, bass.ds(g * GS, GS), :].rearrange("q (p s) l -> q s p l", s=2),
                                 m.ps[:, 5, :].rearrange("q (s p l) -> q s p l", s=2, p=NP), ACT.Identity,
                                 bias=bi[:, 2:3], scale=sc[:, 2:3]).then_inc(h_sb.sem, 1)

        eng.wait_ge(prep, 6)
        eng.wait_ge(c2_pad, 6)
        relu1(0, 0)
        with eng.Fori(0, NG // 2 - 1) as i:
            rest(2 * i, 0, lambda: relu1(2 * i + 1, 1))
            rest(2 * i + 1, 1, lambda: relu1(2 * i + 2, 0))
        rest(NG - 2, 0, lambda: relu1(NG - 1, 1))
        rest(NG - 1, 1, lambda: None)

    return dict(sp=sp, pool=pool, pe=pe, dve=dve, act=act)


def stats(eng, m, h, g, n, done):
    for s in range(n):
        eng.bn_stats(m.stat[:, bass.ds(g * n + s, 1), :], h[:, bass.ds(g * n + s, 1), :]).then_inc(done, 1)


def norm(name, twice=False, after=None):
    def make(nc, ctx, m):
        diff, m2, dd, var, dev, tmp, mean, rstd, rstd2 = m.norm_tiles
        own = ctx.enter_context(nc.semaphore(f"{name}_parts"))
        var_sb = ctx.enter_context(nc.semaphore(f"{name}_var"))
        std_sb = ctx.enter_context(nc.semaphore(f"{name}_std"))
        ready = ctx.enter_context(nc.semaphore(f"{name}_ready"))
        m.norm_ready = ready
        m.norm_value = 3 if twice else 2
        stat_sem, stat_value = m.stat_last

        def dve(eng):
            eng.wait_ge(stat_sem, stat_value)
            st = m.stat
            eng.tensor_tensor(diff[:, :], st[:, :, 1], st[:, :, 4], ALU.subtract).then_inc(own, 1)
            eng.tensor_tensor(tmp[:, :], st[:, :, 1], st[:, :, 4], ALU.add).then_inc(own, 1)
            eng.tensor_tensor(m2[:, :], st[:, :, 2], st[:, :, 5], ALU.add).then_inc(own, 1)
            eng.wait_ge(own, 3)
            eng.scalar_tensor_tensor(out=dd[:, :], in0=diff[:, :], scalar=0.25, in1=diff[:, :],
                                     op0=ALU.mult, op1=ALU.mult).then_inc(own, 1)
            eng.tensor_scalar(mean[:, :], tmp[:, :], 0.5, None, ALU.mult).then_inc(ready, 1)
            eng.wait_ge(own, 4)
            eng.scalar_tensor_tensor(out=var[:, :], in0=m2[:, :], scalar=1.0 / C, in1=dd[:, :],
                                     op0=ALU.mult, op1=ALU.add).then_inc(var_sb, 1)
            eng.wait_ge(std_sb, 1)
            eng.reciprocal(rstd[:, :], dev[:, :]).then_inc(ready, 1)
            if twice:
                eng.wait_ge(ready, 2)
                eng.tensor_tensor(tmp[:, :], var[:, :], rstd[:, :], ALU.mult).then_inc(own, 1)
                eng.wait_ge(own, 5)
                eng.tensor_tensor(m2[:, :], tmp[:, :], rstd[:, :], ALU.mult).then_inc(var_sb, 1)
                eng.wait_ge(std_sb, 2)
                eng.reciprocal(rstd2[:, :], dd[:, :]).then_inc(ready, 1)

        def act(eng):
            eng.wait_ge(var_sb, 1)
            nc.scalar.activation(dev[:, :], var[:, :], ACT.Sqrt, bias=m.eps[:, :]).then_inc(std_sb, 1)
            if twice:
                eng.wait_ge(var_sb, 2)
                nc.scalar.activation(dd[:, :], m2[:, :], ACT.Sqrt, bias=m.eps[:, :]).then_inc(std_sb, 1)

        return dict(dve=dve, act=act)
    return make


def bc(ap, shape):
    return ap.unsqueeze(2).broadcast_to(shape)


class Split:

    def __init__(self, nc, ctx, name, n, mem=None):
        self.hi, self.lo, self.f = ((mem or ctx).enter_context(nc.sbuf_tensor(f"{name}_{k}", [P, n], dt))
                                    for k, dt in (("hi", F32R), ("lo", F32R), ("f", F32)))
        self.sem = ctx.enter_context(nc.semaphore(name + "_split"))

    def make(self, eng, src, scale=None):
        eng.tensor_scalar(self.f[:, :], src, 1.0 if scale is None else scale, None, ALU.mult).then_inc(self.sem, 1)
        eng.wait_ge(self.sem, 1)
        eng.tensor_copy(self.hi[:, :], self.f[:, :]).then_inc(self.sem, 1)
        eng.wait_ge(self.sem, 2)
        eng.tensor_tensor(self.lo[:, :], self.f[:, :], self.hi[:, :].bitcast(F32), ALU.subtract).then_inc(self.sem, 1)


def skewed(eng, n, rest, ahead):
    ahead(0, 0, None)
    with eng.Fori(0, n // 2 - 1) as i:
        rest(2 * i, 0, lambda k: ahead(2 * i + 1, 1, k))
        rest(2 * i + 1, 1, lambda k: ahead(2 * i + 2, 0, k))
    rest(n - 2, 0, lambda k: ahead(n - 1, 1, k))
    rest(n - 1, 1, lambda k: None)


def lagged(eng, n, ahead, rest, early=0):
    for g in range(1 + early):
        ahead(g, g % 2)
    rest(0, 0, 2, False)
    rest(1, 1, 2, True)
    with eng.Fori(1, n // 2 - 1) as i:
        rest(2 * i, 0, 2, True)
        rest(2 * i + 1, 1, 2, True)
    rest(n - 2, 0, 1, True)
    rest(n - 1, 1, 0, True)
    rest(n, 0, None, True)


class Turned:

    def __init__(self, nc, ctx, m, name, src, bank, keep=None):
        self.nc, self.m, self.src, self.bank, self.keep = nc, m, src, bank, keep
        sb = lambda n, s, dt=F32: m.mem.enter_context(nc.sbuf_tensor(f"{name}_{n}", s, dt))
        self.xc = [sb(f"xc{b}", [P, TS, C]) for b in range(2)]
        self.twin = [sb(f"twin{b}", [P, TS, 2 * C]) for b in range(2)]
        self.xn = [t[:, :, 0:C] for t in self.twin]
        self.xs = [sb(f"xs{b}", [P, NT], F32R) for b in range(2)]
        self.mean, self.rstd, self.rstd2 = m.norm_tiles[6:]
        self.norm = (m.norm_ready, m.norm_value)

        def step(n, per=1):
            return Step(nc, ctx, m, f"{name}_{n}", per)
        self.norm_sb = step("norm_sb", 2 if keep is None else 3)
        self.turn_ps = step("turn_ps")
        self.hi_sb = step("hi_sb")
        self.lo_sb = step("lo_sb")

    def pool(self, eng, g, b, free):
        m, sl, sh = self.m, bass.ds(g * TS, TS), [P, TS, C]
        eng.wait_ge(free.sem, free.at(g - 2))
        settle(eng, m)
        eng.tensor_tensor(self.xc[b][:, :, :], self.src[:, sl, :], bc(self.mean[:, sl], sh),
                          ALU.subtract).then_inc(self.norm_sb.sem, 1)
        eng.wait_ge(self.norm_sb.sem, self.norm_sb.at(g, 1))
        last, scale = self.xc[b][:, :, :], self.rstd
        if self.keep is not None:
            settle(eng, m)
            eng.tensor_tensor(self.keep[:, sl, :], self.xc[b][:, :, :], bc(self.rstd[:, sl], sh),
                              ALU.mult).then_inc(self.norm_sb.sem, 1)
            eng.wait_ge(self.norm_sb.sem, self.norm_sb.at(g, 2))
            settle(eng, m)
            last, scale = self.keep[:, sl, :], self.rstd2
        pair = [P, TS, 2, C]
        eng.tensor_tensor(self.twin[b][:, :, :].rearrange("p s (a c) -> p s a c", a=2),
                          last.unsqueeze(2).broadcast_to(pair),
                          scale[:, sl].unsqueeze(2).unsqueeze(3).broadcast_to(pair),
                          ALU.mult).then_inc(self.norm_sb.sem, 1)

    def pe(self, eng, g, b):
        m = self.m
        eng.wait_ge(self.norm_sb.sem, self.norm_sb.at(g))
        eng.wait_ge(self.lo_sb.sem, self.lo_sb.at(g - 1))
        for s in range(TS):
            mm = eng.transpose(m.ps[:, self.bank, s * P:(s + 1) * P], self.twin[b][:, s, :], col(m, "ident"))
        mm.then_inc(self.turn_ps.sem, 1)

    def act(self, eng, g, b, free):
        eng.wait_ge(self.turn_ps.sem, self.turn_ps.at(g))
        eng.wait_ge(free.sem, free.at(g - 2))
        self.nc.scalar.activation(self.xs[b][:, :], self.m.ps[:, self.bank, :],
                                  ACT.Identity).then_inc(self.hi_sb.sem, 1)

    def dve(self, eng, g, b):
        eng.wait_ge(self.hi_sb.sem, self.hi_sb.at(g))
        eng.tensor_tensor(self.xs[b][64:P, :], self.m.ps[64:P, self.bank, :],
                          self.xs[b][64:P, :].bitcast(F32), ALU.subtract).then_inc(self.lo_sb.sem, 1)


def attention0(nc, ctx, m):
    def sb(name, shape, dt=F32):
        return m.mem.enter_context(nc.sbuf_tensor("a0_" + name, shape, dt))

    def step(name, per=1):
        return Step(nc, ctx, m, "a0_" + name, per)

    m.rounds = TG
    HD = C // HEADS
    SCALE = float(HD) ** -0.5
    T = Turned(nc, ctx, m, "a0", m.h, 0, keep=m.y)
    w_kv, w_q, w_tok = (m.split[n] for n in ("wkv2", "wq2", "wtok"))
    kvT = [sb(f"kvT{b}", [P, NT]) for b in range(2)]
    q0T = [sb(f"q0T{b}", [P, NT]) for b in range(2)]
    tok = [sb(f"tok{b}", [P, TS, P]) for b in range(2)]
    bias_kv, bias_q, bias_tok = sb("bias_kv", [P, 1]), sb("bias_q", [P, 1]), sb("bias_tok", [P, P])
    lmax, lneg, lsum, lrec = (sb(n, [P, TS]) for n in ("lmax", "lneg", "lsum", "lrec"))
    kmax, kneg, ksum, krec = (sb(n, [C, TS]) for n in ("kmax", "kneg", "ksum", "krec"))
    qmax, qsum, qrec = (sb(n, [P, TS * HEADS]) for n in ("qmax", "qsum", "qrec"))
    qd, qe, qs = (sb(n, [P, TS, C]) for n in ("qd", "qe", "qs"))
    lex, lprob, lprobT = (sb(n, [P, TS, P]) for n in ("lex", "lprob", "lprobT"))
    ekT = sb("ekT", [C, NT])
    ek, qsT = sb("ek", [P, TS, C]), sb("qsT", [C, NT])
    mask, ctxm = sb("mask", [C, TS, C]), sb("ctxm", [C, TS, C])
    v0 = [sb(f"v0{b}", [P, TS, C]) for b in range(2)]
    aT = sb("aT", [C + 1, NT])

    pre = ctx.enter_context(nc.semaphore("a0_bias_ps"))
    pre_sb = ctx.enter_context(nc.semaphore("a0_bias_sb"))
    once = ctx.enter_context(nc.semaphore("a0_set_once"))
    proj_ps = step("proj_ps", 2)
    kv_sb, q0_sb, tok_sb = step("kv_sb"), step("q0_sb"), step("tok_sb")
    local_ps, local_neg, local_exp = step("local_ps"), step("local_neg", 2), step("local_exp", TS)
    local_rec, local_prob = step("local_rec"), step("local_prob")
    k_neg, k_exp, k_rec = step("k_neg", 2), step("k_exp", TS), step("k_rec")
    q_max, q_diff, q_exp, q_rec, q_soft = step("q_max"), step("q_diff"), step("q_exp"), step("q_rec", 2), step("q_soft")
    k_turn, k_sb = step("k_turn"), step("k_sb")
    q_turn, q_sb = step("q_turn"), step("q_sb")
    p_turn, p_sb = step("p_turn"), step("p_sb")
    v0_sb, mask_sb = step("v0_sb"), step("mask_sb")
    ctx_ps, ctx_sb = step("ctx_ps"), step("ctx_sb")
    attn_ps, attn_sb = step("attn_ps"), step("attn_sb")
    y_ps, x1_sb = step("y_ps"), step("x1_sb")
    x1_stat = step("x1_stat", TS)
    before = (m.h_last.sem, m.h_last.at(m.h_rounds))
    m.stat_last = (x1_stat.sem, x1_stat.at(TG - 1))

    def pool(eng):
        def ahead(g, b):
            T.pool(eng, g, b, proj_ps)

        def rest(g, b, left, back):
            if left is None:
                return
            eng.wait_ge(q_max.sem, q_max.at(g))
            eng.wait_ge(q_exp.sem, q_exp.at(g - 1))
            eng.tensor_tensor(qd[:, :, :].rearrange("p s (h d) -> p (s h) d", d=HD),
                              tok[b][:, :, C:P].rearrange("p s (h d) -> p s h d", d=HD),
                              qmax[:, :].rearrange("p (s h) -> p s h", s=TS).unsqueeze(3).broadcast_to([P, TS, HEADS, HD]),
                              ALU.subtract).then_inc(q_diff.sem, 1)
            eng.wait_ge(attn_ps.sem, attn_ps.at(g - 2))
            settle(eng, m)
            eng.tensor_copy(v0[b][:, :, 0:HD], tok[b][:, :, 0:HD]).then_inc(v0_sb.sem, 1)
            if left > 1:
                ahead(g + 2, b)
            eng.wait_ge(q_rec.sem, q_rec.at(g))
            eng.wait_ge(q_turn.sem, q_turn.at(g - 1))
            eng.tensor_tensor(qs[:, :, :].rearrange("p s (h d) -> p (s h) d", d=HD),
                              qe[:, :, :].rearrange("p s (h d) -> p (s h) d", d=HD),
                              qrec[:, :].unsqueeze(2).broadcast_to([P, TS * HEADS, HD]),
                              ALU.mult).then_inc(q_soft.sem, 1)
            eng.wait_ge(local_rec.sem, local_rec.at(g))
            eng.wait_ge(p_turn.sem, p_turn.at(g - 1))
            eng.tensor_tensor(lprob[:, :, :], lex[:, :, :], lrec[:, :].unsqueeze(2).broadcast_to([P, TS, P]),
                              ALU.mult).then_inc(local_prob.sem, 1)
            eng.wait_ge(k_rec.sem, k_rec.at(g))
            eng.wait_ge(ctx_sb.sem, ctx_sb.at(g - 1))
            eng.tensor_tensor(mask[:, :, :], col(m, "headmask", slice(0, C)).unsqueeze(1).broadcast_to([C, TS, C]),
                              krec[:, :].unsqueeze(2).broadcast_to([C, TS, C]), ALU.mult).then_inc(mask_sb.sem, 1)

        for b in range(2):
            eng.memset(v0[b][:, :, :], 0.0).then_inc(once, 1)
        eng.wait_ge(once, 2)
        eng.memset(aT[C:C + 1, :], 1.0).then_inc(once, 1)
        eng.wait_ge(once, 3)
        eng.wait_ge(*T.norm)
        lagged(eng, TG, ahead, rest, early=1)

    def pe(eng):
        def project(g, b):
            eng.wait_ge(T.lo_sb.sem, T.lo_sb.at(g))
            eng.wait_ge(kv_sb.sem, kv_sb.at(g - 1))
            eng.wait_ge(q0_sb.sem, q0_sb.at(g - 1))
            eng.wait_ge(tok_sb.sem, tok_sb.at(g - 1))
            for bank, w in ((1, w_kv), (2, w_q)):
                eng.matmul(m.ps[:, bank, :], w.hi[:, :], T.xs[b][:, :], start=True, stop=False)
                mm = eng.matmul(m.ps[:, bank, :], w.lo[:, :], T.xs[b][:, :], start=False, stop=True)
            mm.then_inc(proj_ps.sem, 1)
            for s in range(TS):
                sl = slice(s * P, (s + 1) * P)
                eng.matmul(m.ps[:, 3, sl], T.xs[b][:, sl], w_tok.hi[:, :], start=True, stop=False)
                mm = eng.matmul(m.ps[:, 3, sl], T.xs[b][:, sl], w_tok.lo[:, :], start=False, stop=True)
            mm.then_inc(proj_ps.sem, 1)

        def ahead(g, b):
            T.pe(eng, g, b)
            project(g, b)

        def local(g, b):
            eng.wait_ge(kv_sb.sem, kv_sb.at(g))
            eng.wait_ge(q0_sb.sem, q0_sb.at(g))
            eng.wait_ge(local_exp.sem, local_exp.at(g - 1))
            for s in range(TS):
                sl = slice(s * P, (s + 1) * P)
                mm = eng.matmul(m.ps[:, 4, sl], q0T[b][:, sl], kvT[b][:, sl], start=True, stop=True)
            mm.then_inc(local_ps.sem, 1)

        def turn(g, b):
            eng.wait_ge(k_exp.sem, k_exp.at(g))
            eng.wait_ge(ctx_sb.sem, ctx_sb.at(g - 1))
            settle(eng, m)
            for s in range(TS):
                mm = eng.transpose(m.ps[:, 5, s * C:(s + 1) * C], ekT[:, s * P:(s + 1) * P],
                                   m.cst[0:C, AT["ident"][0]:AT["ident"][0] + C])
            mm.then_inc(k_turn.sem, 1)
            eng.wait_ge(q_soft.sem, q_soft.at(g))
            eng.wait_ge(x1_sb.sem, x1_sb.at(g - 1))
            settle(eng, m)
            for s in range(TS):
                mm = eng.transpose(m.ps[0:C, 6, s * P:(s + 1) * P], qs[:, s, :], col(m, "ident"))
            mm.then_inc(q_turn.sem, 1)
            eng.wait_ge(local_prob.sem, local_prob.at(g))
            eng.wait_ge(attn_sb.sem, attn_sb.at(g - 1))
            for s in range(TS):
                mm = eng.transpose(m.ps[:, 7, s * P:(s + 1) * P], lprob[:, s, :], col(m, "ident"))
            mm.then_inc(p_turn.sem, 1)

        def context(g, b):
            eng.wait_ge(k_sb.sem, k_sb.at(g))
            for s in range(TS):
                mm = eng.matmul(m.ps[0:C, 5, 256 + s * C:256 + (s + 1) * C], ek[:, s, :], tok[b][:, s, 0:C],
                                start=True, stop=True)
            mm.then_inc(ctx_ps.sem, 1)

        def attend(g, b):
            eng.wait_ge(q_sb.sem, q_sb.at(g))
            eng.wait_ge(p_sb.sem, p_sb.at(g))
            eng.wait_ge(ctx_sb.sem, ctx_sb.at(g))
            eng.wait_ge(v0_sb.sem, v0_sb.at(g))
            settle(eng, m)
            for s in range(TS):
                sl = slice(s * P, (s + 1) * P)
                eng.matmul(m.ps[0:C, 7, sl], ctxm[:, s, :], qsT[:, sl], start=True, stop=False)
                mm = eng.matmul(m.ps[0:C, 7, sl], v0[b][:, s, :], lprobT[:, s, :], start=False, stop=True)
            mm.then_inc(attn_ps.sem, 1)

        def out(g, b):
            eng.wait_ge(attn_sb.sem, attn_sb.at(g))
            for s in range(TS):
                mm = eng.matmul(m.ps[:, 6, s * C:(s + 1) * C], aT[:, s * P:(s + 1) * P],
                                col(m, "wproj", slice(0, C + 1)), start=True, stop=True)
            mm.then_inc(y_ps.sem, 1)

        def rest(g, b, left, back):
            if left is not None:
                local(g, b)
            if back:
                turn(g - 1, 1 - b)
            if left:
                T.pe(eng, g + 1, 1 - b)
            if back:
                context(g - 1, 1 - b)
                attend(g - 1, 1 - b)
            if left:
                project(g + 1, 1 - b)
            if back:
                out(g - 1, 1 - b)

        eng.wait_ge(*before)
        eng.wait_ge(m.cst2_sem, 16)
        h = slice(0, C)
        eng.matmul(m.ps[:, 0, 0:1], col(m, "wkv2", h), col(m, "n1b", h), start=True, stop=True).then_inc(pre, 1)
        eng.matmul(m.ps[:, 1, 0:1], col(m, "wq2", h), col(m, "n1b", h), start=True, stop=True).then_inc(pre, 1)
        eng.matmul(m.ps[:, 2, 0:P], col(m, "n1b", h).broadcast_to([C, P]), col(m, "wtok", h),
                   start=True, stop=True).then_inc(pre, 1)
        eng.wait_ge(pre_sb, 3)
        for w in (w_kv, w_q, w_tok):
            eng.wait_ge(w.sem, 3)
        eng.wait_ge(once, 3)
        lagged(eng, TG, ahead, rest)

    def dve(eng):
        def tokens(g, b):
            eng.wait_ge(proj_ps.sem, proj_ps.at(g))
            eng.wait_ge(ctx_ps.sem, ctx_ps.at(g - 2))
            eng.wait_ge(v0_sb.sem, v0_sb.at(g - 2))
            eng.tensor_tensor(tok[b][:, :, :], m.ps[:, 3, :].rearrange("p (s n) -> p s n", s=TS),
                              bias_tok[:, :].unsqueeze(1).broadcast_to([P, TS, P]),
                              ALU.add).then_inc(tok_sb.sem, 1)

        def ahead(g, b):
            T.dve(eng, g, b)
            tokens(g, b)

        def key_maxima(g, b):
            eng.wait_ge(kv_sb.sem, kv_sb.at(g))
            eng.tensor_reduce(kmax[:, :], kvT[b][0:C, :].rearrange("p (s t) -> p s t", s=TS), AX,
                              ALU.max).then_inc(k_neg.sem, 1)
            eng.wait_ge(k_neg.sem, k_neg.at(g, 1))
            eng.wait_ge(k_exp.sem, k_exp.at(g - 1))
            eng.tensor_scalar(kneg[:, :], kmax[:, :], -1.0, None, ALU.mult).then_inc(k_neg.sem, 1)

        def maxima(g, b):
            eng.wait_ge(tok_sb.sem, tok_sb.at(g))
            eng.wait_ge(q_diff.sem, q_diff.at(g - 1))
            eng.tensor_reduce(qmax[:, :].rearrange("p (s h) -> p s h", s=TS),
                              tok[b][:, :, C:P].rearrange("p s (h d) -> p s h d", d=HD), AX,
                              ALU.max).then_inc(q_max.sem, 1)
            eng.wait_ge(local_ps.sem, local_ps.at(g))
            eng.tensor_reduce(lmax[:, :], m.ps[:, 4, :].rearrange("p (s t) -> p s t", s=TS), AX,
                              ALU.max).then_inc(local_neg.sem, 1)
            eng.wait_ge(local_neg.sem, local_neg.at(g, 1))
            eng.wait_ge(local_exp.sem, local_exp.at(g - 1))
            eng.tensor_scalar(lneg[:, :], lmax[:, :], -SCALE, None, ALU.mult).then_inc(local_neg.sem, 1)

        def sums(g, b):
            eng.wait_ge(k_exp.sem, k_exp.at(g))
            eng.wait_ge(mask_sb.sem, mask_sb.at(g - 1))
            eng.reciprocal(krec[:, :], ksum[:, :]).then_inc(k_rec.sem, 1)
            eng.wait_ge(q_exp.sem, q_exp.at(g))
            eng.tensor_reduce(qsum[:, :], qe[:, :, :].rearrange("p s (h d) -> p (s h) d", d=HD), AX,
                              ALU.add).then_inc(q_rec.sem, 1)
            eng.wait_ge(q_rec.sem, q_rec.at(g, 1))
            eng.wait_ge(q_soft.sem, q_soft.at(g - 1))
            eng.reciprocal(qrec[:, :], qsum[:, :]).then_inc(q_rec.sem, 1)
            eng.wait_ge(local_exp.sem, local_exp.at(g))
            eng.wait_ge(local_prob.sem, local_prob.at(g - 1))
            eng.reciprocal(lrec[:, :], lsum[:, :]).then_inc(local_rec.sem, 1)

        def keys(g, b):
            eng.wait_ge(k_turn.sem, k_turn.at(g))
            eng.wait_ge(ctx_ps.sem, ctx_ps.at(g - 1))
            eng.tensor_copy(ek[:, :, :], m.ps[:, 5, 0:TS * C].rearrange("p (s c) -> p s c", s=TS)).then_inc(k_sb.sem, 1)

        def context(g, b):
            eng.wait_ge(ctx_ps.sem, ctx_ps.at(g))
            eng.wait_ge(mask_sb.sem, mask_sb.at(g))
            eng.wait_ge(attn_ps.sem, attn_ps.at(g - 1))
            eng.scalar_tensor_tensor(out=ctxm[:, :, :], in0=m.ps[0:C, 5, 256:512].rearrange("p (s c) -> p s c", s=TS),
                                     scalar=SCALE, in1=mask[:, :, :], op0=ALU.mult, op1=ALU.mult).then_inc(ctx_sb.sem, 1)

        def out(g, b):
            rows = m.y[:, bass.ds(g * TS, TS), :]
            eng.wait_ge(y_ps.sem, y_ps.at(g))
            eng.tensor_tensor(rows, m.ps[:, 6, 0:TS * C].rearrange("p (s c) -> p s c", s=TS), rows,
                              ALU.add).then_inc(x1_sb.sem, 1)

        def count(g):
            eng.wait_ge(x1_sb.sem, x1_sb.at(g))
            stats(eng, m, m.y, g, TS, x1_stat.sem)

        def rest(g, b, left, back):
            if back:
                keys(g - 1, 1 - b)
            if left is not None:
                key_maxima(g, b)
            if back:
                context(g - 1, 1 - b)
            if left is not None:
                maxima(g, b)
            if left:
                T.dve(eng, g + 1, 1 - b)
            if left is not None:
                sums(g, b)
            if not isinstance(g, int) or g >= 2:
                count(g - 2)
            if left:
                tokens(g + 1, 1 - b)
            if back:
                out(g - 1, 1 - b)

        eng.wait_ge(m.cst2_sem, 16)
        w_kv.make(eng, col(m, "wkv2"), col(m, "n1g"))
        w_q.make(eng, col(m, "wq2"), col(m, "n1g"))
        w_tok.make(eng, col(m, "wtok"), col(m, "n1g"))
        eng.wait_ge(pre, 3)
        eng.tensor_copy(bias_kv[:, :], m.ps[:, 0, 0:1]).then_inc(pre_sb, 1)
        eng.tensor_copy(bias_q[:, :], m.ps[:, 1, 0:1]).then_inc(pre_sb, 1)
        eng.tensor_copy(bias_tok[:, :], m.ps[:, 2, 0:P]).then_inc(pre_sb, 1)
        eng.wait_ge(pre_sb, 3)
        lagged(eng, TG, ahead, rest)
        count(TG - 1)

    def act(eng):
        def project(g, b):
            eng.wait_ge(proj_ps.sem, proj_ps.at(g, 1))
            eng.wait_ge(local_ps.sem, local_ps.at(g - 2))
            eng.wait_ge(k_exp.sem, k_exp.at(g - 2))
            nc.scalar.activation(kvT[b][:, :], m.ps[:, 1, :], ACT.Identity, bias=bias_kv[:, :]).then_inc(kv_sb.sem, 1)
            nc.scalar.activation(q0T[b][:, :], m.ps[:, 2, :], ACT.Identity, bias=bias_q[:, :]).then_inc(q0_sb.sem, 1)

        def ahead(g, b):
            T.act(eng, g, b, proj_ps)
            project(g, b)

        def keys(g, b):
            eng.wait_ge(k_neg.sem, k_neg.at(g))
            eng.wait_ge(k_turn.sem, k_turn.at(g - 1))
            for s in range(TS):
                sl = slice(s * P, (s + 1) * P)
                nc.scalar.activation(ekT[:, sl], kvT[b][0:C, sl], ACT.Exp, bias=kneg[:, s:s + 1],
                                     accum_out=ksum[:, s:s + 1]).then_inc(k_exp.sem, 1)

        def queries(g, b):
            eng.wait_ge(q_diff.sem, q_diff.at(g))
            eng.wait_ge(q_soft.sem, q_soft.at(g - 1))
            nc.scalar.activation(qe[:, :, :], qd[:, :, :], ACT.Exp).then_inc(q_exp.sem, 1)

        def local(g, b):
            eng.wait_ge(local_neg.sem, local_neg.at(g))
            eng.wait_ge(local_prob.sem, local_prob.at(g - 1))
            for s in range(TS):
                nc.scalar.activation(lex[:, s, :], m.ps[:, 4, s * P:(s + 1) * P], ACT.Exp, bias=lneg[:, s:s + 1],
                                     scale=SCALE, accum_out=lsum[:, s:s + 1]).then_inc(local_exp.sem, 1)

        def turned(g, b):
            eng.wait_ge(q_turn.sem, q_turn.at(g))
            eng.wait_ge(attn_ps.sem, attn_ps.at(g - 1))
            nc.scalar.activation(qsT[:, :], m.ps[0:C, 6, :], ACT.Identity).then_inc(q_sb.sem, 1)
            eng.wait_ge(p_turn.sem, p_turn.at(g))
            nc.scalar.activation(lprobT[:, :, :].rearrange("p s t -> p (s t)"), m.ps[:, 7, :],
                                 ACT.Identity).then_inc(p_sb.sem, 1)

        def attended(g, b):
            eng.wait_ge(attn_ps.sem, attn_ps.at(g))
            eng.wait_ge(y_ps.sem, y_ps.at(g - 1))
            nc.scalar.activation(aT[0:C, :], m.ps[0:C, 7, :], ACT.Identity).then_inc(attn_sb.sem, 1)

        def rest(g, b, left, back):
            if back:
                turned(g - 1, 1 - b)
            if left:
                T.act(eng, g + 1, 1 - b, proj_ps)
            if left is not None:
                keys(g, b)
                queries(g, b)
                local(g, b)
            if back:
                attended(g - 1, 1 - b)
            if left:
                project(g + 1, 1 - b)

        eng.preload_act_table(ACT.Exp)
        eng.wait_ge(pre_sb, 3)
        lagged(eng, TG, ahead, rest)

    return dict(pool=pool, pe=pe, dve=dve, act=act)


def mlp0(nc, ctx, m):
    def sb(name, shape, dt=F32):
        return m.mem.enter_context(nc.sbuf_tensor("m0_" + name, shape, dt))

    def step(name, per=1):
        return Step(nc, ctx, m, "m0_" + name, per)

    m.rounds = TG
    T = Turned(nc, ctx, m, "m0", m.y, 0)
    w1 = m.split["wm1"]
    hid = [[sb(f"hid{b}{n}", [P, NT]) for n in range(2)] for b in range(2)]
    bias = sb("bias", [P, 2])
    pre = ctx.enter_context(nc.semaphore("m0_bias_ps"))
    pre_sb = ctx.enter_context(nc.semaphore("m0_bias_sb"))
    base_sb = step("base_sb", 2)
    hid_ps, hid_sb = step("hid_ps", 2), step("hid_sb", 2)
    out_ps, h_sb, h_stat = step("out_ps"), step("h_sb"), step("h_stat", TS)
    before = m.stat_last
    m.h_last, m.h_rounds, m.stat_last = h_sb, TG - 1, (h_stat.sem, h_stat.at(TG - 1))

    def pool(eng):
        def ahead(g, b):
            T.pool(eng, g, b, hid_ps)
            sl = bass.ds(g * TS, TS)
            settle(eng, m)
            eng.tensor_tensor(m.h[:, sl, :], m.h[:, sl, :], m.y[:, sl, :], ALU.add).then_inc(base_sb.sem, 1)
            eng.wait_ge(base_sb.sem, base_sb.at(g, 1))
            settle(eng, m)
            eng.tensor_tensor(m.h[:, sl, :], m.h[:, sl, :],
                              col(m, "bm2r").unsqueeze(1).broadcast_to([P, TS, C]), ALU.add).then_inc(base_sb.sem, 1)

        eng.wait_ge(*T.norm)
        lagged(eng, TG, ahead, lambda g, b, left, back: ahead(g + 2, b) if (left or 0) > 1 else None, early=1)

    def pe(eng):
        def hidden(g, b):
            eng.wait_ge(T.lo_sb.sem, T.lo_sb.at(g))
            for c in range(2):
                eng.wait_ge(hid_sb.sem, hid_sb.at(g - 1, c + 1))
                sl = slice(c * P, (c + 1) * P)
                eng.matmul(m.ps[:, 1 + c, :], w1.hi[:, sl], T.xs[b][:, :], start=True, stop=False)
                eng.matmul(m.ps[:, 1 + c, :], w1.lo[:, sl], T.xs[b][:, :], start=False,
                           stop=True).then_inc(hid_ps.sem, 1)

        def out(g, b):
            eng.wait_ge(h_sb.sem, h_sb.at(g - 1))
            eng.wait_ge(hid_sb.sem, hid_sb.at(g))
            a = AT["wm2"][0]
            for s in range(TS):
                sl = slice(s * P, (s + 1) * P)
                for c in range(2):
                    mm = eng.matmul(m.ps[:, 3, s * C:(s + 1) * C], hid[b][c][:, sl],
                                    m.cst[:, a + c * C:a + (c + 1) * C], start=(c == 0), stop=(c == 1))
            mm.then_inc(out_ps.sem, 1)

        def rest(g, b, left, back):
            if left is not None:
                hidden(g, b)
            if left:
                T.pe(eng, g + 1, 1 - b)
            if back:
                out(g - 1, 1 - b)

        eng.wait_ge(*before)
        h = slice(0, C)
        a = AT["wm1"][0]
        for c in range(2):
            eng.matmul(m.ps[:, c, 0:1], m.cst[h, a + c * P:a + (c + 1) * P], col(m, "n2b", h),
                       start=True, stop=True).then_inc(pre, 1)
        eng.wait_ge(pre_sb, 2)
        eng.wait_ge(w1.sem, 3)
        lagged(eng, TG, lambda g, b: T.pe(eng, g, b), rest)

    def dve(eng):
        def rest(g, b, left, back):
            if left:
                T.dve(eng, g + 1, 1 - b)
            if back:
                rows = bass.ds(g * TS - TS, TS)
                eng.wait_ge(out_ps.sem, out_ps.at(g - 1))
                eng.wait_ge(base_sb.sem, base_sb.at(g - 1))
                eng.tensor_tensor(m.h[:, rows, :], m.ps[:, 3, 0:TS * C].rearrange("p (s c) -> p s c", s=TS),
                                  m.h[:, rows, :], ALU.add).then_inc(h_sb.sem, 1)
                eng.wait_ge(h_sb.sem, h_sb.at(g - 1))
                stats(eng, m, m.h, g - 1, TS, h_stat.sem)

        w1.make(eng, col(m, "wm1"), col(m, "n2g"))
        eng.wait_ge(pre, 2)
        for c in range(2):
            eng.tensor_tensor(bias[:, c:c + 1], m.ps[:, c, 0:1], m.cst[:, AT["bm1"][0] + c:AT["bm1"][0] + c + 1],
                              ALU.add).then_inc(pre_sb, 1)
        lagged(eng, TG, lambda g, b: T.dve(eng, g, b), rest)

    def act(eng):
        def rest(g, b, left, back):
            for c in range(0 if left is None else 2):
                eng.wait_ge(hid_ps.sem, hid_ps.at(g, c + 1))
                eng.wait_ge(out_ps.sem, out_ps.at(g - 2))
                nc.scalar.activation(hid[b][c][:, :], m.ps[:, 1 + c, :], ACT.Gelu,
                                     bias=bias[:, c:c + 1]).then_inc(hid_sb.sem, 1)
                if c == 0 and left:
                    T.act(eng, g + 1, 1 - b, hid_ps)

        eng.preload_act_table(ACT.Gelu)
        eng.wait_ge(pre_sb, 2)
        lagged(eng, TG, lambda g, b: T.act(eng, g, b, hid_ps), rest)

    return dict(pool=pool, pe=pe, dve=dve, act=act)


def experts0(nc, ctx, m):
    def sb(name, shape, dt=F32):
        return m.mem.enter_context(nc.sbuf_tensor("e0_" + name, shape, dt))

    def step(name, per=1):
        return Step(nc, ctx, m, "e0_" + name, per)

    m.rounds = TG
    E, RING = EXPERTS0, 3
    T = Turned(nc, ctx, m, "e0", m.h, 0)
    gate = m.split["gatew"]
    w1_hi, w1_lo = m.ew1_hi, m.ew1_lo
    w2 = m.ew2_sb
    logit, hot1, hot2, wt = (sb(n, [P, TS, E]) for n in ("logit", "hot1", "hot2", "wt"))
    top, idx = sb("top", [P, TS, 8]), sb("idx", [P, TS, 8], U32)
    idxf = sb("idxf", [P, TS, 2])
    gap, gexp, den, g1, g2 = (sb(n, [P, TS]) for n in ("gap", "gexp", "den", "g1", "g2"))
    wT = sb("wT", [E, NT])
    hid = [sb(f"hid{n}", [P, NT]) for n in range(RING)]
    part = [sb(f"part{n}", [P, TS, C]) for n in range(RING)]
    acc = sb("acc", [P, TS, C])
    logit_ps, logit_sb, top_sb = step("logit_ps"), step("logit_sb"), step("top_sb", TS)
    idx_sb, idxf_sb, gap_sb, gexp_sb = step("idx_sb", TS), step("idxf_sb"), step("gap_sb"), step("gexp_sb")
    hot_sb, soft_sb, wt_sb = step("hot_sb", 2), step("soft_sb", 3), step("wt_sb", 3)
    wT_ps, wT_sb, b2_ps, y_sb = step("wT_ps"), step("wT_sb"), step("b2_ps"), step("y_sb")
    hid_ps, hid_sb, out_ps = step("hid_ps", E), step("hid_sb", E), step("out_ps", E)
    part_sb, sum_sb, y_stat = step("part_sb", E), step("sum_sb", E), step("y_stat", TS)
    beta_sb = step("beta_sb")
    before = m.stat_last
    m.stat_last = (y_stat.sem, y_stat.at(TG - 1))
    m.beta_last = (beta_sb.sem, beta_sb.at(TG - 1))

    def pool(eng):
        def ahead(g, b, k):
            if k in (0, None):
                T.pool(eng, g, b, y_sb)
                sl = bass.ds(g * TS, TS)
                eng.wait_ge(T.norm_sb.sem, T.norm_sb.at(g, 1))
                settle(eng, m)
                eng.tensor_tensor(m.h[:, sl, :], m.h[:, sl, :], col(m, "betr").unsqueeze(1).broadcast_to([P, TS, C]),
                                  ALU.add).then_inc(beta_sb.sem, 1)

        def rest(g, b, ahead):
            eng.wait_ge(hot_sb.sem, hot_sb.at(g))
            eng.wait_ge(soft_sb.sem, soft_sb.at(g))
            sh = [P, TS, E]
            eng.tensor_tensor(hot1[:, :, :], hot1[:, :, :], bc(g1[:, :], sh), ALU.mult).then_inc(wt_sb.sem, 1)
            eng.tensor_tensor(hot2[:, :, :], hot2[:, :, :], bc(g2[:, :], sh), ALU.mult).then_inc(wt_sb.sem, 1)
            eng.wait_ge(wt_sb.sem, wt_sb.at(g, 2))
            eng.wait_ge(part_sb.sem, part_sb.at(g - 1))
            eng.wait_ge(wT_ps.sem, wT_ps.at(g - 1))
            eng.tensor_tensor(wt[:, :, :], hot1[:, :, :], hot2[:, :, :], ALU.add).then_inc(wt_sb.sem, 1)
            for e in range(E):
                eng.wait_ge(part_sb.sem, part_sb.at(g, e + 1))
                if e == 0:
                    eng.wait_ge(y_sb.sem, y_sb.at(g - 1))
                else:
                    eng.wait_ge(sum_sb.sem, sum_sb.at(g, e))
                eng.tensor_tensor(acc[:, :, :], T.xn[b] if e == 0 else acc[:, :, :], part[e % RING][:, :, :],
                                  ALU.add).then_inc(sum_sb.sem, 1)
                if e == 4:
                    ahead(0)

        eng.wait_ge(*T.norm)
        skewed(eng, TG, rest, ahead)

    def pe(eng):
        def ahead(g, b, k):
            T.pe(eng, g, b)

        def rest(g, b, ahead):
            eng.wait_ge(T.lo_sb.sem, T.lo_sb.at(g))
            eng.wait_ge(y_sb.sem, y_sb.at(g - 1))
            for s in range(TS):
                sl = slice(s * P, (s + 1) * P)
                eng.matmul(m.ps[:, 1, s * E:(s + 1) * E], T.xs[b][:, sl], gate.hi[:, :], start=True, stop=False)
                mm = eng.matmul(m.ps[:, 1, s * E:(s + 1) * E], T.xs[b][:, sl], gate.lo[:, :], start=False, stop=True)
            mm.then_inc(logit_ps.sem, 1)

            def hidden(e):
                if e < RING:
                    eng.wait_ge(hid_sb.sem, hid_sb.at(g - 1))
                else:
                    eng.wait_ge(hid_sb.sem, hid_sb.at(g, e - RING + 1))
                sl = slice(e * F0, (e + 1) * F0)
                eng.matmul(m.ps[:, 2 + e % RING, :], w1_hi[:, sl], T.xs[b][:, :], start=True, stop=False)
                eng.matmul(m.ps[:, 2 + e % RING, :], w1_lo[:, sl], T.xs[b][:, :], start=False,
                           stop=True).then_inc(hid_ps.sem, 1)

            def out(e):
                eng.wait_ge(hid_sb.sem, hid_sb.at(g, e + 1))
                if e < RING:
                    eng.wait_ge(part_sb.sem, part_sb.at(g - 1))
                else:
                    eng.wait_ge(part_sb.sem, part_sb.at(g, e - RING + 1))
                for s in range(TS):
                    mm = eng.matmul(m.ps[:, 5 + e % RING, s * P:(s + 1) * P], hid[e % RING][:, s * P:(s + 1) * P],
                                    w2[:, e * C:e * C + P], start=True, stop=True)
                mm.then_inc(out_ps.sem, 1)

            hidden(0)
            hidden(1)
            for e in range(E):
                if e + 2 < E:
                    hidden(e + 2)
                out(e)
                if e == 3:
                    eng.wait_ge(wt_sb.sem, wt_sb.at(g))
                    for s in range(TS):
                        mm = eng.transpose(m.ps[0:E, 1, s * P:(s + 1) * P], wt[:, s, :], col(m, "ident"))
                    mm.then_inc(wT_ps.sem, 1)
                if e == 5:
                    eng.wait_ge(wT_sb.sem, wT_sb.at(g))
                    for s in range(TS):
                        mm = eng.matmul(m.ps[:, 1, s * C:(s + 1) * C], wT[:, s * P:(s + 1) * P],
                                        col(m, "eb2", slice(0, E)), start=True, stop=True)
                    mm.then_inc(b2_ps.sem, 1)
                if e == 10:
                    ahead(0)

        eng.wait_ge(*before)
        eng.wait_ge(gate.sem, 3)
        eng.wait_ge(m.ew_split, 2)
        eng.wait_ge(m.ew2_sem, 16)
        eng.wait_ge(m.ew2_pad, 1)
        skewed(eng, TG, rest, ahead)

    def dve(eng):
        def ahead(g, b, k):
            T.dve(eng, g, b)

        def rest(g, b, ahead):
            eng.wait_ge(logit_ps.sem, logit_ps.at(g))
            eng.tensor_tensor(logit[:, :, :], m.ps[:, 1, 0:TS * E].rearrange("p (s e) -> p s e", s=TS),
                              col(m, "gatebr").unsqueeze(1).broadcast_to([P, TS, E]), ALU.add).then_inc(logit_sb.sem, 1)
            eng.wait_ge(logit_sb.sem, logit_sb.at(g))
            eng.wait_ge(gap_sb.sem, gap_sb.at(g - 1))
            settle(eng, m)
            for s in range(TS):
                eng.max(top[:, s, :], logit[:, s, :]).then_inc(top_sb.sem, 1)
            eng.wait_ge(top_sb.sem, top_sb.at(g))
            settle(eng, m)
            for s in range(TS):
                eng.max_index(idx[:, s, :], top[:, s, :], logit[:, s, :]).then_inc(idx_sb.sem, 1)
            eng.wait_ge(gexp_sb.sem, gexp_sb.at(g - 1))
            eng.tensor_tensor(gap[:, :], top[:, :, 1], top[:, :, 0], ALU.subtract).then_inc(gap_sb.sem, 1)
            eng.wait_ge(idx_sb.sem, idx_sb.at(g))
            eng.tensor_copy(idxf[:, :, :], idx[:, :, 0:2]).then_inc(idxf_sb.sem, 1)
            eng.wait_ge(idxf_sb.sem, idxf_sb.at(g))
            eng.wait_ge(wt_sb.sem, wt_sb.at(g - 1))
            sh = [P, TS, E]
            for n, hot in enumerate((hot1, hot2)):
                eng.tensor_tensor(hot[:, :, :], col(m, "iota16").unsqueeze(1).broadcast_to(sh),
                                  bc(idxf[:, :, n], sh), ALU.is_equal).then_inc(hot_sb.sem, 1)
            eng.wait_ge(gexp_sb.sem, gexp_sb.at(g))
            eng.tensor_scalar(den[:, :], gexp[:, :], 1.0, None, ALU.add).then_inc(soft_sb.sem, 1)
            eng.wait_ge(soft_sb.sem, soft_sb.at(g, 1))
            eng.reciprocal(g1[:, :], den[:, :]).then_inc(soft_sb.sem, 1)
            eng.wait_ge(soft_sb.sem, soft_sb.at(g, 2))
            eng.tensor_tensor(g2[:, :], gexp[:, :], g1[:, :], ALU.mult).then_inc(soft_sb.sem, 1)
            eng.wait_ge(wt_sb.sem, wt_sb.at(g))
            for e in range(E):
                eng.wait_ge(out_ps.sem, out_ps.at(g, e + 1))
                if e < RING:
                    eng.wait_ge(sum_sb.sem, sum_sb.at(g - 1))
                else:
                    eng.wait_ge(sum_sb.sem, sum_sb.at(g, e - RING + 1))
                eng.tensor_tensor(part[e % RING][:, :, :],
                                  m.ps[:, 5 + e % RING, :].rearrange("p (s c) -> p s c", s=TS)[:, :, 0:C],
                                  bc(wt[:, :, e], [P, TS, C]), ALU.mult).then_inc(part_sb.sem, 1)
                if e == 12:
                    ahead(0)
            eng.wait_ge(b2_ps.sem, b2_ps.at(g))
            eng.wait_ge(sum_sb.sem, sum_sb.at(g))
            eng.tensor_tensor(m.y[:, bass.ds(g * TS, TS), :], m.ps[:, 1, 0:TS * C].rearrange("p (s c) -> p s c", s=TS),
                              acc[:, :, :], ALU.add).then_inc(y_sb.sem, 1)
            eng.wait_ge(y_sb.sem, y_sb.at(g))
            stats(eng, m, m.y, g, TS, y_stat.sem)

        gate.make(eng, col(m, "gatew"))
        eng.wait_ge(m.ew1_sem, 16)
        eng.tensor_copy(w1_hi[:, :], m.ew1_f[:, :]).then_inc(m.ew_split, 1)
        eng.wait_ge(m.ew_split, 1)
        eng.tensor_tensor(w1_lo[:, :], m.ew1_f[:, :], w1_hi[:, :].bitcast(F32), ALU.subtract).then_inc(m.ew_split, 1)
        skewed(eng, TG, rest, ahead)

    def act(eng):
        def ahead(g, b, k):
            T.act(eng, g, b, hid_ps)

        def rest(g, b, ahead):
            eng.wait_ge(gap_sb.sem, gap_sb.at(g))
            eng.wait_ge(soft_sb.sem, soft_sb.at(g - 1))
            nc.scalar.activation(gexp[:, :], gap[:, :], ACT.Exp).then_inc(gexp_sb.sem, 1)
            for e in range(E):
                eng.wait_ge(hid_ps.sem, hid_ps.at(g, e + 1))
                if e < RING:
                    eng.wait_ge(out_ps.sem, out_ps.at(g - 1))
                else:
                    eng.wait_ge(out_ps.sem, out_ps.at(g, e - RING + 1))
                nc.scalar.activation(hid[e % RING][:, :], m.ps[:, 2 + e % RING, :], ACT.Relu,
                                     bias=m.cst[:, AT["eb1"][0] + e:AT["eb1"][0] + e + 1]).then_inc(hid_sb.sem, 1)
                if e == 6:
                    eng.wait_ge(wT_ps.sem, wT_ps.at(g))
                    eng.wait_ge(b2_ps.sem, b2_ps.at(g - 1))
                    nc.scalar.activation(wT[:, :], m.ps[0:E, 1, :], ACT.Identity).then_inc(wT_sb.sem, 1)
                if e == 11:
                    ahead(0)

        eng.preload_act_table(ACT.Exp)
        skewed(eng, TG, rest, ahead)

    return dict(pool=pool, pe=pe, dve=dve, act=act)


def spread0(nc, ctx, m):
    N = 8
    m.rounds = S // N
    def step(name, per=1):
        return Step(nc, ctx, m, "s0_" + name, per)

    xn = [m.mem.enter_context(nc.sbuf_tensor(f"s0_xn{b}", [P, N, C], F32)) for b in range(2)]
    t = m.mem.enter_context(nc.sbuf_tensor("s0_t", [P, N, C], F32))
    norm_sb, mul_sb, h_sb, h_stat = step("norm_sb", 2), step("mul_sb"), step("h_sb"), step("h_stat", N)
    ready = (m.norm_ready, m.norm_value)
    mean, rstd = m.norm_tiles[6:8]
    m.h_last, m.h_rounds, m.stat_last = h_sb, S // N - 1, (h_stat.sem, h_stat.at(S // N - 1))
    sh = [P, N, C]

    def pool(eng):
        def round_(g, b):
            sl = bass.ds(g * N, N)
            eng.wait_ge(mul_sb.sem, mul_sb.at(g - 2))
            settle(eng, m)
            eng.tensor_tensor(xn[b][:, :, :], m.y[:, sl, :], bc(mean[:, sl], sh), ALU.subtract).then_inc(norm_sb.sem, 1)
            eng.wait_ge(norm_sb.sem, norm_sb.at(g, 1))
            eng.tensor_tensor(xn[b][:, :, :], xn[b][:, :, :], bc(rstd[:, sl], sh), ALU.mult).then_inc(norm_sb.sem, 1)

        eng.wait_ge(*ready)
        with eng.Fori(0, S // N // 2) as i:
            round_(2 * i, 0)
            round_(2 * i + 1, 1)

    def dve(eng):
        def round_(g, b):
            sl = bass.ds(g * N, N)
            eng.wait_ge(norm_sb.sem, norm_sb.at(g))
            eng.wait_ge(h_sb.sem, h_sb.at(g - 1))
            eng.tensor_tensor(t[:, :, :], xn[b][:, :, :], col(m, "gamr").unsqueeze(1).broadcast_to(sh),
                              ALU.mult).then_inc(mul_sb.sem, 1)
            eng.wait_ge(mul_sb.sem, mul_sb.at(g))
            eng.tensor_tensor(m.h[:, sl, :], m.h[:, sl, :], t[:, :, :], ALU.add).then_inc(h_sb.sem, 1)
            eng.wait_ge(h_sb.sem, h_sb.at(g))
            stats(eng, m, m.h, g, N, h_stat.sem)

        eng.wait_ge(*m.beta_last)
        with eng.Fori(0, S // N // 2) as i:
            round_(2 * i, 0)
            round_(2 * i + 1, 1)

    return dict(pool=pool, dve=dve)


def attention1(nc, ctx, m):
    def sb(name, shape, dt=F32):
        return m.mem.enter_context(nc.sbuf_tensor("a1_" + name, shape, dt))

    def step(name, per=1):
        return Step(nc, ctx, m, "a1_" + name, per)

    m.rounds = TG
    H, V, W = HEADS, C + 1, 96
    T = Turned(nc, ctx, m, "a1", m.h, 0)
    w_a, w_m = Split(nc, ctx, "a1_a", H * C, m.mem), Split(nc, ctx, "a1_m", H * C, m.mem)
    xt = [[sb(f"xt{h}{b}", [P, NT]) for b in range(2)] for h in range(2)]
    u = [sb(f"u{b}", [P, TS, H // 2, P]) for b in range(2)]
    v = [sb(f"v{b}", [P, TS, H * V + W - V]) for b in range(2)]
    diff = sb("diff", [P, H, P])
    ex = [sb(f"ex{b}", [P, H, P]) for b in range(2)]
    prob = [sb(f"prob{b}", [P, H, P]) for b in range(2)]
    rmax, rec = sb("rmax", [P, H]), sb("rec", [P, H])
    part, sum4, sum2, sum1 = (sb(n, [P, k, C]) for n, k in (("part", H), ("sum4", 4), ("sum2", 2), ("sum1", 1)))

    w_ps = ctx.enter_context(nc.semaphore("a1_weights_ps"))
    once = ctx.enter_context(nc.semaphore("a1_set_once"))
    base_sb = step("base_sb")
    xt_sb = [step("xt0_sb"), step("xt1_sb")]
    uv_ps, uv_sb = step("uv_ps", 8), step("uv_sb", 8)
    score_ps, max_sb, diff_sb, exp_sb = step("score_ps", TS), step("max_sb", TS), step("diff_sb", TS), step("exp_sb", TS)
    turn_ps, prob_sb = step("turn_ps", TS), step("prob_sb", TS)
    sum_ps, rec_sb, part_sb = step("sum_ps", TS), step("rec_sb", TS), step("part_sb", TS)
    add_sb, h_sb, h_stat = step("add_sb", 3 * TS), step("h_sb", TS), step("h_stat", TS)
    before = m.stat_last
    m.h_last, m.h_rounds, m.stat_last = h_sb, TG - 1, (h_stat.sem, h_stat.at(TG - 1))

    def rounds(eng, order, turned, piece=None, early=0, **parts):
        lags = dict(now=0, lag1=1, lag2=2, lag3=3)
        slots = {(0, "x1"): lambda g, b: turned(g + early, (b + early) % 2)}
        for n, at in enumerate(((1, "x0"), (1, "x1"), (1, "x2"), (2, "x1"), (2, "x2"), (3, "x0"), (3, "x1"), (3, "x2"))):
            slots[at] = (lambda g, b, n=n: piece(g, b, n)) if piece else None

        def rest(g, b, first=False, more=True):
            for s in range(TS):
                for name in order:
                    if name in lags:
                        back = s - lags[name]
                        if back >= 0:
                            parts[name](g, b, back)
                        elif not first:
                            parts[name](g - 1, 1 - b, back + TS)
                    elif more and slots.get((s, name)):
                        slots[s, name](g + 1, 1 - b)

        for g in range(1 + early):
            turned(g, g % 2)
        for k in range(8 if piece else 0):
            piece(0, 0, k)
        rest(0, 0, first=True)
        rest(1, 1)
        with eng.Fori(1, TG // 2 - 1) as i:
            rest(2 * i, 0)
            rest(2 * i + 1, 1)
        rest(TG - 2, 0, more=not early)
        rest(TG - 1, 1, more=False)
        for s in range(TS, TS + 3):
            for name in order:
                if name in lags and s - lags[name] < TS:
                    parts[name](TG - 1, 1, s - lags[name])

    def sample(g, s):
        return bass.ds(g * TS + s, 1)

    def pool(eng):
        def turned(g, b):
            T.pool(eng, g, b, uv_ps)
            sl = bass.ds(g * TS, TS)
            eng.wait_ge(T.norm_sb.sem, T.norm_sb.at(g, 1))
            settle(eng, m)
            eng.tensor_tensor(m.h[:, sl, :], m.h[:, sl, :],
                              col(m, "boutr").unsqueeze(1).broadcast_to([P, TS, C]), ALU.add).then_inc(base_sb.sem, 1)

        def lag2(g, b, s):
            eng.wait_ge(part_sb.sem, part_sb.at(g, s + 1))
            eng.tensor_tensor(sum4[:, :, :], part[:, 0:4, :], part[:, 4:8, :], ALU.add).then_inc(add_sb.sem, 1)
            eng.wait_ge(add_sb.sem, add_sb.at(g, 3 * s + 1))
            eng.tensor_tensor(sum2[:, :, :], sum4[:, 0:2, :], sum4[:, 2:4, :], ALU.add).then_inc(add_sb.sem, 1)
            eng.wait_ge(add_sb.sem, add_sb.at(g, 3 * s + 2))
            eng.tensor_tensor(sum1[:, :, :], sum2[:, 0:1, :], sum2[:, 1:2, :], ALU.add).then_inc(add_sb.sem, 1)
            eng.wait_ge(add_sb.sem, add_sb.at(g, 3 * s + 3))
            eng.wait_ge(base_sb.sem, base_sb.at(g))
            settle(eng, m)
            eng.tensor_tensor(m.h[:, sample(g, s), :], m.h[:, sample(g, s), :], sum1[:, :, :], ALU.add).then_inc(h_sb.sem, 1)

        eng.wait_ge(*T.norm)
        for b in range(2):
            eng.memset(v[b][:, :, :], 1.0).then_inc(once, 1)
        for b in range(2):
            eng.wait_ge(once, 2 + 2 * b)
            eng.memset(xt[0][b][64:P, :], 0.0).then_inc(once, 1)
            eng.wait_ge(once, 3 + 2 * b)
            eng.memset(xt[1][b][0:64, :], 0.0).then_inc(once, 1)
        eng.wait_ge(once, 6)
        rounds(eng, ("lag2", "x1"), turned, early=1, lag2=lag2)

    def pe(eng):
        def turned(g, b):
            for x in xt_sb:
                eng.wait_ge(x.sem, x.at(g - 1))
            T.pe(eng, g, b)

        def piece(g, b, k):
            if k == 0:
                eng.wait_ge(T.lo_sb.sem, T.lo_sb.at(g))
            if k > 0:
                eng.wait_ge(uv_sb.sem, uv_sb.at(g, k))
            else:
                eng.wait_ge(uv_sb.sem, uv_sb.at(g - 1))
            n = k // 2
            sl = slice(n * P, (n + 1) * P)
            if k % 2 == 0:
                eng.matmul(m.ps[:, 1, :], w_a.hi[:, sl], T.xs[b][:, :], start=True, stop=False)
                mm = eng.matmul(m.ps[:, 1, :], w_a.lo[:, sl], T.xs[b][:, :], start=False, stop=True)
            else:
                eng.matmul(m.ps[:, 1, :], T.xs[b][:, sl], w_m.hi[:, :], start=True, stop=False)
                mm = eng.matmul(m.ps[:, 1, :], T.xs[b][:, sl], w_m.lo[:, :], start=False, stop=True)
            mm.then_inc(uv_ps.sem, 1)

        def now(g, b, s):
            if s == 0:
                eng.wait_ge(uv_sb.sem, uv_sb.at(g))
                for x in xt_sb:
                    eng.wait_ge(x.sem, x.at(g))
                eng.wait_ge(diff_sb.sem, diff_sb.at(g - 1))
            else:
                eng.wait_ge(diff_sb.sem, diff_sb.at(g, s))
            for h in range(2):
                mm = eng.matmul(m.ps[:, 2 + h, :], xt[h][b][:, s * P:(s + 1) * P],
                                u[b][:, s, :, :].rearrange("p h t -> p (h t)"), start=True, stop=True)
            mm.then_inc(score_ps.sem, 1)

        def lag1(g, b, s):
            eng.wait_ge(prob_sb.sem, prob_sb.at(g, s) if s else prob_sb.at(g - 1))
            eng.wait_ge(exp_sb.sem, exp_sb.at(g, s + 1))
            for j in range(H):
                mm = eng.transpose(m.ps[:, 4 + j // 4, (j % 4) * P:(j % 4 + 1) * P], ex[s % 2][:, j, :],
                                   col(m, "ident"))
            mm.then_inc(turn_ps.sem, 1)

        def lag2(g, b, s):
            eng.wait_ge(prob_sb.sem, prob_sb.at(g, s + 1))
            if s > 0:
                eng.wait_ge(part_sb.sem, part_sb.at(g, s))
            else:
                eng.wait_ge(part_sb.sem, part_sb.at(g - 1))
            for j in range(H):
                head = 2 * (j % 4) + j // 4
                mm = eng.matmul(m.ps[:, 6 + j // 4, (j % 4) * P:(j % 4) * P + W], prob[s % 2][:, j, :],
                                v[b][:, s, head * V:head * V + W], start=True, stop=True)
            mm.then_inc(sum_ps.sem, 1)

        eng.wait_ge(*before)
        d = slice(0, C)
        for h in range(H):
            out, dup = slice(h * C, (h + 1) * C), slice(h * P, (h + 1) * P)
            for bank, (l, r) in enumerate((("wkT", "wqT"), ("wvT", "wout"))):
                mm = eng.matmul(m.ps[:, bank, out], col(m, l, d)[:, dup], col(m, r, d)[:, out], start=True, stop=True)
        mm.then_inc(w_ps, 1)
        eng.wait_ge(w_a.sem, 3)
        eng.wait_ge(w_m.sem, 3)
        eng.wait_ge(once, 6)
        rounds(eng, ("now", "x0", "lag1", "x1", "lag2", "x2"), turned, piece, now=now, lag1=lag1, lag2=lag2)

    def dve(eng):
        def turned(g, b):
            T.dve(eng, g, b)
            eng.wait_ge(score_ps.sem, score_ps.at(g - 2))
            eng.tensor_copy(xt[1][b][64:P, :], m.ps[64:P, 0, :]).then_inc(xt_sb[1].sem, 1)

        def now(g, b, s):
            eng.wait_ge(score_ps.sem, score_ps.at(g, s + 1))
            src = m.ps[:, 2:4, :].rearrange("p a (j t) -> p (a j) t", t=P)
            eng.tensor_reduce(rmax[:, :], src, AX, ALU.max).then_inc(max_sb.sem, 1)
            eng.wait_ge(max_sb.sem, max_sb.at(g, s + 1))
            eng.wait_ge(exp_sb.sem, exp_sb.at(g, s) if s else exp_sb.at(g - 1))
            eng.tensor_tensor(diff[:, :, :], src, bc(rmax[:, :], [P, H, P]), ALU.subtract).then_inc(diff_sb.sem, 1)

        def lag2(g, b, s):
            eng.wait_ge(sum_ps.sem, sum_ps.at(g, s + 1))
            src = m.ps[:, 6:8, :].rearrange("p a (j t) -> p (a j) t", t=P)
            eng.reciprocal(rec[:, :], src[:, :, C]).then_inc(rec_sb.sem, 1)
            eng.wait_ge(rec_sb.sem, rec_sb.at(g, s + 1))
            eng.wait_ge(add_sb.sem, add_sb.at(g, 3 * s - 2) if s else add_sb.at(g - 1, 3 * TS - 2))
            eng.tensor_tensor(part[:, :, :], src[:, :, 0:C], bc(rec[:, :], [P, H, C]), ALU.mult).then_inc(part_sb.sem, 1)

        def lag3(g, b, s):
            eng.wait_ge(h_sb.sem, h_sb.at(g, s + 1))
            eng.bn_stats(m.stat[:, sample(g, s), :], m.h[:, sample(g, s), :]).then_inc(h_stat.sem, 1)

        eng.wait_ge(w_ps, 1)
        w_a.make(eng, m.ps[:, 0, :], float(C / H) ** -0.5)
        w_m.make(eng, m.ps[:, 1, :])
        eng.wait_ge(once, 6)
        rounds(eng, ("now", "lag3", "x1", "lag2"), turned, now=now, lag2=lag2, lag3=lag3)

    def act(eng):
        def turned(g, b):
            T.act(eng, g, b, uv_ps)
            eng.wait_ge(score_ps.sem, score_ps.at(g - 2))
            nc.scalar.activation(xt[0][b][0:64, :], m.ps[0:64, 0, :], ACT.Identity).then_inc(xt_sb[0].sem, 1)

        def piece(g, b, k):
            eng.wait_ge(uv_ps.sem, uv_ps.at(g, k + 1))
            n = k // 2
            if k % 2 == 0:
                eng.wait_ge(score_ps.sem, score_ps.at(g - 2))
                nc.scalar.activation(u[b][:, :, n, :], m.ps[:, 1, :].rearrange("p (s t) -> p s t", s=TS),
                                     ACT.Identity).then_inc(uv_sb.sem, 1)
            else:
                eng.wait_ge(sum_ps.sem, sum_ps.at(g - 2))
                nc.scalar.activation(v[b][:, n, 0:H * V].rearrange("p (h c) -> p h c", c=V)[:, :, 0:C],
                                     m.ps[:, 1, :].rearrange("p (h c) -> p h c", c=C), ACT.Identity).then_inc(uv_sb.sem, 1)

        def now(g, b, s):
            eng.wait_ge(diff_sb.sem, diff_sb.at(g, s + 1))
            eng.wait_ge(turn_ps.sem, turn_ps.at(g, s - 1) if s >= 2 else turn_ps.at(g - 1, s + 3))
            nc.scalar.activation(ex[s % 2][:, :, :], diff[:, :, :], ACT.Exp).then_inc(exp_sb.sem, 1)

        def lag1(g, b, s):
            eng.wait_ge(turn_ps.sem, turn_ps.at(g, s + 1))
            eng.wait_ge(sum_ps.sem, sum_ps.at(g, s - 1) if s >= 2 else sum_ps.at(g - 1, s + 3))
            nc.scalar.activation(prob[s % 2][:, :, :], m.ps[:, 4:6, :].rearrange("p a (j t) -> p (a j) t", t=P),
                                 ACT.Identity).then_inc(prob_sb.sem, 1)

        eng.preload_act_table(ACT.Exp)
        eng.wait_ge(once, 6)
        rounds(eng, ("x0", "lag1", "x1", "now", "x2"), turned, piece, now=now, lag1=lag1)

    return dict(pool=pool, pe=pe, dve=dve, act=act)


def experts1(nc, ctx, m):
    def sb(name, shape, dt=F32):
        return m.mem.enter_context(nc.sbuf_tensor("e1_" + name, shape, dt))

    def step(name, per=1):
        return Step(nc, ctx, m, "e1_" + name, per)

    m.rounds = TG
    E, NC = EXPERTS1, HID1 // P
    T = Turned(nc, ctx, m, "e1", m.h, 0)
    rout, w1 = m.split["routw"], m.split["fw1"]
    sel = sb("sel", [E, HID1], BF16)
    logit, hot = sb("logit", [P, TS, E]), sb("hot", [P, TS, E])
    top, idx, idxf = sb("top", [P, TS, 8]), sb("idx", [P, TS, 8], U32), sb("idxf", [P, TS])
    hotT, hotT16 = sb("hotT", [E, NT]), sb("hotT16", [E, NT], BF16)
    hid = [sb(f"hid{n}", [P, NT]) for n in range(NC)]
    kept = [sb(f"kept{n}", [P, NT]) for n in range(NC)]
    res = [sb(f"res{b}", [P, TS, C]) for b in range(2)]
    sel_sb = ctx.enter_context(nc.semaphore("e1_sel"))
    logit_ps, logit_sb, top_sb = step("logit_ps"), step("logit_sb"), step("top_sb", TS)
    idx_sb, idxf_sb, hot_sb = step("idx_sb", TS), step("idxf_sb"), step("hot_sb")
    hotT_ps, hotT_sb, hotT16_sb = step("hotT_ps"), step("hotT_sb"), step("hotT16_sb")
    hid_ps, hid_sb, mask_ps, kept_sb = step("hid_ps", NC), step("hid_sb", NC), step("mask_ps", NC), step("kept_sb", NC)
    out_ps, res_sb = step("out_ps"), step("res_sb")
    stored = [ctx.enter_context(nc.semaphore(f"out_stored{b}")) for b in range(2)]
    before = m.stat_last

    def sp(eng):
        dst = m.out.rearrange("s t c -> t s c")
        with eng.Fori(0, TG // 2) as i:
            for b in range(2):
                g = 2 * i + b
                eng.wait_ge(res_sb.sem, res_sb.at(g))
                eng.dma_start(dst[:, bass.ds(g * TS, TS), :], res[b][:, :, :]).then_inc(stored[b], 16)
        for b in range(2):
            eng.wait_ge(stored[b], 16 * (TG // 2) + 16)

    def pool(eng):
        eng.wait_ge(*T.norm)
        skewed(eng, TG, lambda g, b, a: a(0), lambda g, b, k: T.pool(eng, g, b, hid_ps))

    def pe(eng):
        def ahead(g, b, k):
            T.pe(eng, g, b)

        def rest(g, b, ahead):
            eng.wait_ge(T.lo_sb.sem, T.lo_sb.at(g))
            eng.wait_ge(hotT_sb.sem, hotT_sb.at(g - 1))
            eng.wait_ge(hotT16_sb.sem, hotT16_sb.at(g - 1))
            for s in range(TS):
                sl, to = slice(s * P, (s + 1) * P), slice(s * E, (s + 1) * E)
                eng.matmul(m.ps[:, 1, to], T.xs[b][:, sl], rout.hi[:, :], start=True, stop=False)
                mm = eng.matmul(m.ps[:, 1, to], T.xs[b][:, sl], rout.lo[:, :], start=False, stop=True)
            mm.then_inc(logit_ps.sem, 1)

            def hidden(c):
                sl = slice(c * P, (c + 1) * P)
                eng.wait_ge(hid_sb.sem, hid_sb.at(g, c - 1) if c >= 2 else hid_sb.at(g - 1))
                eng.matmul(m.ps[:, 2 + c % 2, :], w1.hi[:, sl], T.xs[b][:, :], start=True, stop=False)
                eng.matmul(m.ps[:, 2 + c % 2, :], w1.lo[:, sl], T.xs[b][:, :], start=False,
                           stop=True).then_inc(hid_ps.sem, 1)

            def mask(c):
                eng.wait_ge(kept_sb.sem, kept_sb.at(g, c - 1) if c >= 2 else kept_sb.at(g - 1))
                eng.matmul(m.ps[:, 4 + c % 2, :], sel[:, c * P:(c + 1) * P], hotT16[:, :], start=True,
                           stop=True).then_inc(mask_ps.sem, 1)

            hidden(0)
            hidden(1)
            ahead(0)
            eng.wait_ge(hot_sb.sem, hot_sb.at(g))
            for s in range(TS):
                mm = eng.transpose(m.ps[0:E, 1, s * P:(s + 1) * P], hot[:, s, :], col(m, "ident"))
            mm.then_inc(hotT_ps.sem, 1)
            hidden(2)
            hidden(3)
            eng.wait_ge(hotT16_sb.sem, hotT16_sb.at(g))
            for c in range(NC):
                mask(c)
            eng.wait_ge(hotT_sb.sem, hotT_sb.at(g))
            eng.wait_ge(kept_sb.sem, kept_sb.at(g))
            eng.wait_ge(res_sb.sem, res_sb.at(g - 1))
            a, b2 = AT["fw2"][0], AT["fb2"][0]
            for s in range(TS):
                sl = slice(s * P, (s + 1) * P)
                for c in range(NC):
                    eng.matmul(m.ps[:, 6, sl], kept[c][:, sl], m.cst[:, a + c * C:a + c * C + P],
                               start=(c == 0), stop=False)
                mm = eng.matmul(m.ps[:, 6, sl], hotT[:, sl], m.cst[0:E, b2:b2 + P], start=False, stop=True)
            mm.then_inc(out_ps.sem, 1)

        eng.wait_ge(*before)
        eng.wait_ge(rout.sem, 3)
        eng.wait_ge(w1.sem, 3)
        eng.wait_ge(sel_sb, 1)
        skewed(eng, TG, rest, ahead)

    def dve(eng):
        def ahead(g, b, k):
            T.dve(eng, g, b)

        def rest(g, b, ahead):
            eng.wait_ge(logit_ps.sem, logit_ps.at(g))
            sh = [P, TS, E]
            eng.tensor_tensor(logit[:, :, :], m.ps[:, 1, 0:TS * E].rearrange("p (s e) -> p s e", s=TS),
                              col(m, "routbr").unsqueeze(1).broadcast_to(sh), ALU.add).then_inc(logit_sb.sem, 1)
            eng.wait_ge(logit_sb.sem, logit_sb.at(g))
            settle(eng, m)
            for s in range(TS):
                eng.max(top[:, s, :], logit[:, s, :]).then_inc(top_sb.sem, 1)
            eng.wait_ge(top_sb.sem, top_sb.at(g))
            settle(eng, m)
            for s in range(TS):
                eng.max_index(idx[:, s, :], top[:, s, :], logit[:, s, :]).then_inc(idx_sb.sem, 1)
            ahead(0)
            eng.wait_ge(idx_sb.sem, idx_sb.at(g))
            eng.tensor_copy(idxf[:, :], idx[:, :, 0]).then_inc(idxf_sb.sem, 1)
            eng.wait_ge(idxf_sb.sem, idxf_sb.at(g))
            eng.wait_ge(hotT_ps.sem, hotT_ps.at(g - 1))
            eng.tensor_tensor(hot[:, :, :], col(m, "iota32").unsqueeze(1).broadcast_to(sh), bc(idxf[:, :], sh),
                              ALU.is_equal).then_inc(hot_sb.sem, 1)
            eng.wait_ge(hotT_ps.sem, hotT_ps.at(g))
            eng.wait_ge(hotT_sb.sem, hotT_sb.at(g))
            eng.wait_ge(mask_ps.sem, mask_ps.at(g - 1))
            eng.tensor_copy(hotT16[:, :], m.ps[0:E, 1, :]).then_inc(hotT16_sb.sem, 1)
            for c in range(NC):
                eng.wait_ge(mask_ps.sem, mask_ps.at(g, c + 1))
                eng.wait_ge(hid_sb.sem, hid_sb.at(g, c + 1))
                if c == 0:
                    eng.wait_ge(out_ps.sem, out_ps.at(g - 1))
                eng.tensor_tensor(kept[c][:, :], m.ps[:, 4 + c % 2, :], hid[c][:, :], ALU.mult).then_inc(kept_sb.sem, 1)
            eng.wait_ge(out_ps.sem, out_ps.at(g))
            for k in range(2):
                if b == k:
                    eng.wait_ge(stored[b], store_value(g, b))
            eng.scalar_tensor_tensor(out=res[b][:, :, :], in0=m.ps[:, 6, :].rearrange("p (s c) -> p s c", s=TS)[:, :, 0:C],
                                     scalar=0.0, in1=m.h[:, bass.ds(g * TS, TS), :], op0=ALU.max,
                                     op1=ALU.add).then_inc(res_sb.sem, 1)

        eng.tensor_copy(sel[:, :], col(m, "sel32", slice(0, E))).then_inc(sel_sb, 1)
        rout.make(eng, col(m, "routw"))
        w1.make(eng, col(m, "fw1"))
        skewed(eng, TG, rest, ahead)

    def store_value(g, b):
        return (g - b) * 8 + 16

    def act(eng):
        def ahead(g, b, k):
            T.act(eng, g, b, hid_ps)

        def rest(g, b, ahead):
            for c in range(NC):
                eng.wait_ge(hid_ps.sem, hid_ps.at(g, c + 1))
                if c == 0:
                    eng.wait_ge(kept_sb.sem, kept_sb.at(g - 1))
                nc.scalar.activation(hid[c][:, :], m.ps[:, 2 + c % 2, :], ACT.Relu,
                                     bias=m.cst[:, AT["fb1"][0] + c:AT["fb1"][0] + c + 1]).then_inc(hid_sb.sem, 1)
                if c == 1:
                    ahead(0)
                    eng.wait_ge(hotT_ps.sem, hotT_ps.at(g))
                    eng.wait_ge(out_ps.sem, out_ps.at(g - 1))
                    nc.scalar.activation(hotT[:, :], m.ps[0:E, 1, :], ACT.Identity).then_inc(hotT_sb.sem, 1)

        skewed(eng, TG, rest, ahead)

    m.ahead_of_stores = stored
    return dict(sp=sp, pool=pool, pe=pe, dve=dve, act=act)


PHASES = [tokenizer, norm("n1", twice=True), attention0, norm("n2"), mlp0, norm("n3"), experts0, norm("n4"),
          spread0, norm("n5"), attention1, norm("n6"), experts1]


def audio_tower_kernel(nc, x, cst, ew1, ew2, out):
    with ExitStack() as ctx:
        m = Memory()
        m.x, m.ended, m.raised, m.ahead_of_stores = x, [], [], []
        m.cst = ctx.enter_context(nc.sbuf_tensor("cst", [P, NCOL], F32))
        m.h = ctx.enter_context(nc.sbuf_tensor("h", [P, S, C], F32))
        m.y = ctx.enter_context(nc.sbuf_tensor("y", [P, S, C], F32))
        m.stat = ctx.enter_context(nc.sbuf_tensor("stat", [P, S, 6], F32))
        m.eps = ctx.enter_context(nc.sbuf_tensor("eps", [P, 1], F32))
        m.ps = ctx.enter_context(nc.psum_tensor("ps", [P, 8, 512], F32))
        m.cst_sem = ctx.enter_context(nc.semaphore("constants_loaded"))
        m.cst2_sem = ctx.enter_context(nc.semaphore("layer_constants_loaded"))
        m.eps_sem = ctx.enter_context(nc.semaphore("eps_set"))
        m.waited = ctx.enter_context(nc.semaphore("waits_alone"))
        m.dve_pre = ctx.enter_context(nc.semaphore("dve_pre"))
        m.out, m.ew1, m.ew2 = out, ew1, ew2
        m.norm_tiles = [ctx.enter_context(nc.sbuf_tensor(f"norm_{n}", [P, S], F32)) for n in
                        ("diff", "m2", "dd", "var", "dev", "tmp", "mean", "rstd", "rstd2")]
        m.split = {n: Split(nc, ctx, n, AT[n][1]) for n in ("wkv2", "wq2", "wtok", "wm1", "gatew", "routw", "fw1")}
        m.ew1_hi = ctx.enter_context(nc.sbuf_tensor("ew1_hi", [P, EXPERTS0 * F0], F32R))
        m.ew1_lo = ctx.enter_context(nc.sbuf_tensor("ew1_lo", [P, EXPERTS0 * F0], F32R))
        m.ew1_f = ctx.enter_context(nc.sbuf_tensor("ew1_f", [P, EXPERTS0 * F0], F32))
        m.ew2_sb = ctx.enter_context(nc.sbuf_tensor("ew2_sb", [P, EXPERTS0 * C + C], F32))
        m.ew1_sem, m.ew2_sem, m.ew2_pad, m.ew_split = (ctx.enter_context(nc.semaphore(n)) for n in
                                            ("ew1_loaded", "ew2_loaded", "ew2_padded", "ew1_split"))
        phases = []
        for make in PHASES:
            with ExitStack() as m.mem:
                m.steps = []
                phases.append(make(nc, ctx, m))
            m.ended += m.steps
        block = ctx.enter_context(nc.Block())

        @block.sync
        def _(eng):
            eng.dma_start(m.cst[:, 0:TOK_END], cst[:, 0:TOK_END]).then_inc(m.cst_sem, 16)
            eng.dma_start(m.ew1_f[:, :], ew1).then_inc(m.ew1_sem, 16)
            eng.dma_start(m.ew2_sb[:, 0:EXPERTS0 * C], ew2).then_inc(m.ew2_sem, 16)
            for step in m.raised:
                eng.sem_inc(step.sem, step.start)
            for sem in m.ahead_of_stores:
                eng.sem_inc(sem, 16)
            for p in phases:
                if "sp" in p:
                    p["sp"](eng)

        @block.gpsimd
        def _(eng):
            eng.memset(m.ew2_sb[:, EXPERTS0 * C:], 0.0).then_inc(m.ew2_pad, 1)
            eng.memset(m.eps[:, :], EPS).then_inc(m.eps_sem, 1)
            for p in phases:
                if "pool" in p:
                    p["pool"](eng)

        @block.tensor
        def _(eng):
            eng.wait_ge(m.cst_sem, 16)
            for p in phases:
                if "pe" in p:
                    p["pe"](eng)

        @block.vector
        def _(eng):
            eng.wait_ge(m.cst_sem, 16)
            for p in phases:
                if "dve" in p:
                    p["dve"](eng)

        @block.scalar
        def _(eng):
            eng.dma_start(m.cst[:, TOK_END:NCOL], cst[:, TOK_END:NCOL]).then_inc(m.cst2_sem, 16)
            eng.wait_ge(m.cst_sem, 16)
            eng.wait_ge(m.eps_sem, 1)
            for p in phases:
                if "act" in p:
                    p["act"](eng)


def constants(i):
    import numpy as np

    c = np.zeros((P, NCOL), np.float32)

    def put(name, a, row=0):
        at, w = AT[name]
        a = np.asarray(a)
        a = a.reshape(a.shape[0], -1)
        c[row:row + a.shape[0], at:at + a.shape[1]] = a

    def rows(name, v):
        put(name, np.broadcast_to(np.asarray(v).reshape(1, -1), (P, np.asarray(v).size)))

    def tok(n):
        return np.asarray(i["L0_tok_" + n])

    put("ident", np.eye(P, dtype=np.float32))
    rows("g1r", np.tile(tok("g1"), 8)), rows("v1r", np.tile(tok("v1"), 8))
    rows("g2r", np.tile(tok("g2"), 2)), rows("v2r", np.tile(tok("v2"), 2))
    for n, reps in ((1, 8), (2, 2), (3, 1)):
        for k in ("b", "m", "g", "be", "v"):
            put(f"{k}{n}", np.tile(tok(f"{k}{n}"), reps)[:, None])
    w1, w2, w3 = (tok(n) for n in ("w1", "w2", "w3"))
    a = np.zeros((3, 8, 2, 8, 16), np.float32)
    for s in range(8):
        a[:, s, :, s, :] = w1.transpose(2, 1, 0)
    put("w1", a.reshape(48, P))
    a = np.zeros((3, 2, 16, 2, 64), np.float32)
    for s in range(2):
        a[:, s, :, s, :] = w2.transpose(2, 1, 0)
    put("w2", a.reshape(96, P))
    put("gamma", np.broadcast_to(tok("gamma"), (P, 1)))
    for s in range(2):
        put(f"wq{s}", np.pad(tok("wq").T, ((0, 0), (64 * s, 56 - 64 * s + 64))), 64 * s)
        put(f"bq{s}", tok("bq")[:, None], 64 * s)
        put("bk", tok("bk")[:, None], 64 * s)
    a = np.zeros((2, 64, 2, 64), np.float32)
    b = np.zeros((2, 64, 2, 64), np.float32)
    for s in range(2):
        a[s, :, s, :8] = tok("wk").T
        b[s, :, s, :] = tok("wv").T
    put("wk", a.reshape(P, P)), put("wv", b.reshape(P, P))
    rows("bvr", np.tile(tok("bv"), 2))
    a = np.zeros((2, 64, 2, 4, P), np.float32)
    for s in range(2):
        a[s, :, s] = w3.transpose(1, 2, 0)
    put("w3", a.reshape(P, 8 * P))
    more_constants(i, put, rows)
    return c


def kernel(**inputs):
    import numpy as np
    import concourse.bacc as bacc
    from concourse.bass_utils import run_bass_kernel_spmd as run

    nc = bacc.Bacc("TRN2", target_bir_lowering=False, num_devices=1)
    x = np.asarray(inputs["x"]).reshape(S, 2, L)
    ew1, ew2 = expert_layout(inputs)
    arrays = {"x_dram": np.pad(x, ((0, 0), (0, 0), (1, 1))), "cst_dram": constants(inputs),
              "ew1_dram": ew1, "ew2_dram": ew2}
    args = [nc.dram_tensor(n, a.shape, F32, kind="ExternalInput").ap() for n, a in arrays.items()]
    args.append(nc.dram_tensor("out_dram", (S, P, C), F32, kind="ExternalOutput").ap())
    audio_tower_kernel(nc, *args)
    r = run(nc, [arrays], core_ids=[0])
    return r.results[0]["out_dram"]


def more_constants(i, put, rows):
    import numpy as np

    def twice(name, a):
        put(name, np.concatenate([a, a]))

    def a0(n):
        return np.asarray(i["L0_attn_" + n])

    def f0(n):
        return np.asarray(i["L0_ffn_" + n])

    def a1(n):
        return np.asarray(i["L1_attn_" + n])

    def f1(n):
        return np.asarray(i["L1_ffn_" + n])

    twice("n1g", a0("norm1_g")[:, None]), twice("n1b", a0("norm1_b")[:, None])
    twice("n2g", a0("norm2_g")[:, None]), twice("n2b", a0("norm2_b")[:, None])
    wq, wkv = a0("Wq").T, a0("Wkv").T
    twice("wkv2", wkv), twice("wq2", wq[:, :8]), twice("wtok", np.concatenate([wkv, wq], 1))
    put("wproj", np.concatenate([a0("Wproj").T, a0("bproj")[None]]))
    head = np.arange(C) // 8
    put("headmask", ((head[:, None] == head[None]) & (head[:, None] > 0)).astype(np.float32))
    twice("wm1", a0("W1").T)
    put("bm1", a0("b1").reshape(2, P).T)
    put("wm2", a0("W2").T.reshape(2, P, C).transpose(1, 0, 2))
    rows("bm2r", a0("b2"))
    twice("gatew", f0("gate_w")), rows("gatebr", f0("gate_b"))
    rows("iota16", np.arange(EXPERTS0, dtype=np.float32))
    put("eb1", f0("b1").T), put("eb2", f0("b2"))
    rows("gamr", f0("gamma")), rows("betr", f0("beta"))

    def heads(w):
        w = w.reshape(C, HEADS, C).transpose(2, 1, 0)
        return np.stack([w, w], 2)

    put("wkT", heads(a1("WK"))), put("wvT", heads(a1("WV")))
    put("wqT", a1("WQ").reshape(C, HEADS, C).transpose(2, 1, 0))
    put("wout", a1("Wout").reshape(HEADS, C, C).transpose(1, 0, 2))
    rows("boutr", a1("bout"))
    twice("routw", f1("router_w").T), rows("routbr", f1("router_b"))
    rows("iota32", np.arange(EXPERTS1, dtype=np.float32))
    twice("fw1", f1("W1").transpose(1, 0, 2).reshape(C, HID1))
    put("fb1", f1("b1").reshape(4, P).T)
    put("fw2", f1("W2").reshape(4, P, C).transpose(1, 0, 2))
    put("fb2", f1("b2"))
    put("sel32", (np.arange(EXPERTS1)[:, None] == np.arange(HID1)[None] // F1).astype(np.float32))


def expert_layout(i):
    import numpy as np

    w1 = np.asarray(i["L0_ffn_w1"]).transpose(1, 0, 2).reshape(C, EXPERTS0 * F0)
    return np.concatenate([w1, w1]), np.asarray(i["L0_ffn_w2"]).transpose(1, 0, 2).reshape(F0, EXPERTS0 * C)
```

```python
from contextlib import ExitStack

import concourse.bass as bass
from concourse import mybir

F32 = mybir.dt.float32
F32R = mybir.dt.float32r
BF16 = mybir.dt.bfloat16
U32 = mybir.dt.uint32
ACT = mybir.ActivationFunctionType
ALU = mybir.AluOpType
AX = mybir.AxisListType.X

P = 128
S = 64
C = 64
L = 4096
EPS = 1e-5
GS = 8
NG = S // GS
POOL1, POOL2 = 8, 4
L1 = L // POOL1
TS = 4
TG = S // TS
NT = TS * P
HEADS = 8
EXPERTS0, F0 = 16, 128
EXPERTS1, F1 = 32, 16
HID1 = EXPERTS1 * F1
MLP = 256

COLS = [("ident", P)]
COLS += [("g1r", P), ("v1r", P), ("w1", P), ("g2r", P), ("v2r", P), ("w2", P)]
COLS += [(n + str(i), 1) for i in (1, 2, 3) for n in ("b", "m", "g", "be", "v")]
COLS += [("gamma", 1), ("wq0", P), ("wq1", P), ("wk", P), ("bq0", 1), ("bq1", 1), ("bk", 1),
         ("wv", P), ("bvr", P), ("w3", 8 * P)]
TOK_END = sum(w for _, w in COLS)
COLS += [("n1g", 1), ("n1b", 1), ("wkv2", P), ("wq2", P), ("wtok", P), ("wproj", C), ("headmask", C),
         ("n2g", 1), ("n2b", 1), ("wm1", MLP), ("bm1", 2), ("wm2", 2 * C), ("bm2r", C)]
COLS += [("gatew", EXPERTS0), ("gatebr", EXPERTS0), ("iota16", EXPERTS0), ("eb1", EXPERTS0),
         ("eb2", C), ("gamr", C), ("betr", C)]
COLS += [("wqT", HEADS * C), ("wkT", HEADS * P), ("wvT", HEADS * P), ("wout", HEADS * C), ("boutr", C)]
COLS += [("routw", EXPERTS1), ("routbr", EXPERTS1), ("iota32", EXPERTS1), ("fw1", HID1), ("fb1", 4),
         ("fw2", 4 * C), ("fb2", C), ("sel32", HID1)]
NCOL = sum(w for _, w in COLS)
AT = {}
for _n, _w in COLS:
    AT[_n] = (sum(w for _, w in COLS[:[n for n, _ in COLS].index(_n)]), _w)


class Step:

    def __init__(self, nc, ctx, m, name, per=1):
        self.per = per
        fit = [f for f in m.ended if f.end >= 2 * per]
        if fit:
            m.ended.remove(fit[0])
            self.sem, self.start = fit[0].sem, fit[0].end
        else:
            self.sem, self.start = ctx.enter_context(nc.semaphore(name)), 2 * per
            m.raised.append(self)
        self.end = self.start + per * m.rounds
        m.steps.append(self)

    def at(self, r, k=None):
        return r * self.per + (self.start + (self.per if k is None else k))


def col(m, name, rows=slice(0, P)):
    a, w = AT[name]
    return m.cst[rows, a:a + w]


def settle(eng, m):
    eng.sem_inc(m.waited, 1)


class Memory:
    pass


def tokenizer(nc, ctx, m):
    def sb(name, shape, dt=F32):
        return m.mem.enter_context(nc.sbuf_tensor(name, shape, dt))

    def step(name, per=1):
        return Step(nc, ctx, m, name, per)

    m.rounds = NG
    NP = GS // 2
    PAIRS = (1, 2, 3, 0)
    TAPS = ((1, 0, L1 - 1), (0, 0, L1), (0, 1, L1 - 1))
    K2 = 96
    x_in = [sb(f"x_in{b}", [K2, L]) for b in range(2)]
    c1_max = [sb(f"c1_max{b}", [P, L1]) for b in range(2)]
    c2_in = [sb(f"c2_in{b}", [K2, NP, L1]) for b in range(2)]
    c2_max = sb("c2_max", [P, NP * P])
    x2 = sb("x2", [P, NP * P])
    x3 = sb("x3", [P, NP, P + 2])
    qk = sb("qk", [P, 3, NP * P])
    v_tok = sb("v_tok", [P, NP, P])
    ex = sb("t_ex", [P, GS, P])
    prob = sb("t_prob", [P, GS, P])
    probT = sb("t_probT", [P, GS, P])
    row_max = sb("t_rmax", [P, GS])
    neg_max = sb("t_nmax", [P, GS])
    row_sum = sb("t_rsum", [P, GS])
    rec = sb("t_rec", [P, GS])
    row_scale = sb("t_rscale", [P, GS])
    w1s, w2s = sb("w1s", [P, P]), sb("w2s", [P, P])
    r1, r2 = sb("r1", [P, P]), sb("r2", [P, P])
    rr = sb("rr", [P, 3])
    sc = sb("sc", [P, 3])
    bi = sb("bi", [P, 3])

    x_sem = [ctx.enter_context(nc.semaphore(f"x_loaded{b}")) for b in range(2)]
    x_pad = [ctx.enter_context(nc.semaphore(f"x_padded{b}")) for b in range(2)]
    c2_pad = ctx.enter_context(nc.semaphore("c2_padded"))
    std = ctx.enter_context(nc.semaphore("norm_std"))
    prep = ctx.enter_context(nc.semaphore("norm_folded"))
    conv1_ps = step("conv1_ps", 4)
    conv1_max = step("conv1_max", 4)
    pooled1 = step("pooled1", 3 * (NP - 1))
    pooled1_last = step("pooled1_last", 3)
    conv2_ps = step("conv2_ps", NP)
    conv2_max = step("conv2_max", NP)
    pooled2 = step("pooled2")
    qkv_ps = step("qkv_ps", 4)
    qk_sb = step("qk_sb", 2)
    k_sb = step("t_k_sb")
    v_sb = step("v_sb")
    energy_ps = step("energy_ps")
    negmax = step("negmax", 2)
    exp_sb = step("exp_sb", GS)
    scale_sb = step("scale_sb", 2)
    prob_sb = step("prob_sb")
    half_sb = step("half_sb")
    probT_ps = step("probT_ps")
    probT_sb = step("probT_sb")
    attn_ps = step("attn_ps")
    x3_sb = step("x3_sb")
    conv3_ps = step("conv3_ps")
    h_sb = step("h0_sb")
    h_stat = step("h0_stat", GS)
    m.stat_last = (h_stat.sem, h_stat.at(NG - 1))
    m.h_last, m.h_rounds = h_sb, NG - 1

    def sp(eng):
        def load(g, b, j):
            if j is not None:
                eng.wait_ge(conv1_ps.sem, conv1_ps.at(g - 2))
            for k in range(3):
                if k == 2 and j is None:
                    eng.wait_ge(x_pad[b], 2)
                rows = m.x[bass.ds(g * GS, GS), :, k:k + L].rearrange("s c l -> (s c) l")
                eng.dma_start(x_in[b][16 * k:16 * k + 16, :], rows).then_inc(x_sem[b], 16)
        load(0, 0, None)
        load(1, 1, None)
        m.load_layers(eng)
        with eng.Fori(1, NG // 2) as i:
            load(2 * i, 0, i)
            load(2 * i + 1, 1, i)

    def pool(eng):
        eng.wait_ge(m.eps_sem, 1)
        for b in range(2):
            if b:
                eng.wait_ge(x_pad[0], 2)
            eng.memset(x_in[b][32:64, :], 0.0).then_inc(x_pad[b], 1)
        eng.wait_ge(x_pad[1], 2)
        for b in range(2):
            if b:
                eng.wait_ge(c2_pad, 2)
            eng.memset(c2_in[b][0:32, :, 0:1], 0.0).then_inc(c2_pad, 1)
            eng.wait_ge(c2_pad, 2 * b + 1)
            eng.memset(c2_in[b][64:96, :, L1 - 1:L1], 0.0).then_inc(c2_pad, 1)
        eng.wait_ge(c2_pad, 4)
        eng.memset(x3[:, :, 0:1], 0.0).then_inc(c2_pad, 1)
        eng.memset(x3[:, :, P + 1:P + 2], 0.0).then_inc(c2_pad, 1)
        eng.wait_ge(c2_pad, 6)

        def relu1(g, b):
            p, q = NP - 1, 32 * (NP - 1)
            eng.wait_ge(conv1_max.sem, conv1_max.at(g))
            eng.wait_ge(conv2_ps.sem, conv2_ps.at(g - 2))
            eng.wait_ge(half_sb.sem, half_sb.at(g - 2))
            for k, (to, of, n) in enumerate(TAPS):
                settle(eng, m)
                eng.tensor_scalar(c2_in[b][32 * k:32 * k + 32, p, to:to + n], c1_max[b][q:q + 32, of:of + n],
                                  bi[q:q + 32, 0:1], 0.0, ALU.add, ALU.max).then_inc(pooled1_last.sem, 1)
                eng.wait_ge(pooled1_last.sem, pooled1_last.at(g, k + 1))

        def rest(g, b, left, back):
            if left is None:
                return
            half = slice(GS // 2, GS)
            if left:
                relu1(g + 1, 1 - b)
            eng.wait_ge(scale_sb.sem, scale_sb.at(g))
            eng.wait_ge(probT_ps.sem, probT_ps.at(g - 1))
            eng.tensor_tensor(prob[:, half, :], ex[:, half, :], row_scale[:, half].unsqueeze(2).broadcast_to([P, GS // 2, P]),
                              ALU.mult).then_inc(half_sb.sem, 1)

        eng.wait_ge(prep, 6)
        lagged(eng, NG, relu1, rest)

    def pe(eng):
        def conv1(g, b, h):
            if h == 0:
                eng.wait_ge(x_sem[b], (g - b) * 24 + 48)
            if h < 2:
                eng.wait_ge(conv1_max.sem, conv1_max.at(g - 1, h + 3))
            else:
                eng.wait_ge(conv1_max.sem, conv1_max.at(g, h - 1))
            for t in range(2):
                mm = eng.matmul(m.ps[:, 2 * (h % 2) + t, :], w1s[0:K2, :],
                                x_in[b][:, (2 * h + t) * 512:(2 * h + t + 1) * 512],
                                start=True, stop=True)
            mm.then_inc(conv1_ps.sem, 1)

        def conv3(g):
            eng.wait_ge(x3_sb.sem, x3_sb.at(g))
            eng.wait_ge(h_sb.sem, h_sb.at(g - 1))
            for s in range(2):
                for k in range(4):
                    a = AT["w3"][0] + (4 * s + k) * P
                    mm = eng.matmul(m.ps[:, 5, s * 256:(s + 1) * 256], m.cst[:, a:a + P],
                                    x3[:, :, k:k + P - 1:2], start=(k == 0), stop=(k == 3))
            mm.then_inc(conv3_ps.sem, 1)

        def rest(g, b, left, back):
            if left is None:
                conv3(g - 1)
                return
            eng.wait_ge(h_sb.sem, h_sb.at(g - 2))
            for p in PAIRS:
                if p == 0:
                    eng.wait_ge(x3_sb.sem, x3_sb.at(g - 1))
                if p < NP - 1:
                    eng.wait_ge(pooled1.sem, pooled1.at(g, 3 * p + 3))
                else:
                    eng.wait_ge(pooled1_last.sem, pooled1_last.at(g))
                eng.matmul(m.ps[:, 4 + p, :], w2s[0:K2, :], c2_in[b][:, p, :],
                           start=True, stop=True).then_inc(conv2_ps.sem, 1)
            if left > 1:
                conv1(g + 2, b, 0)
            eng.wait_ge(pooled2.sem, pooled2.at(g))
            for n, w in ((2, "wk"), (0, "wq0"), (1, "wq1")):
                eng.matmul(m.ps[:, 4 + n, :], col(m, w), x2[:, :], start=True, stop=True).then_inc(qkv_ps.sem, 1)
            for p in range(NP):
                mm = eng.matmul(m.ps[:, 7, p * P:(p + 1) * P], x2[:, p * P:(p + 1) * P],
                                col(m, "wv"), start=True, stop=True)
            mm.then_inc(qkv_ps.sem, 1)
            eng.wait_ge(qk_sb.sem, qk_sb.at(g))
            eng.wait_ge(k_sb.sem, k_sb.at(g))
            for s in range(GS):
                p = s // 2
                mm = eng.matmul(m.ps[:, 4 + s // 4, (s % 4) * P:(s % 4 + 1) * P],
                                qk[:, s % 2, p * P:(p + 1) * P], qk[:, 2, p * P:(p + 1) * P],
                                start=True, stop=True)
            mm.then_inc(energy_ps.sem, 1)
            if left > 1:
                for h in range(1, 4):
                    conv1(g + 2, b, h)
            eng.wait_ge(v_sb.sem, v_sb.at(g))
            for half, ready in enumerate((prob_sb, half_sb)):
                eng.wait_ge(ready.sem, ready.at(g))
                for s in range(4 * half, 4 * half + 4):
                    mm = eng.transpose(m.ps[:, 6 + half, (s % 4) * P:(s % 4 + 1) * P], prob[:, s, :],
                                       col(m, "ident"))
            mm.then_inc(probT_ps.sem, 1)
            if back:
                conv3(g - 1)
            eng.wait_ge(probT_sb.sem, probT_sb.at(g))
            for s in range(GS):
                r = 64 * (s % 2)
                mm = eng.matmul(m.ps[r:r + 64, 4, (s // 2) * P:(s // 2 + 1) * P],
                                v_tok[:, s // 2, r:r + 64], probT[:, s, :], start=True, stop=True)
            mm.then_inc(attn_ps.sem, 1)

        eng.wait_ge(m.cst_sem, 16)
        eng.wait_ge(prep, 6)
        for pad in x_pad:
            eng.wait_ge(pad, 2)
        eng.wait_ge(c2_pad, 6)
        lagged(eng, NG, lambda g, b: [conv1(g, b, h) for h in range(4)], rest, early=1)

    def dve(eng):
        for b in range(2):
            eng.memset(x_in[b][64:K2, :], 0.0).then_inc(x_pad[b], 1)
        eng.wait_ge(m.cst_sem, 16)
        eng.wait_ge(std, 3)
        eng.reciprocal(r1[:, :], r1[:, :]).then_inc(m.dve_pre, 1)
        eng.reciprocal(r2[:, :], r2[:, :]).then_inc(m.dve_pre, 1)
        eng.reciprocal(rr[:, :], rr[:, :]).then_inc(m.dve_pre, 1)
        eng.wait_ge(m.dve_pre, 3)
        eng.tensor_tensor(r1[:, :], r1[:, :], col(m, "g1r"), ALU.mult).then_inc(m.dve_pre, 1)
        eng.tensor_tensor(r2[:, :], r2[:, :], col(m, "g2r"), ALU.mult).then_inc(m.dve_pre, 1)
        for n in range(3):
            eng.tensor_tensor(sc[:, n:n + 1], rr[:, n:n + 1], col(m, f"g{n + 1}"), ALU.mult).then_inc(m.dve_pre, 1)
            eng.tensor_tensor(bi[:, n:n + 1], col(m, f"b{n + 1}"), col(m, f"m{n + 1}"), ALU.subtract).then_inc(m.dve_pre, 1)
        eng.wait_ge(m.dve_pre, 11)
        eng.tensor_tensor(w1s[:, :], r1[:, :], col(m, "w1"), ALU.mult).then_inc(prep, 1)
        eng.tensor_tensor(w2s[:, :], r2[:, :], col(m, "w2"), ALU.mult).then_inc(prep, 1)
        eng.tensor_tensor(bi[:, :], bi[:, :], sc[:, :], ALU.mult).then_inc(prep, 1)
        eng.wait_ge(prep, 3)
        for n in range(3):
            eng.tensor_tensor(bi[:, n:n + 1], bi[:, n:n + 1], col(m, f"be{n + 1}"), ALU.add).then_inc(prep, 1)

        def reduce1(g, b, h):
            eng.wait_ge(conv1_ps.sem, conv1_ps.at(g, h + 1))
            if h == 0:
                eng.wait_ge(pooled1.sem, pooled1.at(g - 2))
                eng.wait_ge(pooled1_last.sem, pooled1_last.at(g - 2))
            src = m.ps[:, 2 * (h % 2):2 * (h % 2) + 2, :].rearrange("p a (l k) -> p (a l) k", k=POOL1)
            eng.tensor_reduce(c1_max[b][:, h * P:(h + 1) * P], src, AX, ALU.max).then_inc(conv1_max.sem, 1)

        def count(g, half):
            eng.wait_ge(h_sb.sem, h_sb.at(g))
            stats(eng, m, m.h, g, GS, h_stat.sem, (GS // 2 * half, GS // 2 * (half + 1)))

        def rest(g, b, left, back):
            if left is None:
                count(g - 2, 1)
                count(g - 1, 0)
                count(g - 1, 1)
                return
            for n, p in enumerate(PAIRS):
                eng.wait_ge(conv2_ps.sem, conv2_ps.at(g, n + 1))
                if n == 0:
                    eng.wait_ge(pooled2.sem, pooled2.at(g - 1))
                src = m.ps[:, 4 + p, :].rearrange("p (l k) -> p l k", k=POOL2)
                eng.tensor_reduce(c2_max[:, p * P:(p + 1) * P], src, AX, ALU.max).then_inc(conv2_max.sem, 1)
            if left > 1:
                reduce1(g + 2, b, 0)
            if not isinstance(g, int) or g >= 2:
                count(g - 2, 1)
            eng.wait_ge(qkv_ps.sem, qkv_ps.at(g, 1))
            eng.wait_ge(energy_ps.sem, energy_ps.at(g - 1))
            eng.tensor_scalar(qk[:, 2, :], m.ps[:, 6, :], col(m, "bk"), None, ALU.add).then_inc(k_sb.sem, 1)
            eng.wait_ge(qkv_ps.sem, qkv_ps.at(g))
            eng.tensor_tensor(v_tok[:, :, :], m.ps[:, 7, :].rearrange("p (n c) -> p n c", n=NP),
                              col(m, "bvr").unsqueeze(1).broadcast_to([P, NP, P]),
                              ALU.add).then_inc(v_sb.sem, 1)
            eng.wait_ge(energy_ps.sem, energy_ps.at(g))
            eng.tensor_reduce(row_max[:, :], m.ps[:, 4:6, :].rearrange("p a (s j) -> p (a s) j", j=P), AX,
                              ALU.max).then_inc(negmax.sem, 1)
            eng.wait_ge(negmax.sem, negmax.at(g, 1))
            eng.wait_ge(exp_sb.sem, exp_sb.at(g - 1))
            eng.tensor_scalar(neg_max[:, :], row_max[:, :], -1.0, None, ALU.mult).then_inc(negmax.sem, 1)
            if left > 1:
                reduce1(g + 2, b, 1)
                reduce1(g + 2, b, 2)
            eng.wait_ge(exp_sb.sem, exp_sb.at(g))
            eng.reciprocal(rec[:, :], row_sum[:, :]).then_inc(scale_sb.sem, 1)
            eng.wait_ge(scale_sb.sem, scale_sb.at(g, 1))
            eng.wait_ge(half_sb.sem, half_sb.at(g - 1))
            eng.tensor_scalar(row_scale[:, :], rec[:, :], col(m, "gamma"), None, ALU.mult).then_inc(scale_sb.sem, 1)
            eng.wait_ge(scale_sb.sem, scale_sb.at(g))
            eng.wait_ge(probT_ps.sem, probT_ps.at(g - 1))
            eng.tensor_tensor(prob[:, 0:GS // 2, :], ex[:, 0:GS // 2, :],
                              row_scale[:, 0:GS // 2].unsqueeze(2).broadcast_to([P, GS // 2, P]),
                              ALU.mult).then_inc(prob_sb.sem, 1)
            if left > 1:
                reduce1(g + 2, b, 3)
            eng.wait_ge(attn_ps.sem, attn_ps.at(g))
            eng.wait_ge(conv3_ps.sem, conv3_ps.at(g - 1))
            eng.tensor_tensor(x3[:, :, 1:P + 1], m.ps[:, 4, :].rearrange("p (n l) -> p n l", n=NP),
                              x2[:, :].rearrange("p (n l) -> p n l", n=NP), ALU.add).then_inc(x3_sb.sem, 1)
            if back:
                count(g - 1, 0)

        eng.wait_ge(c2_pad, 6)
        lagged(eng, NG, lambda g, b: [reduce1(g, b, h) for h in range(4)], rest, early=1)

    def act(eng):
        nc.scalar.activation(r1[:, :], col(m, "v1r"), ACT.Sqrt, bias=m.eps[:, :]).then_inc(std, 1)
        nc.scalar.activation(r2[:, :], col(m, "v2r"), ACT.Sqrt, bias=m.eps[:, :]).then_inc(std, 1)
        a = AT["v1"][0]
        d = AT["v2"][0] - a
        nc.scalar.activation(rr[:, :], m.cst[:, a:a + 2 * d + 1:d], ACT.Sqrt, bias=m.eps[:, :]).then_inc(std, 1)
        eng.preload_act_table(ACT.Exp)

        def relu1(g, b, p):
            if p == 0:
                eng.wait_ge(conv1_max.sem, conv1_max.at(g))
                eng.wait_ge(conv2_ps.sem, conv2_ps.at(g - 2))
            q = 32 * p
            for k, (to, of, n) in enumerate(TAPS):
                nc.scalar.activation(c2_in[b][32 * k:32 * k + 32, p, to:to + n],
                                     c1_max[b][q:q + 32, of:of + n], ACT.Relu,
                                     bias=bi[q:q + 32, 0:1]).then_inc(pooled1.sem, 1)

        def rest(g, b, left, back):
            def more(p):
                if left:
                    relu1(g + 1, 1 - b, p)

            def last(g):
                eng.wait_ge(conv3_ps.sem, conv3_ps.at(g))
                nc.scalar.activation(m.h[:, bass.ds(g * GS, GS), :].rearrange("q (p s) l -> q s p l", s=2),
                                     m.ps[:, 5, :].rearrange("q (s p l) -> q s p l", s=2, p=NP), ACT.Identity,
                                     bias=bi[:, 2:3], scale=sc[:, 2:3]).then_inc(h_sb.sem, 1)

            if left is None:
                last(g - 1)
                return
            eng.wait_ge(conv2_max.sem, conv2_max.at(g))
            eng.wait_ge(x3_sb.sem, x3_sb.at(g - 1))
            nc.scalar.activation(x2[:, :], c2_max[:, :], ACT.Relu, bias=bi[:, 1:2]).then_inc(pooled2.sem, 1)
            more(0)
            for n, w in enumerate(("bq0", "bq1")):
                eng.wait_ge(qkv_ps.sem, qkv_ps.at(g, n + 2))
                nc.scalar.activation(qk[:, n, :], m.ps[:, 4 + n, :], ACT.Identity, bias=col(m, w)).then_inc(qk_sb.sem, 1)
            eng.wait_ge(negmax.sem, negmax.at(g))
            eng.wait_ge(prob_sb.sem, prob_sb.at(g - 1))
            eng.wait_ge(half_sb.sem, half_sb.at(g - 1))
            for s in range(GS):
                nc.scalar.activation(ex[:, s, :], m.ps[:, 4 + s // 4, (s % 4) * P:(s % 4 + 1) * P], ACT.Exp,
                                     bias=neg_max[:, s:s + 1], accum_out=row_sum[:, s:s + 1]).then_inc(exp_sb.sem, 1)
            more(1)
            eng.wait_ge(probT_ps.sem, probT_ps.at(g))
            nc.scalar.activation(probT[:, :, :], m.ps[:, 6:8, :].rearrange("p a (s j) -> p (a s) j", j=P),
                                 ACT.Identity).then_inc(probT_sb.sem, 1)
            more(2)
            if back:
                last(g - 1)

        eng.wait_ge(prep, 6)
        eng.wait_ge(c2_pad, 6)
        lagged(eng, NG, lambda g, b: [relu1(g, b, p) for p in range(NP - 1)], rest)

    return dict(sp=sp, pool=pool, pe=pe, dve=dve, act=act)


def stats(eng, m, h, g, n, done, some=None):
    for s in range(*(some or (n,))):
        eng.bn_stats(m.stat[:, bass.ds(g * n + s, 1), :], h[:, bass.ds(g * n + s, 1), :]).then_inc(done, 1)


def norm(name, twice=False, after=None):
    def make(nc, ctx, m):
        diff, m2, dd, var, dev, tmp, mean, rstd, rstd2 = m.norm_tiles
        own = ctx.enter_context(nc.semaphore(f"{name}_parts"))
        var_sb = ctx.enter_context(nc.semaphore(f"{name}_var"))
        std_sb = ctx.enter_context(nc.semaphore(f"{name}_std"))
        ready = ctx.enter_context(nc.semaphore(f"{name}_ready"))
        m.norm_ready = ready
        m.norm_value = 3 if twice else 2
        stat_sem, stat_value = m.stat_last

        def dve(eng):
            eng.wait_ge(stat_sem, stat_value)
            st = m.stat
            eng.tensor_tensor(diff[:, :], st[:, :, 1], st[:, :, 4], ALU.subtract).then_inc(own, 1)
            eng.tensor_tensor(tmp[:, :], st[:, :, 1], st[:, :, 4], ALU.add).then_inc(own, 1)
            eng.tensor_tensor(m2[:, :], st[:, :, 2], st[:, :, 5], ALU.add).then_inc(own, 1)
            eng.wait_ge(own, 3)
            eng.scalar_tensor_tensor(out=dd[:, :], in0=diff[:, :], scalar=0.25, in1=diff[:, :],
                                     op0=ALU.mult, op1=ALU.mult).then_inc(own, 1)
            eng.tensor_scalar(mean[:, :], tmp[:, :], 0.5, None, ALU.mult).then_inc(ready, 1)
            eng.wait_ge(own, 4)
            eng.scalar_tensor_tensor(out=var[:, :], in0=m2[:, :], scalar=1.0 / C, in1=dd[:, :],
                                     op0=ALU.mult, op1=ALU.add).then_inc(var_sb, 1)
            eng.wait_ge(std_sb, 1)
            eng.reciprocal(rstd[:, :], dev[:, :]).then_inc(ready, 1)
            if twice:
                eng.wait_ge(ready, 2)
                eng.tensor_tensor(tmp[:, :], var[:, :], rstd[:, :], ALU.mult).then_inc(own, 1)
                eng.wait_ge(own, 5)
                eng.tensor_tensor(m2[:, :], tmp[:, :], rstd[:, :], ALU.mult).then_inc(var_sb, 1)
                eng.wait_ge(std_sb, 2)
                eng.reciprocal(rstd2[:, :], dd[:, :]).then_inc(ready, 1)

        def act(eng):
            eng.wait_ge(var_sb, 1)
            nc.scalar.activation(dev[:, :], var[:, :], ACT.Sqrt, bias=m.eps[:, :]).then_inc(std_sb, 1)
            if twice:
                eng.wait_ge(var_sb, 2)
                nc.scalar.activation(dd[:, :], m2[:, :], ACT.Sqrt, bias=m.eps[:, :]).then_inc(std_sb, 1)

        return dict(dve=dve, act=act)
    return make


def bc(ap, shape):
    return ap.unsqueeze(2).broadcast_to(shape)


class Split:

    def __init__(self, nc, ctx, name, n, mem=None):
        self.hi, self.lo, self.f = ((mem or ctx).enter_context(nc.sbuf_tensor(f"{name}_{k}", [P, n], dt))
                                    for k, dt in (("hi", F32R), ("lo", F32R), ("f", F32)))
        self.sem = ctx.enter_context(nc.semaphore(name + "_split"))

    def make(self, eng, src, scale=None):
        eng.tensor_scalar(self.f[:, :], src, 1.0 if scale is None else scale, None, ALU.mult).then_inc(self.sem, 1)
        eng.wait_ge(self.sem, 1)
        eng.tensor_copy(self.hi[:, :], self.f[:, :]).then_inc(self.sem, 1)
        eng.wait_ge(self.sem, 2)
        eng.tensor_tensor(self.lo[:, :], self.f[:, :], self.hi[:, :].bitcast(F32), ALU.subtract).then_inc(self.sem, 1)


def lagged(eng, n, ahead, rest, early=0):
    for g in range(1 + early):
        ahead(g, g % 2)
    rest(0, 0, 2, False)
    rest(1, 1, 2, True)
    with eng.Fori(1, n // 2 - 1) as i:
        rest(2 * i, 0, 2, True)
        rest(2 * i + 1, 1, 2, True)
    rest(n - 2, 0, 1, True)
    rest(n - 1, 1, 0, True)
    rest(n, 0, None, True)


class Turned:

    def __init__(self, nc, ctx, m, name, src, bank, keep=None):
        self.nc, self.m, self.src, self.bank, self.keep = nc, m, src, bank, keep
        sb = lambda n, s, dt=F32: m.mem.enter_context(nc.sbuf_tensor(f"{name}_{n}", s, dt))
        self.xc = [sb(f"xc{b}", [P, TS, C]) for b in range(2)]
        self.twin = [sb(f"twin{b}", [P, TS, 2 * C]) for b in range(2)]
        self.xn = [t[:, :, 0:C] for t in self.twin]
        self.xs = [sb(f"xs{b}", [P, NT], F32R) for b in range(2)]
        self.mean, self.rstd, self.rstd2 = m.norm_tiles[6:]
        self.norm = (m.norm_ready, m.norm_value)

        def step(n, per=1):
            return Step(nc, ctx, m, f"{name}_{n}", per)
        self.norm_sb = step("norm_sb", 2 if keep is None else 3)
        self.turn_ps = step("turn_ps")
        self.hi_sb = step("hi_sb")
        self.lo_sb = step("lo_sb")

    def pool(self, eng, g, b):
        m, sl, sh = self.m, bass.ds(g * TS, TS), [P, TS, C]
        eng.wait_ge(self.turn_ps.sem, self.turn_ps.at(g - 2))
        settle(eng, m)
        eng.tensor_tensor(self.xc[b][:, :, :], self.src[:, sl, :], bc(self.mean[:, sl], sh),
                          ALU.subtract).then_inc(self.norm_sb.sem, 1)
        eng.wait_ge(self.norm_sb.sem, self.norm_sb.at(g, 1))
        last, scale = self.xc[b][:, :, :], self.rstd
        if self.keep is not None:
            settle(eng, m)
            eng.tensor_tensor(self.keep[:, sl, :], self.xc[b][:, :, :], bc(self.rstd[:, sl], sh),
                              ALU.mult).then_inc(self.norm_sb.sem, 1)
            eng.wait_ge(self.norm_sb.sem, self.norm_sb.at(g, 2))
            settle(eng, m)
            last, scale = self.keep[:, sl, :], self.rstd2
        pair = [P, TS, 2, C]
        eng.tensor_tensor(self.twin[b][:, :, :].rearrange("p s (a c) -> p s a c", a=2),
                          last.unsqueeze(2).broadcast_to(pair),
                          scale[:, sl].unsqueeze(2).unsqueeze(3).broadcast_to(pair),
                          ALU.mult).then_inc(self.norm_sb.sem, 1)

    def pe(self, eng, g, b):
        m = self.m
        eng.wait_ge(self.norm_sb.sem, self.norm_sb.at(g))
        eng.wait_ge(self.lo_sb.sem, self.lo_sb.at(g - 1))
        for s in range(TS):
            mm = eng.transpose(m.ps[:, self.bank, s * P:(s + 1) * P], self.twin[b][:, s, :], col(m, "ident"))
        mm.then_inc(self.turn_ps.sem, 1)

    def act(self, eng, g, b, free):
        eng.wait_ge(self.turn_ps.sem, self.turn_ps.at(g))
        eng.wait_ge(free.sem, free.at(g - 2))
        self.nc.scalar.activation(self.xs[b][:, :], self.m.ps[:, self.bank, :],
                                  ACT.Identity).then_inc(self.hi_sb.sem, 1)

    def dve(self, eng, g, b):
        eng.wait_ge(self.hi_sb.sem, self.hi_sb.at(g))
        eng.tensor_tensor(self.xs[b][64:P, :], self.m.ps[64:P, self.bank, :],
                          self.xs[b][64:P, :].bitcast(F32), ALU.subtract).then_inc(self.lo_sb.sem, 1)


def attention0(nc, ctx, m):
    def sb(name, shape, dt=F32):
        return m.mem.enter_context(nc.sbuf_tensor("a0_" + name, shape, dt))

    def step(name, per=1):
        return Step(nc, ctx, m, "a0_" + name, per)

    m.rounds = TG
    HD = C // HEADS
    SCALE = float(HD) ** -0.5
    T = Turned(nc, ctx, m, "a0", m.h, 0, keep=m.y)
    w_kv, w_q, w_tok = (m.split[n] for n in ("wkv2", "wq2", "wtok"))
    kvT = [sb(f"kvT{b}", [P, NT]) for b in range(2)]
    q0T = [sb(f"q0T{b}", [P, NT]) for b in range(2)]
    tok = [sb(f"tok{b}", [P, TS, P]) for b in range(2)]
    bias_kv, bias_q, bias_tok = sb("bias_kv", [P, 1]), sb("bias_q", [P, 1]), sb("bias_tok", [P, P])
    lmax, lneg, lsum, lrec = (sb(n, [P, TS]) for n in ("lmax", "lneg", "lsum", "lrec"))
    kmax, kneg, ksum, krec = (sb(n, [C, TS]) for n in ("kmax", "kneg", "ksum", "krec"))
    qmax, qsum, qrec = (sb(n, [P, TS * HEADS]) for n in ("qmax", "qsum", "qrec"))
    qd, qe, qs = (sb(n, [P, TS, C]) for n in ("qd", "qe", "qs"))
    lex, lprob, lprobT = (sb(n, [P, TS, P]) for n in ("lex", "lprob", "lprobT"))
    ekT = sb("ekT", [C, NT])
    ek, qsT = sb("ek", [P, TS, C]), sb("qsT", [C, NT])
    mask, ctxm = sb("mask", [C, TS, C]), sb("ctxm", [C, TS, C])
    v0 = [sb(f"v0{b}", [P, TS, C]) for b in range(2)]
    aT = sb("aT", [C + 1, NT])

    pre = ctx.enter_context(nc.semaphore("a0_bias_ps"))
    pre_sb = ctx.enter_context(nc.semaphore("a0_bias_sb"))
    once = ctx.enter_context(nc.semaphore("a0_set_once"))
    proj_ps = step("proj_ps", 2)
    kv_sb, q0_sb, tok_sb = step("kv_sb"), step("q0_sb"), step("tok_sb")
    local_ps, local_neg, local_exp = step("local_ps"), step("local_neg", 2), step("local_exp", TS)
    local_rec, local_prob = step("local_rec"), step("local_prob")
    k_neg, k_exp, k_rec = step("k_neg", 2), step("k_exp", TS), step("k_rec")
    q_max, q_diff, q_exp, q_rec, q_soft = step("q_max"), step("q_diff"), step("q_exp"), step("q_rec", 2), step("q_soft")
    k_turn, k_sb = step("k_turn"), step("k_sb")
    q_turn, q_sb = step("q_turn"), step("q_sb")
    p_turn, p_sb = step("p_turn"), step("p_sb")
    v0_sb, mask_sb = step("v0_sb"), step("mask_sb")
    ctx_ps, ctx_sb = step("ctx_ps"), step("ctx_sb")
    attn_ps, attn_sb = step("attn_ps"), step("attn_sb")
    y_ps, x1_sb = step("y_ps"), step("x1_sb")
    x1_stat = step("x1_stat", TS)
    before = (m.h_last.sem, m.h_last.at(m.h_rounds))
    m.stat_last = (x1_stat.sem, x1_stat.at(TG - 1))

    def pool(eng):
        def ahead(g, b):
            T.pool(eng, g, b)

        def rest(g, b, left, back):
            if left is None:
                return
            eng.wait_ge(q_max.sem, q_max.at(g))
            eng.wait_ge(q_exp.sem, q_exp.at(g - 1))
            eng.tensor_tensor(qd[:, :, :].rearrange("p s (h d) -> p (s h) d", d=HD),
                              tok[b][:, :, C:P].rearrange("p s (h d) -> p s h d", d=HD),
                              qmax[:, :].rearrange("p (s h) -> p s h", s=TS).unsqueeze(3).broadcast_to([P, TS, HEADS, HD]),
                              ALU.subtract).then_inc(q_diff.sem, 1)
            eng.wait_ge(attn_ps.sem, attn_ps.at(g - 2))
            settle(eng, m)
            eng.tensor_copy(v0[b][:, :, 0:HD], tok[b][:, :, 0:HD]).then_inc(v0_sb.sem, 1)
            if left > 1:
                ahead(g + 2, b)
            eng.wait_ge(q_rec.sem, q_rec.at(g))
            eng.wait_ge(q_turn.sem, q_turn.at(g - 1))
            eng.tensor_tensor(qs[:, :, :].rearrange("p s (h d) -> p (s h) d", d=HD),
                              qe[:, :, :].rearrange("p s (h d) -> p (s h) d", d=HD),
                              qrec[:, :].unsqueeze(2).broadcast_to([P, TS * HEADS, HD]),
                              ALU.mult).then_inc(q_soft.sem, 1)
            eng.wait_ge(local_rec.sem, local_rec.at(g))
            eng.wait_ge(p_turn.sem, p_turn.at(g - 1))
            eng.tensor_tensor(lprob[:, :, :], lex[:, :, :], lrec[:, :].unsqueeze(2).broadcast_to([P, TS, P]),
                              ALU.mult).then_inc(local_prob.sem, 1)
            eng.wait_ge(k_rec.sem, k_rec.at(g))
            eng.wait_ge(ctx_sb.sem, ctx_sb.at(g - 1))
            eng.tensor_tensor(mask[:, :, :], col(m, "headmask", slice(0, C)).unsqueeze(1).broadcast_to([C, TS, C]),
                              krec[:, :].unsqueeze(2).broadcast_to([C, TS, C]), ALU.mult).then_inc(mask_sb.sem, 1)

        for b in range(2):
            eng.memset(v0[b][:, :, :], 0.0).then_inc(once, 1)
        eng.wait_ge(once, 2)
        eng.memset(aT[C:C + 1, :], 1.0).then_inc(once, 1)
        eng.wait_ge(once, 3)
        eng.wait_ge(*T.norm)
        lagged(eng, TG, ahead, rest, early=1)

    def pe(eng):
        def project(g, b):
            eng.wait_ge(T.lo_sb.sem, T.lo_sb.at(g))
            eng.wait_ge(kv_sb.sem, kv_sb.at(g - 1))
            eng.wait_ge(q0_sb.sem, q0_sb.at(g - 1))
            eng.wait_ge(tok_sb.sem, tok_sb.at(g - 1))
            for bank, w in ((1, w_kv), (2, w_q)):
                eng.matmul(m.ps[:, bank, :], w.hi[:, :], T.xs[b][:, :], start=True, stop=False)
                mm = eng.matmul(m.ps[:, bank, :], w.lo[:, :], T.xs[b][:, :], start=False, stop=True)
            mm.then_inc(proj_ps.sem, 1)
            for s in range(TS):
                sl = slice(s * P, (s + 1) * P)
                eng.matmul(m.ps[:, 3, sl], T.xs[b][:, sl], w_tok.hi[:, :], start=True, stop=False)
                mm = eng.matmul(m.ps[:, 3, sl], T.xs[b][:, sl], w_tok.lo[:, :], start=False, stop=True)
            mm.then_inc(proj_ps.sem, 1)

        def ahead(g, b):
            T.pe(eng, g, b)
            project(g, b)

        def local(g, b):
            eng.wait_ge(kv_sb.sem, kv_sb.at(g))
            eng.wait_ge(q0_sb.sem, q0_sb.at(g))
            eng.wait_ge(local_exp.sem, local_exp.at(g - 1))
            for s in range(TS):
                sl = slice(s * P, (s + 1) * P)
                mm = eng.matmul(m.ps[:, 4, sl], q0T[b][:, sl], kvT[b][:, sl], start=True, stop=True)
            mm.then_inc(local_ps.sem, 1)

        def turn(g, b):
            eng.wait_ge(k_exp.sem, k_exp.at(g))
            eng.wait_ge(ctx_sb.sem, ctx_sb.at(g - 1))
            settle(eng, m)
            for s in range(TS):
                mm = eng.transpose(m.ps[:, 5, s * C:(s + 1) * C], ekT[:, s * P:(s + 1) * P],
                                   m.cst[0:C, AT["ident"][0]:AT["ident"][0] + C])
            mm.then_inc(k_turn.sem, 1)
            eng.wait_ge(q_soft.sem, q_soft.at(g))
            eng.wait_ge(x1_sb.sem, x1_sb.at(g - 1))
            settle(eng, m)
            for s in range(TS):
                mm = eng.transpose(m.ps[0:C, 6, s * P:(s + 1) * P], qs[:, s, :], col(m, "ident"))
            mm.then_inc(q_turn.sem, 1)
            eng.wait_ge(local_prob.sem, local_prob.at(g))
            eng.wait_ge(attn_sb.sem, attn_sb.at(g - 1))
            for s in range(TS):
                mm = eng.transpose(m.ps[:, 7, s * P:(s + 1) * P], lprob[:, s, :], col(m, "ident"))
            mm.then_inc(p_turn.sem, 1)

        def context(g, b):
            eng.wait_ge(k_sb.sem, k_sb.at(g))
            for s in range(TS):
                mm = eng.matmul(m.ps[0:C, 5, 256 + s * C:256 + (s + 1) * C], ek[:, s, :], tok[b][:, s, 0:C],
                                start=True, stop=True)
            mm.then_inc(ctx_ps.sem, 1)

        def attend(g, b):
            eng.wait_ge(q_sb.sem, q_sb.at(g))
            eng.wait_ge(p_sb.sem, p_sb.at(g))
            eng.wait_ge(ctx_sb.sem, ctx_sb.at(g))
            eng.wait_ge(v0_sb.sem, v0_sb.at(g))
            settle(eng, m)
            for s in range(TS):
                sl = slice(s * P, (s + 1) * P)
                eng.matmul(m.ps[0:C, 7, sl], ctxm[:, s, :], qsT[:, sl], start=True, stop=False)
                mm = eng.matmul(m.ps[0:C, 7, sl], v0[b][:, s, :], lprobT[:, s, :], start=False, stop=True)
            mm.then_inc(attn_ps.sem, 1)

        def out(g, b):
            eng.wait_ge(attn_sb.sem, attn_sb.at(g))
            for s in range(TS):
                mm = eng.matmul(m.ps[:, 6, s * C:(s + 1) * C], aT[:, s * P:(s + 1) * P],
                                col(m, "wproj", slice(0, C + 1)), start=True, stop=True)
            mm.then_inc(y_ps.sem, 1)

        def rest(g, b, left, back):
            if left:
                T.pe(eng, g + 1, 1 - b)
            if back:
                turn(g - 1, 1 - b)
                context(g - 1, 1 - b)
            if left is not None:
                local(g, b)
            if back:
                attend(g - 1, 1 - b)
            if left:
                project(g + 1, 1 - b)
            if back:
                out(g - 1, 1 - b)

        eng.wait_ge(*before)
        eng.wait_ge(m.cst2_sem, 16)
        h = slice(0, C)
        eng.matmul(m.ps[:, 0, 0:1], col(m, "wkv2", h), col(m, "n1b", h), start=True, stop=True).then_inc(pre, 1)
        eng.matmul(m.ps[:, 1, 0:1], col(m, "wq2", h), col(m, "n1b", h), start=True, stop=True).then_inc(pre, 1)
        eng.matmul(m.ps[:, 2, 0:P], col(m, "n1b", h).broadcast_to([C, P]), col(m, "wtok", h),
                   start=True, stop=True).then_inc(pre, 1)
        eng.wait_ge(pre_sb, 3)
        for w in (w_kv, w_q, w_tok):
            eng.wait_ge(w.sem, 3)
        eng.wait_ge(once, 3)
        lagged(eng, TG, ahead, rest)

    def dve(eng):
        def tokens(g, b):
            eng.wait_ge(proj_ps.sem, proj_ps.at(g))
            eng.wait_ge(ctx_ps.sem, ctx_ps.at(g - 2))
            eng.wait_ge(v0_sb.sem, v0_sb.at(g - 2))
            eng.tensor_tensor(tok[b][:, :, :], m.ps[:, 3, :].rearrange("p (s n) -> p s n", s=TS),
                              bias_tok[:, :].unsqueeze(1).broadcast_to([P, TS, P]),
                              ALU.add).then_inc(tok_sb.sem, 1)

        def ahead(g, b):
            T.dve(eng, g, b)
            tokens(g, b)

        def key_maxima(g, b):
            eng.wait_ge(kv_sb.sem, kv_sb.at(g))
            eng.tensor_reduce(kmax[:, :], kvT[b][0:C, :].rearrange("p (s t) -> p s t", s=TS), AX,
                              ALU.max).then_inc(k_neg.sem, 1)
            eng.wait_ge(k_neg.sem, k_neg.at(g, 1))
            eng.wait_ge(k_exp.sem, k_exp.at(g - 1))
            eng.tensor_scalar(kneg[:, :], kmax[:, :], -1.0, None, ALU.mult).then_inc(k_neg.sem, 1)

        def maxima(g, b):
            eng.wait_ge(tok_sb.sem, tok_sb.at(g))
            eng.wait_ge(q_diff.sem, q_diff.at(g - 1))
            eng.tensor_reduce(qmax[:, :].rearrange("p (s h) -> p s h", s=TS),
                              tok[b][:, :, C:P].rearrange("p s (h d) -> p s h d", d=HD), AX,
                              ALU.max).then_inc(q_max.sem, 1)
            eng.wait_ge(local_ps.sem, local_ps.at(g))
            eng.tensor_reduce(lmax[:, :], m.ps[:, 4, :].rearrange("p (s t) -> p s t", s=TS), AX,
                              ALU.max).then_inc(local_neg.sem, 1)
            eng.wait_ge(local_neg.sem, local_neg.at(g, 1))
            eng.wait_ge(local_exp.sem, local_exp.at(g - 1))
            eng.tensor_scalar(lneg[:, :], lmax[:, :], -SCALE, None, ALU.mult).then_inc(local_neg.sem, 1)

        def sums(g, b):
            eng.wait_ge(k_exp.sem, k_exp.at(g))
            eng.wait_ge(mask_sb.sem, mask_sb.at(g - 1))
            eng.reciprocal(krec[:, :], ksum[:, :]).then_inc(k_rec.sem, 1)
            eng.wait_ge(q_exp.sem, q_exp.at(g))
            eng.tensor_reduce(qsum[:, :], qe[:, :, :].rearrange("p s (h d) -> p (s h) d", d=HD), AX,
                              ALU.add).then_inc(q_rec.sem, 1)
            eng.wait_ge(q_rec.sem, q_rec.at(g, 1))
            eng.wait_ge(q_soft.sem, q_soft.at(g - 1))
            eng.reciprocal(qrec[:, :], qsum[:, :]).then_inc(q_rec.sem, 1)
            eng.wait_ge(local_exp.sem, local_exp.at(g))
            eng.wait_ge(local_prob.sem, local_prob.at(g - 1))
            eng.reciprocal(lrec[:, :], lsum[:, :]).then_inc(local_rec.sem, 1)

        def keys(g, b):
            eng.wait_ge(k_turn.sem, k_turn.at(g))
            eng.wait_ge(ctx_ps.sem, ctx_ps.at(g - 1))
            eng.tensor_copy(ek[:, :, :], m.ps[:, 5, 0:TS * C].rearrange("p (s c) -> p s c", s=TS)).then_inc(k_sb.sem, 1)

        def context(g, b):
            eng.wait_ge(ctx_ps.sem, ctx_ps.at(g))
            eng.wait_ge(mask_sb.sem, mask_sb.at(g))
            eng.wait_ge(attn_ps.sem, attn_ps.at(g - 1))
            eng.scalar_tensor_tensor(out=ctxm[:, :, :], in0=m.ps[0:C, 5, 256:512].rearrange("p (s c) -> p s c", s=TS),
                                     scalar=SCALE, in1=mask[:, :, :], op0=ALU.mult, op1=ALU.mult).then_inc(ctx_sb.sem, 1)

        def out(g, b):
            rows = m.y[:, bass.ds(g * TS, TS), :]
            eng.wait_ge(y_ps.sem, y_ps.at(g))
            eng.tensor_tensor(rows, m.ps[:, 6, 0:TS * C].rearrange("p (s c) -> p s c", s=TS), rows,
                              ALU.add).then_inc(x1_sb.sem, 1)

        def count(g):
            eng.wait_ge(x1_sb.sem, x1_sb.at(g))
            stats(eng, m, m.y, g, TS, x1_stat.sem)

        def rest(g, b, left, back):
            if back:
                keys(g - 1, 1 - b)
            if left is not None:
                key_maxima(g, b)
            if back:
                context(g - 1, 1 - b)
            if left is not None:
                maxima(g, b)
            if left:
                T.dve(eng, g + 1, 1 - b)
            if left is not None:
                sums(g, b)
            if not isinstance(g, int) or g >= 2:
                count(g - 2)
            if left:
                tokens(g + 1, 1 - b)
            if back:
                out(g - 1, 1 - b)

        eng.wait_ge(m.cst2_sem, 16)
        w_kv.make(eng, col(m, "wkv2"), col(m, "n1g"))
        w_q.make(eng, col(m, "wq2"), col(m, "n1g"))
        w_tok.make(eng, col(m, "wtok"), col(m, "n1g"))
        eng.wait_ge(pre, 3)
        eng.tensor_copy(bias_kv[:, :], m.ps[:, 0, 0:1]).then_inc(pre_sb, 1)
        eng.tensor_copy(bias_q[:, :], m.ps[:, 1, 0:1]).then_inc(pre_sb, 1)
        eng.tensor_copy(bias_tok[:, :], m.ps[:, 2, 0:P]).then_inc(pre_sb, 1)
        eng.wait_ge(pre_sb, 3)
        lagged(eng, TG, ahead, rest)
        count(TG - 1)

    def act(eng):
        def project(g, b):
            eng.wait_ge(proj_ps.sem, proj_ps.at(g, 1))
            eng.wait_ge(local_ps.sem, local_ps.at(g - 2))
            eng.wait_ge(k_exp.sem, k_exp.at(g - 2))
            nc.scalar.activation(kvT[b][:, :], m.ps[:, 1, :], ACT.Identity, bias=bias_kv[:, :]).then_inc(kv_sb.sem, 1)
            nc.scalar.activation(q0T[b][:, :], m.ps[:, 2, :], ACT.Identity, bias=bias_q[:, :]).then_inc(q0_sb.sem, 1)

        def ahead(g, b):
            T.act(eng, g, b, proj_ps)
            project(g, b)

        def keys(g, b):
            eng.wait_ge(k_neg.sem, k_neg.at(g))
            eng.wait_ge(k_turn.sem, k_turn.at(g - 1))
            for s in range(TS):
                sl = slice(s * P, (s + 1) * P)
                nc.scalar.activation(ekT[:, sl], kvT[b][0:C, sl], ACT.Exp, bias=kneg[:, s:s + 1],
                                     accum_out=ksum[:, s:s + 1]).then_inc(k_exp.sem, 1)

        def queries(g, b):
            eng.wait_ge(q_diff.sem, q_diff.at(g))
            eng.wait_ge(q_soft.sem, q_soft.at(g - 1))
            nc.scalar.activation(qe[:, :, :], qd[:, :, :], ACT.Exp).then_inc(q_exp.sem, 1)

        def local(g, b):
            eng.wait_ge(local_neg.sem, local_neg.at(g))
            eng.wait_ge(local_prob.sem, local_prob.at(g - 1))
            for s in range(TS):
                nc.scalar.activation(lex[:, s, :], m.ps[:, 4, s * P:(s + 1) * P], ACT.Exp, bias=lneg[:, s:s + 1],
                                     scale=SCALE, accum_out=lsum[:, s:s + 1]).then_inc(local_exp.sem, 1)

        def turned(g, b):
            eng.wait_ge(q_turn.sem, q_turn.at(g))
            eng.wait_ge(attn_ps.sem, attn_ps.at(g - 1))
            nc.scalar.activation(qsT[:, :], m.ps[0:C, 6, :], ACT.Identity).then_inc(q_sb.sem, 1)
            eng.wait_ge(p_turn.sem, p_turn.at(g))
            nc.scalar.activation(lprobT[:, :, :].rearrange("p s t -> p (s t)"), m.ps[:, 7, :],
                                 ACT.Identity).then_inc(p_sb.sem, 1)

        def attended(g, b):
            eng.wait_ge(attn_ps.sem, attn_ps.at(g))
            eng.wait_ge(y_ps.sem, y_ps.at(g - 1))
            nc.scalar.activation(aT[0:C, :], m.ps[0:C, 7, :], ACT.Identity).then_inc(attn_sb.sem, 1)

        def rest(g, b, left, back):
            if left:
                T.act(eng, g + 1, 1 - b, proj_ps)
            if back:
                turned(g - 1, 1 - b)
            if left is not None:
                keys(g, b)
                queries(g, b)
                local(g, b)
            if back:
                attended(g - 1, 1 - b)
            if left:
                project(g + 1, 1 - b)

        eng.preload_act_table(ACT.Exp)
        eng.wait_ge(pre_sb, 3)
        lagged(eng, TG, ahead, rest)

    return dict(pool=pool, pe=pe, dve=dve, act=act)


def mlp0(nc, ctx, m):
    def sb(name, shape, dt=F32):
        return m.mem.enter_context(nc.sbuf_tensor("m0_" + name, shape, dt))

    def step(name, per=1):
        return Step(nc, ctx, m, "m0_" + name, per)

    m.rounds = TG
    T = Turned(nc, ctx, m, "m0", m.y, 0)
    w1 = m.split["wm1"]
    hid = [[sb(f"hid{b}{n}", [P, NT]) for n in range(2)] for b in range(2)]
    bias = sb("bias", [P, 2])
    pre = ctx.enter_context(nc.semaphore("m0_bias_ps"))
    pre_sb = ctx.enter_context(nc.semaphore("m0_bias_sb"))
    base_sb = step("base_sb", 2)
    hid_ps, hid_sb = step("hid_ps", 2), step("hid_sb", 2)
    out_ps, h_sb, h_stat = step("out_ps"), step("h_sb"), step("h_stat", TS)
    before = m.stat_last
    m.h_last, m.h_rounds, m.stat_last = h_sb, TG - 1, (h_stat.sem, h_stat.at(TG - 1))

    def pool(eng):
        def ahead(g, b):
            T.pool(eng, g, b)
            sl = bass.ds(g * TS, TS)
            settle(eng, m)
            eng.tensor_tensor(m.h[:, sl, :], m.h[:, sl, :], m.y[:, sl, :], ALU.add).then_inc(base_sb.sem, 1)
            eng.wait_ge(base_sb.sem, base_sb.at(g, 1))
            settle(eng, m)
            eng.tensor_tensor(m.h[:, sl, :], m.h[:, sl, :],
                              col(m, "bm2r").unsqueeze(1).broadcast_to([P, TS, C]), ALU.add).then_inc(base_sb.sem, 1)

        eng.wait_ge(*T.norm)
        lagged(eng, TG, ahead, lambda g, b, left, back: ahead(g + 2, b) if (left or 0) > 1 else None, early=1)

    def pe(eng):
        def hidden(g, b):
            eng.wait_ge(T.lo_sb.sem, T.lo_sb.at(g))
            for c in range(2):
                eng.wait_ge(hid_sb.sem, hid_sb.at(g - 1, c + 1))
                sl = slice(c * P, (c + 1) * P)
                eng.matmul(m.ps[:, 1 + c, :], w1.hi[:, sl], T.xs[b][:, :], start=True, stop=False)
                eng.matmul(m.ps[:, 1 + c, :], w1.lo[:, sl], T.xs[b][:, :], start=False,
                           stop=True).then_inc(hid_ps.sem, 1)

        def out(g, b):
            eng.wait_ge(h_sb.sem, h_sb.at(g - 1))
            eng.wait_ge(hid_sb.sem, hid_sb.at(g))
            a = AT["wm2"][0]
            for s in range(TS):
                sl = slice(s * P, (s + 1) * P)
                for c in range(2):
                    mm = eng.matmul(m.ps[:, 3, s * C:(s + 1) * C], hid[b][c][:, sl],
                                    m.cst[:, a + c * C:a + (c + 1) * C], start=(c == 0), stop=(c == 1))
            mm.then_inc(out_ps.sem, 1)

        def rest(g, b, left, back):
            if left is not None:
                hidden(g, b)
            if left:
                T.pe(eng, g + 1, 1 - b)
            if back:
                out(g - 1, 1 - b)

        eng.wait_ge(*before)
        h = slice(0, C)
        a = AT["wm1"][0]
        for c in range(2):
            eng.matmul(m.ps[:, c, 0:1], m.cst[h, a + c * P:a + (c + 1) * P], col(m, "n2b", h),
                       start=True, stop=True).then_inc(pre, 1)
        eng.wait_ge(pre_sb, 2)
        eng.wait_ge(w1.sem, 3)
        lagged(eng, TG, lambda g, b: T.pe(eng, g, b), rest)

    def dve(eng):
        def rest(g, b, left, back):
            if left:
                T.dve(eng, g + 1, 1 - b)
            if back:
                rows = bass.ds(g * TS - TS, TS)
                eng.wait_ge(out_ps.sem, out_ps.at(g - 1))
                eng.wait_ge(base_sb.sem, base_sb.at(g - 1))
                eng.tensor_tensor(m.h[:, rows, :], m.ps[:, 3, 0:TS * C].rearrange("p (s c) -> p s c", s=TS),
                                  m.h[:, rows, :], ALU.add).then_inc(h_sb.sem, 1)
                eng.wait_ge(h_sb.sem, h_sb.at(g - 1))
                stats(eng, m, m.h, g - 1, TS, h_stat.sem)

        w1.make(eng, col(m, "wm1"), col(m, "n2g"))
        eng.wait_ge(pre, 2)
        for c in range(2):
            eng.tensor_tensor(bias[:, c:c + 1], m.ps[:, c, 0:1], m.cst[:, AT["bm1"][0] + c:AT["bm1"][0] + c + 1],
                              ALU.add).then_inc(pre_sb, 1)
        lagged(eng, TG, lambda g, b: T.dve(eng, g, b), rest)

    def act(eng):
        def rest(g, b, left, back):
            for c in range(0 if left is None else 2):
                eng.wait_ge(hid_ps.sem, hid_ps.at(g, c + 1))
                eng.wait_ge(out_ps.sem, out_ps.at(g - 2))
                nc.scalar.activation(hid[b][c][:, :], m.ps[:, 1 + c, :], ACT.Gelu,
                                     bias=bias[:, c:c + 1]).then_inc(hid_sb.sem, 1)
                if c == 0 and left:
                    T.act(eng, g + 1, 1 - b, hid_ps)

        eng.preload_act_table(ACT.Gelu)
        eng.wait_ge(pre_sb, 2)
        lagged(eng, TG, lambda g, b: T.act(eng, g, b, hid_ps), rest)

    return dict(pool=pool, pe=pe, dve=dve, act=act)


def experts0(nc, ctx, m):
    def sb(name, shape, dt=F32):
        return m.mem.enter_context(nc.sbuf_tensor("e0_" + name, shape, dt))

    def step(name, per=1):
        return Step(nc, ctx, m, "e0_" + name, per)

    m.rounds = TG
    E, RING = EXPERTS0, 3
    T = Turned(nc, ctx, m, "e0", m.h, 0)
    gate = m.split["gatew"]
    w1_hi, w1_lo = m.ew1_hi, m.ew1_lo
    w2 = m.ew2_sb
    logit, hot1, hot2, *wt = (sb(n, [P, TS, E]) for n in ("logit", "hot1", "hot2", "wt0", "wt1"))
    top, idx = sb("top", [P, TS, 8]), sb("idx", [P, TS, 8], U32)
    idxf = sb("idxf", [P, TS, 2])
    gap, gexp, den, g1, g2 = (sb(n, [P, TS]) for n in ("gap", "gexp", "den", "g1", "g2"))
    wT = sb("wT", [E, NT])
    hid = [sb(f"hid{n}", [P, NT]) for n in range(RING)]
    part = [sb(f"part{n}", [P, TS, C]) for n in range(RING)]
    acc = sb("acc", [P, TS, C])
    logit_ps, logit_sb, top_sb = step("logit_ps"), step("logit_sb"), step("top_sb", TS)
    idx_sb, idxf_sb, gap_sb, gexp_sb = step("idx_sb", TS), step("idxf_sb"), step("gap_sb"), step("gexp_sb")
    hot_sb, soft_sb, wt_sb = step("hot_sb", 2), step("soft_sb", 3), step("wt_sb", 3)
    wT_ps, wT_sb, b2_ps, y_sb = step("wT_ps"), step("wT_sb"), step("b2_ps"), step("y_sb")
    hid_ps, hid_sb, out_ps = step("hid_ps", E), step("hid_sb", E), step("out_ps", E)
    part_sb, sum_sb, y_stat = step("part_sb", E), step("sum_sb", E), step("y_stat", TS)
    own_sb, var_sb, dev_sb, rstd_sb = step("own_sb", 4), step("var_sb", 2), step("dev_sb"), step("rstd_sb")
    yc_sb, yn_sb, h_sb, h_stat = step("yc_sb"), step("yn_sb", 2), step("h_sb"), step("h_stat", TS)
    y_diff, y_sum, y_m2, y_dd, y_mean, y_var, y_dev, y_rstd = (
        sb("y_" + n, [P, TS]) for n in ("diff", "sum", "m2", "dd", "mean", "var", "dev", "rstd"))
    yc, yn = sb("yc", [P, TS, C]), sb("yn", [P, TS, C])
    beta_sb = step("beta_sb")
    before = m.stat_last
    m.h_last, m.h_rounds, m.stat_last = h_sb, TG - 1, (h_stat.sem, h_stat.at(TG - 1))
    m.banks_last = (y_sb.sem, y_sb.at(TG - 1))
    ALL = [P, TS, C]

    def rounds(eng, rest, ahead, finish=None):
        def call(f, g, b):
            return lambda k: f(g, b, k) if f else None

        ahead(0, 0, None)
        rest(0, 0, call(ahead, 1, 1), call(None, 0, 0))
        rest(1, 1, call(ahead, 2, 0), call(finish, 0, 0))
        with eng.Fori(1, TG // 2 - 1) as i:
            rest(2 * i, 0, call(ahead, 2 * i + 1, 1), call(finish, 2 * i - 1, 1))
            rest(2 * i + 1, 1, call(ahead, 2 * i + 2, 0), call(finish, 2 * i, 0))
        rest(TG - 2, 0, call(ahead, TG - 1, 1), call(finish, TG - 3, 1))
        rest(TG - 1, 1, call(None, 0, 0), call(finish, TG - 2, 0))
        for k in range(E if finish else 0):
            finish(TG - 1, 1, k)

    def pool(eng):
        def ahead(g, b, k):
            if k in (0, None):
                T.pool(eng, g, b)
                sl = bass.ds(g * TS, TS)
                eng.wait_ge(T.norm_sb.sem, T.norm_sb.at(g, 1))
                settle(eng, m)
                eng.tensor_tensor(m.h[:, sl, :], m.h[:, sl, :], col(m, "betr").unsqueeze(1).broadcast_to([P, TS, C]),
                                  ALU.add).then_inc(beta_sb.sem, 1)

            if k is None:
                eng.wait_ge(m.ew_split, 1)
                eng.tensor_tensor(w1_lo[:, :], m.ew1_f[:, :], w1_hi[:, :].bitcast(F32),
                                  ALU.subtract).then_inc(m.ew_split, 1)
            if k in (1, None):
                weigh(g, b)

        def finish(g, b, k):
            if k == 3:
                sl = bass.ds(g * TS, TS)
                eng.wait_ge(var_sb.sem, var_sb.at(g))
                eng.wait_ge(yn_sb.sem, yn_sb.at(g - 1))
                settle(eng, m)
                eng.tensor_tensor(yc[:, :, :], m.y[:, sl, :], bc(y_mean[:, :], ALL), ALU.subtract).then_inc(yc_sb.sem, 1)

        def weigh(g, b):
            eng.wait_ge(hot_sb.sem, hot_sb.at(g))
            eng.wait_ge(soft_sb.sem, soft_sb.at(g))
            sh = [P, TS, E]
            eng.tensor_tensor(hot1[:, :, :], hot1[:, :, :], bc(g1[:, :], sh), ALU.mult).then_inc(wt_sb.sem, 1)
            eng.tensor_tensor(hot2[:, :, :], hot2[:, :, :], bc(g2[:, :], sh), ALU.mult).then_inc(wt_sb.sem, 1)
            eng.wait_ge(wt_sb.sem, wt_sb.at(g, 2))
            eng.wait_ge(part_sb.sem, part_sb.at(g - 2))
            eng.wait_ge(wT_ps.sem, wT_ps.at(g - 2))
            eng.tensor_tensor(wt[b][:, :, :], hot1[:, :, :], hot2[:, :, :], ALU.add).then_inc(wt_sb.sem, 1)

        def rest(g, b, ahead, finish):
            for e in range(E):
                eng.wait_ge(part_sb.sem, part_sb.at(g, e + 1))
                if e == 0:
                    eng.wait_ge(y_sb.sem, y_sb.at(g - 1))
                else:
                    eng.wait_ge(sum_sb.sem, sum_sb.at(g, e))
                eng.tensor_tensor(acc[:, :, :], T.xn[b] if e == 0 else acc[:, :, :], part[e % RING][:, :, :],
                                  ALU.add).then_inc(sum_sb.sem, 1)
                finish(e)
                if e == 1:
                    ahead(0)
                if e == 14:
                    ahead(1)

        eng.wait_ge(*T.norm)
        rounds(eng, rest, ahead, finish)

    def pe(eng):
        def ahead(g, b, k):
            if k in (0, None):
                eng.wait_ge(logit_sb.sem, logit_sb.at(g - 1))
                T.pe(eng, g, b)
            if k in (1, None):
                eng.wait_ge(T.lo_sb.sem, T.lo_sb.at(g))
                for s in range(TS):
                    sl, to = slice(s * P, (s + 1) * P), slice(s * E, (s + 1) * E)
                    eng.matmul(m.ps[:, 0, to], T.xs[b][:, sl], gate.hi[:, :], start=True, stop=False)
                    mm = eng.matmul(m.ps[:, 0, to], T.xs[b][:, sl], gate.lo[:, :], start=False, stop=True)
                mm.then_inc(logit_ps.sem, 1)
            if k is None:
                eng.wait_ge(m.ew_split, 2)

        def rest(g, b, ahead, finish):
            def hidden(e):
                if e < RING:
                    eng.wait_ge(hid_sb.sem, hid_sb.at(g - 1))
                else:
                    eng.wait_ge(hid_sb.sem, hid_sb.at(g, e - RING + 1))
                sl = slice(e * F0, (e + 1) * F0)
                eng.matmul(m.ps[:, 2 + e % RING, :], w1_hi[:, sl], T.xs[b][:, :], start=True, stop=False)
                eng.matmul(m.ps[:, 2 + e % RING, :], w1_lo[:, sl], T.xs[b][:, :], start=False,
                           stop=True).then_inc(hid_ps.sem, 1)

            def out(e):
                eng.wait_ge(hid_sb.sem, hid_sb.at(g, e + 1))
                if e < RING:
                    eng.wait_ge(part_sb.sem, part_sb.at(g - 1))
                else:
                    eng.wait_ge(part_sb.sem, part_sb.at(g, e - RING + 1))
                for s in range(TS):
                    mm = eng.matmul(m.ps[:, 5 + e % RING, s * P:(s + 1) * P], hid[e % RING][:, s * P:(s + 1) * P],
                                    w2[:, e * C:e * C + P], start=True, stop=True)
                mm.then_inc(out_ps.sem, 1)

            hidden(0)
            hidden(1)
            for e in range(E):
                if e + 2 < E:
                    hidden(e + 2)
                out(e)
                if e == 3:
                    eng.wait_ge(wt_sb.sem, wt_sb.at(g))
                    eng.wait_ge(y_sb.sem, y_sb.at(g - 1))
                    for s in range(TS):
                        mm = eng.transpose(m.ps[0:E, 1, s * P:(s + 1) * P], wt[b][:, s, :], col(m, "ident"))
                    mm.then_inc(wT_ps.sem, 1)
                if e == 5:
                    eng.wait_ge(wT_sb.sem, wT_sb.at(g))
                    for s in range(TS):
                        mm = eng.matmul(m.ps[:, 1, s * C:(s + 1) * C], wT[:, s * P:(s + 1) * P],
                                        col(m, "eb2", slice(0, E)), start=True, stop=True)
                    mm.then_inc(b2_ps.sem, 1)
                if e == 5:
                    ahead(0)
                if e == 8:
                    ahead(1)

        eng.wait_ge(gate.sem, 3)
        eng.wait_ge(m.ew2_sem, 16)
        eng.wait_ge(m.ew2_pad, 1)
        rounds(eng, rest, ahead)

    def dve(eng):
        def ahead(g, b, k):
            if k in (0, None):
                T.dve(eng, g, b)
            if k in (1, None):
                choose(g)
            if k in (2, None):
                soften(g)

        def finish(g, b, k):
            sl = bass.ds(g * TS, TS)
            st = m.stat[:, sl, :]
            if k == 1:
                eng.wait_ge(y_stat.sem, y_stat.at(g))
                eng.tensor_tensor(y_diff[:, :], st[:, :, 1], st[:, :, 4], ALU.subtract).then_inc(own_sb.sem, 1)
                eng.tensor_tensor(y_sum[:, :], st[:, :, 1], st[:, :, 4], ALU.add).then_inc(own_sb.sem, 1)
                eng.tensor_tensor(y_m2[:, :], st[:, :, 2], st[:, :, 5], ALU.add).then_inc(own_sb.sem, 1)
            if k == 2:
                eng.wait_ge(own_sb.sem, own_sb.at(g, 3))
                eng.wait_ge(yc_sb.sem, yc_sb.at(g - 1))
                eng.scalar_tensor_tensor(out=y_dd[:, :], in0=y_diff[:, :], scalar=0.25, in1=y_diff[:, :],
                                         op0=ALU.mult, op1=ALU.mult).then_inc(own_sb.sem, 1)
                eng.tensor_scalar(y_mean[:, :], y_sum[:, :], 0.5, None, ALU.mult).then_inc(var_sb.sem, 1)
                eng.wait_ge(own_sb.sem, own_sb.at(g))
                eng.scalar_tensor_tensor(out=y_var[:, :], in0=y_m2[:, :], scalar=1.0 / C, in1=y_dd[:, :],
                                         op0=ALU.mult, op1=ALU.add).then_inc(var_sb.sem, 1)
            if k == 6:
                eng.wait_ge(dev_sb.sem, dev_sb.at(g))
                eng.reciprocal(y_rstd[:, :], y_dev[:, :]).then_inc(rstd_sb.sem, 1)
            if k == 7:
                eng.wait_ge(yc_sb.sem, yc_sb.at(g))
                eng.wait_ge(rstd_sb.sem, rstd_sb.at(g))
                eng.tensor_tensor(yn[:, :, :], yc[:, :, :], bc(y_rstd[:, :], ALL), ALU.mult).then_inc(yn_sb.sem, 1)
            if k == 9:
                eng.wait_ge(yn_sb.sem, yn_sb.at(g, 1))
                eng.tensor_tensor(yn[:, :, :], yn[:, :, :], col(m, "gamr").unsqueeze(1).broadcast_to(ALL),
                                  ALU.mult).then_inc(yn_sb.sem, 1)
            if k == 10:
                eng.wait_ge(yn_sb.sem, yn_sb.at(g))
                eng.wait_ge(beta_sb.sem, beta_sb.at(g))
                eng.tensor_tensor(m.h[:, sl, :], m.h[:, sl, :], yn[:, :, :], ALU.add).then_inc(h_sb.sem, 1)
            if k == 14:
                eng.wait_ge(h_sb.sem, h_sb.at(g))
                settle(eng, m)
                stats(eng, m, m.h, g, TS, h_stat.sem)

        def choose(g):
            eng.wait_ge(logit_ps.sem, logit_ps.at(g))
            eng.tensor_tensor(logit[:, :, :], m.ps[:, 0, 0:TS * E].rearrange("p (s e) -> p s e", s=TS),
                              col(m, "gatebr").unsqueeze(1).broadcast_to([P, TS, E]), ALU.add).then_inc(logit_sb.sem, 1)
            eng.wait_ge(logit_sb.sem, logit_sb.at(g))
            eng.wait_ge(gap_sb.sem, gap_sb.at(g - 1))
            settle(eng, m)
            for s in range(TS):
                eng.max(top[:, s, :], logit[:, s, :]).then_inc(top_sb.sem, 1)
            eng.wait_ge(top_sb.sem, top_sb.at(g))
            settle(eng, m)
            for s in range(TS):
                eng.max_index(idx[:, s, :], top[:, s, :], logit[:, s, :]).then_inc(idx_sb.sem, 1)
            eng.wait_ge(gexp_sb.sem, gexp_sb.at(g - 1))
            eng.tensor_tensor(gap[:, :], top[:, :, 1], top[:, :, 0], ALU.subtract).then_inc(gap_sb.sem, 1)
            eng.wait_ge(idx_sb.sem, idx_sb.at(g))
            eng.tensor_copy(idxf[:, :, :], idx[:, :, 0:2]).then_inc(idxf_sb.sem, 1)
            eng.wait_ge(idxf_sb.sem, idxf_sb.at(g))
            eng.wait_ge(wt_sb.sem, wt_sb.at(g - 1))
            sh = [P, TS, E]
            for n, hot in enumerate((hot1, hot2)):
                eng.tensor_tensor(hot[:, :, :], col(m, "iota16").unsqueeze(1).broadcast_to(sh),
                                  bc(idxf[:, :, n], sh), ALU.is_equal).then_inc(hot_sb.sem, 1)

        def soften(g):
            eng.wait_ge(gexp_sb.sem, gexp_sb.at(g))
            eng.tensor_scalar(den[:, :], gexp[:, :], 1.0, None, ALU.add).then_inc(soft_sb.sem, 1)
            eng.wait_ge(soft_sb.sem, soft_sb.at(g, 1))
            eng.reciprocal(g1[:, :], den[:, :]).then_inc(soft_sb.sem, 1)
            eng.wait_ge(soft_sb.sem, soft_sb.at(g, 2))
            eng.tensor_tensor(g2[:, :], gexp[:, :], g1[:, :], ALU.mult).then_inc(soft_sb.sem, 1)

        def rest(g, b, ahead, finish):
            eng.wait_ge(wt_sb.sem, wt_sb.at(g))
            for e in range(E):
                eng.wait_ge(out_ps.sem, out_ps.at(g, e + 1))
                if e < RING:
                    eng.wait_ge(sum_sb.sem, sum_sb.at(g - 1))
                else:
                    eng.wait_ge(sum_sb.sem, sum_sb.at(g, e - RING + 1))
                eng.tensor_tensor(part[e % RING][:, :, :],
                                  m.ps[:, 5 + e % RING, :].rearrange("p (s c) -> p s c", s=TS)[:, :, 0:C],
                                  bc(wt[b][:, :, e], [P, TS, C]), ALU.mult).then_inc(part_sb.sem, 1)
                finish(e)
                if e == 6:
                    ahead(0)
                if e == 9:
                    ahead(1)
                if e == 12:
                    ahead(2)
            eng.wait_ge(b2_ps.sem, b2_ps.at(g))
            eng.wait_ge(sum_sb.sem, sum_sb.at(g))
            eng.tensor_tensor(m.y[:, bass.ds(g * TS, TS), :], m.ps[:, 1, 0:TS * C].rearrange("p (s c) -> p s c", s=TS),
                              acc[:, :, :], ALU.add).then_inc(y_sb.sem, 1)
            eng.wait_ge(y_sb.sem, y_sb.at(g))
            stats(eng, m, m.y, g, TS, y_stat.sem)

        gate.make(eng, col(m, "gatew"))
        eng.wait_ge(m.ew1_sem, 16)
        eng.tensor_copy(w1_hi[:, :], m.ew1_f[:, :]).then_inc(m.ew_split, 1)
        rounds(eng, rest, ahead, finish)

    def act(eng):
        def ahead(g, b, k):
            if k in (0, None):
                T.act(eng, g, b, hid_ps)
            if k in (1, None):
                eng.wait_ge(gap_sb.sem, gap_sb.at(g))
                eng.wait_ge(soft_sb.sem, soft_sb.at(g - 1))
                nc.scalar.activation(gexp[:, :], gap[:, :], ACT.Exp).then_inc(gexp_sb.sem, 1)

        def finish(g, b, k):
            if k == 4:
                eng.wait_ge(var_sb.sem, var_sb.at(g))
                eng.wait_ge(rstd_sb.sem, rstd_sb.at(g - 1))
                nc.scalar.activation(y_dev[:, :], y_var[:, :], ACT.Sqrt, bias=m.eps[:, :]).then_inc(dev_sb.sem, 1)

        def rest(g, b, ahead, finish):
            for e in range(E):
                eng.wait_ge(hid_ps.sem, hid_ps.at(g, e + 1))
                if e < RING:
                    eng.wait_ge(out_ps.sem, out_ps.at(g - 1))
                else:
                    eng.wait_ge(out_ps.sem, out_ps.at(g, e - RING + 1))
                nc.scalar.activation(hid[e % RING][:, :], m.ps[:, 2 + e % RING, :], ACT.Relu,
                                     bias=m.cst[:, AT["eb1"][0] + e:AT["eb1"][0] + e + 1]).then_inc(hid_sb.sem, 1)
                if e == 6:
                    eng.wait_ge(wT_ps.sem, wT_ps.at(g))
                    eng.wait_ge(b2_ps.sem, b2_ps.at(g - 1))
                    nc.scalar.activation(wT[:, :], m.ps[0:E, 1, :], ACT.Identity).then_inc(wT_sb.sem, 1)
                finish(e)
                if e == 7:
                    ahead(0)
                if e == 13:
                    ahead(1)

        eng.preload_act_table(ACT.Exp)
        rounds(eng, rest, ahead, finish)

    return dict(pool=pool, pe=pe, dve=dve, act=act)


def attention1(nc, ctx, m):
    def sb(name, shape, dt=F32):
        return m.mem.enter_context(nc.sbuf_tensor("a1_" + name, shape, dt))

    def step(name, per=1):
        return Step(nc, ctx, m, "a1_" + name, per)

    m.rounds = TG
    H, V, W = HEADS, C + 1, 96
    T = Turned(nc, ctx, m, "a1", m.h, 0)
    w_a, w_m = Split(nc, ctx, "a1_a", H * C, m.mem), Split(nc, ctx, "a1_m", H * C, m.mem)
    xt = [[sb(f"xt{h}{b}", [P, NT]) for b in range(2)] for h in range(2)]
    u = [sb(f"u{b}", [P, TS, H // 2, P]) for b in range(2)]
    v = [sb(f"v{b}", [P, TS, H * V + W - V]) for b in range(2)]
    diff = sb("diff", [P, H, P])
    ex = [sb(f"ex{b}", [P, H, P]) for b in range(2)]
    prob = [sb(f"prob{b}", [P, H, P]) for b in range(2)]
    rmax, rec = sb("rmax", [P, H]), sb("rec", [P, H])
    part, sum4, sum2, sum1 = (sb(n, [P, k, C]) for n, k in (("part", H), ("sum4", 4), ("sum2", 2), ("sum1", 1)))

    w_ps = ctx.enter_context(nc.semaphore("a1_weights_ps"))
    ones_set, zeros_set = (ctx.enter_context(nc.semaphore("a1_" + n)) for n in ("ones_set", "zeros_set"))
    base_sb = step("base_sb")
    xt_sb = [step("xt0_sb"), step("xt1_sb")]
    uv_ps, uv_sb = step("uv_ps", 8), step("uv_sb", 8)
    score_ps, max_sb, diff_sb, exp_sb = step("score_ps", TS), step("max_sb", TS), step("diff_sb", TS), step("exp_sb", TS)
    turn_ps, prob_sb = step("turn_ps", TS), step("prob_sb", TS)
    sum_ps, rec_sb, part_sb = step("sum_ps", TS), step("rec_sb", TS), step("part_sb", TS)
    add_sb, h_sb, h_stat = step("add_sb", 3 * TS), step("h_sb", TS), step("h_stat", TS)
    before = m.stat_last
    m.h_last, m.h_rounds, m.stat_last = h_sb, TG - 1, (h_stat.sem, h_stat.at(TG - 1))
    weights = ((w_a, m.ps[:, 2, :], float(C / H) ** -0.5), (w_m, m.ps[:, 3, :], 1.0))

    def rounds(eng, order, turned, piece=None, early=0, prepare=None, **parts):
        lags = dict(now=0, lag1=1, lag2=2, lag3=3)
        slots = {(0, "x1"): lambda g, b: turned(g + early, (b + early) % 2)}
        places = ((1, "x1"), (1, "x2"), (2, "x0"), (2, "x1"), (2, "x2"), (3, "x0"), (3, "x1"), (3, "x2"))
        for n, at in enumerate(places):
            slots[at] = (lambda g, b, n=n: piece(g, b, n)) if piece else None

        def rest(g, b, first=False, more=True):
            for s in range(TS):
                for name in order:
                    if name in lags:
                        back = s - lags[name]
                        if back >= 0:
                            parts[name](g, b, back)
                        elif not first:
                            parts[name](g - 1, 1 - b, back + TS)
                    elif more and slots.get((s, name)):
                        slots[s, name](g + 1, 1 - b)

        turned(0, 0)
        if prepare:
            prepare()
        if early:
            turned(1, 1)
        for k in range(8 if piece else 0):
            piece(0, 0, k, banks=2)
        rest(0, 0, first=True)
        rest(1, 1)
        with eng.Fori(1, TG // 2 - 1) as i:
            rest(2 * i, 0)
            rest(2 * i + 1, 1)
        rest(TG - 2, 0, more=not early)
        rest(TG - 1, 1, more=False)
        for s in range(TS, TS + 3):
            for name in order:
                if name in lags and s - lags[name] < TS:
                    parts[name](TG - 1, 1, s - lags[name])

    def sample(g, s):
        return bass.ds(g * TS + s, 1)

    def pool(eng):
        def turned(g, b):
            T.pool(eng, g, b)
            sl = bass.ds(g * TS, TS)
            eng.wait_ge(T.norm_sb.sem, T.norm_sb.at(g, 1))
            settle(eng, m)
            eng.tensor_tensor(m.h[:, sl, :], m.h[:, sl, :],
                              col(m, "boutr").unsqueeze(1).broadcast_to([P, TS, C]), ALU.add).then_inc(base_sb.sem, 1)

        def lag2(g, b, s):
            eng.wait_ge(part_sb.sem, part_sb.at(g, s + 1))
            eng.tensor_tensor(sum4[:, :, :], part[:, 0:4, :], part[:, 4:8, :], ALU.add).then_inc(add_sb.sem, 1)
            eng.wait_ge(add_sb.sem, add_sb.at(g, 3 * s + 1))
            eng.tensor_tensor(sum2[:, :, :], sum4[:, 0:2, :], sum4[:, 2:4, :], ALU.add).then_inc(add_sb.sem, 1)
            eng.wait_ge(add_sb.sem, add_sb.at(g, 3 * s + 2))
            eng.tensor_tensor(sum1[:, :, :], sum2[:, 0:1, :], sum2[:, 1:2, :], ALU.add).then_inc(add_sb.sem, 1)
            eng.wait_ge(add_sb.sem, add_sb.at(g, 3 * s + 3))
            eng.wait_ge(base_sb.sem, base_sb.at(g))
            settle(eng, m)
            eng.tensor_tensor(m.h[:, sample(g, s), :], m.h[:, sample(g, s), :], sum1[:, :, :], ALU.add).then_inc(h_sb.sem, 1)

        def prepare():
            for w, _, _ in weights:
                eng.wait_ge(w.sem, 2)
                eng.tensor_tensor(w.lo[:, :], w.f[:, :], w.hi[:, :].bitcast(F32), ALU.subtract).then_inc(w.sem, 1)

        eng.wait_ge(*before)
        for b in range(2):
            sums = v[b][:, :, 0:H * V].rearrange("p s (h c) -> p s h c", c=V)[:, :, :, C]
            eng.memset(sums, 1.0).then_inc(ones_set, 1)
            eng.memset(v[b][:, :, H * V:], 1.0).then_inc(ones_set, 1)
        eng.wait_ge(*T.norm)
        rounds(eng, ("lag2", "x1"), turned, early=1, prepare=prepare, lag2=lag2)

    def pe(eng):
        def turned(g, b):
            for x in xt_sb:
                eng.wait_ge(x.sem, x.at(g - 1))
            T.pe(eng, g, b)

        def piece(g, b, k, banks=1):
            bank = (1, 6)[k % banks]
            if k == 0:
                eng.wait_ge(T.lo_sb.sem, T.lo_sb.at(g))
                eng.wait_ge(uv_sb.sem, uv_sb.at(g - 1))
            if k >= banks:
                eng.wait_ge(uv_sb.sem, uv_sb.at(g, k - banks + 1))
            n = k // 2
            sl = slice(n * P, (n + 1) * P)
            if k % 2 == 0:
                eng.matmul(m.ps[:, bank, :], w_a.hi[:, sl], T.xs[b][:, :], start=True, stop=False)
                mm = eng.matmul(m.ps[:, bank, :], w_a.lo[:, sl], T.xs[b][:, :], start=False, stop=True)
            else:
                eng.matmul(m.ps[:, bank, :], T.xs[b][:, sl], w_m.hi[:, :], start=True, stop=False)
                mm = eng.matmul(m.ps[:, bank, :], T.xs[b][:, sl], w_m.lo[:, :], start=False, stop=True)
            mm.then_inc(uv_ps.sem, 1)

        def now(g, b, s):
            if s == 0:
                eng.wait_ge(uv_sb.sem, uv_sb.at(g, 7))
                for x in xt_sb:
                    eng.wait_ge(x.sem, x.at(g))
                eng.wait_ge(diff_sb.sem, diff_sb.at(g - 1))
            else:
                eng.wait_ge(diff_sb.sem, diff_sb.at(g, s))
            for h in range(2):
                mm = eng.matmul(m.ps[:, 2 + h, :], xt[h][b][:, s * P:(s + 1) * P],
                                u[b][:, s, :, :].rearrange("p h t -> p (h t)"), start=True, stop=True)
            mm.then_inc(score_ps.sem, 1)

        def lag1(g, b, s):
            eng.wait_ge(prob_sb.sem, prob_sb.at(g, s) if s else prob_sb.at(g - 1))
            eng.wait_ge(exp_sb.sem, exp_sb.at(g, s + 1))
            for j in range(H):
                mm = eng.transpose(m.ps[:, 4 + j // 4, (j % 4) * P:(j % 4 + 1) * P], ex[s % 2][:, j, :],
                                   col(m, "ident"))
            mm.then_inc(turn_ps.sem, 1)

        def lag2(g, b, s):
            first = isinstance(g, int) and g + s == 0
            eng.wait_ge(uv_sb.sem, uv_sb.at(g, 8 if first else 2 * s + 2))
            eng.wait_ge(prob_sb.sem, prob_sb.at(g, s + 1))
            if s > 0:
                eng.wait_ge(part_sb.sem, part_sb.at(g, s))
            else:
                eng.wait_ge(part_sb.sem, part_sb.at(g - 1))
            for j in range(H):
                head = 2 * (j % 4) + j // 4
                mm = eng.matmul(m.ps[:, 6 + j // 4, (j % 4) * P:(j % 4) * P + W], prob[s % 2][:, j, :],
                                v[b][:, s, head * V:head * V + W], start=True, stop=True)
            mm.then_inc(sum_ps.sem, 1)

        eng.wait_ge(*m.banks_last)
        d = slice(0, C)
        for h in range(H):
            out, dup = slice(h * C, (h + 1) * C), slice(h * P, (h + 1) * P)
            for bank, l, r in ((2, "wkT", "wqT"), (3, "wvT", "wout")):
                mm = eng.matmul(m.ps[:, bank, out], col(m, l, d)[:, dup], col(m, r, d)[:, out], start=True, stop=True)
        mm.then_inc(w_ps, 1)

        def prepare():
            eng.wait_ge(w_a.sem, 3)
            eng.wait_ge(w_m.sem, 3)
            eng.wait_ge(ones_set, 4)
            eng.wait_ge(zeros_set, 4)

        rounds(eng, ("now", "x0", "lag1", "x1", "lag2", "x2"), turned, piece, prepare=prepare,
               now=now, lag1=lag1, lag2=lag2)

    def dve(eng):
        def turned(g, b):
            T.dve(eng, g, b)
            eng.wait_ge(score_ps.sem, score_ps.at(g - 2))
            eng.tensor_copy(xt[1][b][64:P, :], m.ps[64:P, 0, :]).then_inc(xt_sb[1].sem, 1)

        def now(g, b, s):
            eng.wait_ge(score_ps.sem, score_ps.at(g, s + 1))
            src = m.ps[:, 2:4, :].rearrange("p a (j t) -> p (a j) t", t=P)
            eng.tensor_reduce(rmax[:, :], src, AX, ALU.max).then_inc(max_sb.sem, 1)
            eng.wait_ge(max_sb.sem, max_sb.at(g, s + 1))
            eng.wait_ge(exp_sb.sem, exp_sb.at(g, s) if s else exp_sb.at(g - 1))
            eng.tensor_tensor(diff[:, :, :], src, bc(rmax[:, :], [P, H, P]), ALU.subtract).then_inc(diff_sb.sem, 1)

        def lag2(g, b, s):
            eng.wait_ge(sum_ps.sem, sum_ps.at(g, s + 1))
            src = m.ps[:, 6:8, :].rearrange("p a (j t) -> p (a j) t", t=P)
            eng.reciprocal(rec[:, :], src[:, :, C]).then_inc(rec_sb.sem, 1)
            eng.wait_ge(rec_sb.sem, rec_sb.at(g, s + 1))
            eng.wait_ge(add_sb.sem, add_sb.at(g, 3 * s - 2) if s else add_sb.at(g - 1, 3 * TS - 2))
            eng.tensor_tensor(part[:, :, :], src[:, :, 0:C], bc(rec[:, :], [P, H, C]), ALU.mult).then_inc(part_sb.sem, 1)

        def lag3(g, b, s):
            eng.wait_ge(h_sb.sem, h_sb.at(g, s + 1))
            eng.bn_stats(m.stat[:, sample(g, s), :], m.h[:, sample(g, s), :]).then_inc(h_stat.sem, 1)

        for b in range(2):
            eng.memset(xt[0][b][64:P, :], 0.0).then_inc(zeros_set, 1)
            eng.memset(xt[1][b][0:64, :], 0.0).then_inc(zeros_set, 1)
        rounds(eng, ("now", "lag3", "x1", "lag2"), turned, now=now, lag2=lag2, lag3=lag3)

    def act(eng):
        def turned(g, b):
            T.act(eng, g, b, uv_ps)
            eng.wait_ge(score_ps.sem, score_ps.at(g - 2))
            nc.scalar.activation(xt[0][b][0:64, :], m.ps[0:64, 0, :], ACT.Identity).then_inc(xt_sb[0].sem, 1)

        def piece(g, b, k, banks=1):
            bank = (1, 6)[k % banks]
            eng.wait_ge(uv_ps.sem, uv_ps.at(g, k + 1))
            n = k // 2
            if k % 2 == 0:
                eng.wait_ge(score_ps.sem, score_ps.at(g - 2))
                nc.scalar.activation(u[b][:, :, n, :], m.ps[:, bank, :].rearrange("p (s t) -> p s t", s=TS),
                                     ACT.Identity).then_inc(uv_sb.sem, 1)
            else:
                eng.wait_ge(sum_ps.sem, sum_ps.at(g - 2))
                nc.scalar.activation(v[b][:, n, 0:H * V].rearrange("p (h c) -> p h c", c=V)[:, :, 0:C],
                                     m.ps[:, bank, :].rearrange("p (h c) -> p h c", c=C), ACT.Identity).then_inc(uv_sb.sem, 1)

        def now(g, b, s):
            eng.wait_ge(diff_sb.sem, diff_sb.at(g, s + 1))
            eng.wait_ge(turn_ps.sem, turn_ps.at(g, s - 1) if s >= 2 else turn_ps.at(g - 1, s + 3))
            nc.scalar.activation(ex[s % 2][:, :, :], diff[:, :, :], ACT.Exp).then_inc(exp_sb.sem, 1)

        def lag1(g, b, s):
            eng.wait_ge(turn_ps.sem, turn_ps.at(g, s + 1))
            eng.wait_ge(sum_ps.sem, sum_ps.at(g, s - 1) if s >= 2 else sum_ps.at(g - 1, s + 3))
            nc.scalar.activation(prob[s % 2][:, :, :], m.ps[:, 4:6, :].rearrange("p a (j t) -> p (a j) t", t=P),
                                 ACT.Identity).then_inc(prob_sb.sem, 1)

        eng.preload_act_table(ACT.Exp)
        eng.wait_ge(w_ps, 1)
        for w, src, scale in weights:
            for to in (w.f, w.hi):
                nc.scalar.activation(to[:, :], src, ACT.Identity, scale=scale).then_inc(w.sem, 1)
        rounds(eng, ("x0", "lag1", "x1", "now", "x2"), turned, piece, now=now, lag1=lag1)

    return dict(pool=pool, pe=pe, dve=dve, act=act)


def experts1(nc, ctx, m):
    def sb(name, shape, dt=F32):
        return m.mem.enter_context(nc.sbuf_tensor("e1_" + name, shape, dt))

    def step(name, per=1):
        return Step(nc, ctx, m, "e1_" + name, per)

    m.rounds = TG
    E, NC = EXPERTS1, HID1 // P
    MASK_BANKS = (4, 5, 7, 4)
    T = Turned(nc, ctx, m, "e1", m.h, 0)
    rout, w1 = m.split["routw"], m.split["fw1"]
    sel = sb("sel", [E, HID1], BF16)
    logit, hot = sb("logit", [P, TS, E]), sb("hot", [P, TS, E])
    top, idx, idxf = sb("top", [P, TS, 8]), sb("idx", [P, TS, 8], U32), sb("idxf", [P, TS])
    hotT, hotT16 = [sb(f"hotT{b}", [E, NT]) for b in range(2)], sb("hotT16", [E, NT], BF16)
    hid = [sb(f"hid{n}", [P, NT]) for n in range(NC)]
    kept = [sb(f"kept{n}", [P, NT]) for n in range(NC)]
    res = [sb(f"res{b}", [P, TS, C]) for b in range(2)]
    sel_sb = ctx.enter_context(nc.semaphore("e1_sel"))
    logit_ps, logit_sb, top_sb = step("logit_ps"), step("logit_sb"), step("top_sb", TS)
    idx_sb, idxf_sb, hot_sb = step("idx_sb", TS), step("idxf_sb"), step("hot_sb")
    hotT_ps, hotT_sb, hotT16_sb = step("hotT_ps"), step("hotT_sb"), step("hotT16_sb")
    hid_ps, hid_sb, mask_ps, kept_sb = step("hid_ps", NC), step("hid_sb", NC), step("mask_ps", NC), step("kept_sb", NC)
    out_ps, res_sb = step("out_ps"), step("res_sb")
    stored = [ctx.enter_context(nc.semaphore(f"out_stored{b}")) for b in range(2)]
    before = m.stat_last

    def sp(eng):
        dst = m.out.rearrange("s t c -> t s c")
        with eng.Fori(0, TG // 2) as i:
            for b in range(2):
                g = 2 * i + b
                eng.wait_ge(res_sb.sem, res_sb.at(g))
                eng.dma_start(dst[:, bass.ds(g * TS, TS), :], res[b][:, :, :]).then_inc(stored[b], 16)
        for b in range(2):
            eng.wait_ge(stored[b], 16 * (TG // 2) + 16)

    def pool(eng):
        eng.wait_ge(*T.norm)
        lagged(eng, TG, lambda g, b: T.pool(eng, g, b),
               lambda g, b, left, back: T.pool(eng, g + 2, b) if (left or 0) > 1 else None, early=1)

    def pe(eng):
        def logits(g, b):
            eng.wait_ge(T.lo_sb.sem, T.lo_sb.at(g))
            eng.wait_ge(hotT_sb.sem, hotT_sb.at(g - 1))
            eng.wait_ge(hotT16_sb.sem, hotT16_sb.at(g - 1))
            for s in range(TS):
                sl, to = slice(s * P, (s + 1) * P), slice(s * E, (s + 1) * E)
                eng.matmul(m.ps[:, 1, to], T.xs[b][:, sl], rout.hi[:, :], start=True, stop=False)
                mm = eng.matmul(m.ps[:, 1, to], T.xs[b][:, sl], rout.lo[:, :], start=False, stop=True)
            mm.then_inc(logit_ps.sem, 1)

        def hidden(g, b, c):
            sl = slice(c * P, (c + 1) * P)
            eng.wait_ge(hid_sb.sem, hid_sb.at(g, c - 1) if c >= 2 else hid_sb.at(g - 1))
            eng.matmul(m.ps[:, 2 + c % 2, :], w1.hi[:, sl], T.xs[b][:, :], start=True, stop=False)
            eng.matmul(m.ps[:, 2 + c % 2, :], w1.lo[:, sl], T.xs[b][:, :], start=False,
                       stop=True).then_inc(hid_ps.sem, 1)

        def mask(g, c):
            if c == 0:
                eng.wait_ge(hotT16_sb.sem, hotT16_sb.at(g))
            eng.wait_ge(kept_sb.sem, kept_sb.at(g, 1) if c == 3 else kept_sb.at(g - 1))
            eng.matmul(m.ps[:, MASK_BANKS[c], :], sel[:, c * P:(c + 1) * P], hotT16[:, :], start=True,
                       stop=True).then_inc(mask_ps.sem, 1)

        def turn_hot(g, b):
            eng.wait_ge(hot_sb.sem, hot_sb.at(g))
            for s in range(TS):
                mm = eng.transpose(m.ps[0:E, 1, s * P:(s + 1) * P], hot[:, s, :], col(m, "ident"))
            mm.then_inc(hotT_ps.sem, 1)

        def out(g, b, half):
            eng.wait_ge(hotT_sb.sem, hotT_sb.at(g))
            eng.wait_ge(kept_sb.sem, kept_sb.at(g))
            eng.wait_ge(res_sb.sem, res_sb.at(g - 1))
            a, b2 = AT["fw2"][0], AT["fb2"][0]
            for s in range(2 * half, 2 * half + 2):
                sl = slice(s * P, (s + 1) * P)
                for c in range(NC):
                    eng.matmul(m.ps[:, 6, sl], kept[c][:, sl], m.cst[:, a + c * C:a + c * C + P],
                               start=(c == 0), stop=False)
                mm = eng.matmul(m.ps[:, 6, sl], hotT[b][:, sl], m.cst[0:E, b2:b2 + P], start=False, stop=True)
            if half:
                mm.then_inc(out_ps.sem, 1)

        def rest(g, b, left, back):
            if back:
                hidden(g - 1, 1 - b, 0)
                hidden(g - 1, 1 - b, 1)
                mask(g - 1, 0)
                mask(g - 1, 1)
                hidden(g - 1, 1 - b, 2)
                mask(g - 1, 2)
                hidden(g - 1, 1 - b, 3)
                mask(g - 1, 3)
            if left is not None:
                logits(g, b)
            if left:
                T.pe(eng, g + 1, 1 - b)
            if back:
                out(g - 1, 1 - b, 0)
            if left is not None:
                turn_hot(g, b)
            if back:
                out(g - 1, 1 - b, 1)

        def ahead(g, b):
            T.pe(eng, g, b)
            eng.wait_ge(rout.sem, 3)
            eng.wait_ge(w1.sem, 3)
            eng.wait_ge(sel_sb, 1)

        lagged(eng, TG, ahead, rest)

    def dve(eng):
        def choose(g, b):
            eng.wait_ge(logit_ps.sem, logit_ps.at(g))
            sh = [P, TS, E]
            eng.tensor_tensor(logit[:, :, :], m.ps[:, 1, 0:TS * E].rearrange("p (s e) -> p s e", s=TS),
                              col(m, "routbr").unsqueeze(1).broadcast_to(sh), ALU.add).then_inc(logit_sb.sem, 1)
            eng.wait_ge(logit_sb.sem, logit_sb.at(g))
            settle(eng, m)
            for s in range(TS):
                eng.max(top[:, s, :], logit[:, s, :]).then_inc(top_sb.sem, 1)
            eng.wait_ge(top_sb.sem, top_sb.at(g))
            settle(eng, m)
            for s in range(TS):
                eng.max_index(idx[:, s, :], top[:, s, :], logit[:, s, :]).then_inc(idx_sb.sem, 1)
            eng.wait_ge(idx_sb.sem, idx_sb.at(g))
            eng.tensor_copy(idxf[:, :], idx[:, :, 0]).then_inc(idxf_sb.sem, 1)
            eng.wait_ge(idxf_sb.sem, idxf_sb.at(g))
            eng.wait_ge(hotT_ps.sem, hotT_ps.at(g - 1))
            eng.tensor_tensor(hot[:, :, :], col(m, "iota32").unsqueeze(1).broadcast_to(sh), bc(idxf[:, :], sh),
                              ALU.is_equal).then_inc(hot_sb.sem, 1)

        def keep(g):
            for c in range(NC):
                eng.wait_ge(mask_ps.sem, mask_ps.at(g, c + 1))
                eng.wait_ge(hid_sb.sem, hid_sb.at(g, c + 1))
                if c == 0:
                    eng.wait_ge(out_ps.sem, out_ps.at(g - 1))
                eng.tensor_tensor(kept[c][:, :], m.ps[:, MASK_BANKS[c], :], hid[c][:, :], ALU.mult).then_inc(kept_sb.sem, 1)

        def turned_hot(g, b):
            eng.wait_ge(hotT_ps.sem, hotT_ps.at(g))
            eng.wait_ge(hotT_sb.sem, hotT_sb.at(g))
            eng.wait_ge(mask_ps.sem, mask_ps.at(g - 1))
            eng.tensor_copy(hotT16[:, :], m.ps[0:E, 1, :]).then_inc(hotT16_sb.sem, 1)

        def result(g, b):
            eng.wait_ge(out_ps.sem, out_ps.at(g))
            eng.wait_ge(stored[b], store_value(g, b))
            eng.scalar_tensor_tensor(out=res[b][:, :, :], in0=m.ps[:, 6, :].rearrange("p (s c) -> p s c", s=TS)[:, :, 0:C],
                                     scalar=0.0, in1=m.h[:, bass.ds(g * TS, TS), :], op0=ALU.max,
                                     op1=ALU.add).then_inc(res_sb.sem, 1)

        def rest(g, b, left, back):
            if back:
                keep(g - 1)
            if left is not None:
                choose(g, b)
            if left:
                T.dve(eng, g + 1, 1 - b)
            if left is not None:
                turned_hot(g, b)
            if back:
                result(g - 1, 1 - b)

        eng.tensor_copy(sel[:, :], col(m, "sel32", slice(0, E))).then_inc(sel_sb, 1)
        rout.make(eng, col(m, "routw"))
        w1.make(eng, col(m, "fw1"))
        lagged(eng, TG, lambda g, b: T.dve(eng, g, b), rest)

    def store_value(g, b):
        return (g - b) * 8 + 16

    def act(eng):
        def rest(g, b, left, back):
            if back:
                for c in range(NC):
                    eng.wait_ge(hid_ps.sem, hid_ps.at(g - 1, c + 1))
                    if c == 0:
                        eng.wait_ge(kept_sb.sem, kept_sb.at(g - 2))
                    nc.scalar.activation(hid[c][:, :], m.ps[:, 2 + c % 2, :], ACT.Relu,
                                         bias=m.cst[:, AT["fb1"][0] + c:AT["fb1"][0] + c + 1]).then_inc(hid_sb.sem, 1)
            if left:
                T.act(eng, g + 1, 1 - b, hid_ps)
            if left is not None:
                eng.wait_ge(hotT_ps.sem, hotT_ps.at(g))
                eng.wait_ge(out_ps.sem, out_ps.at(g - 2))
                nc.scalar.activation(hotT[b][:, :], m.ps[0:E, 1, :], ACT.Identity).then_inc(hotT_sb.sem, 1)

        lagged(eng, TG, lambda g, b: T.act(eng, g, b, hid_ps), rest)

    m.ahead_of_stores = stored
    return dict(sp=sp, pool=pool, pe=pe, dve=dve, act=act)


PHASES = [tokenizer, norm("n1", twice=True), attention0, norm("n2"), mlp0, norm("n3"), experts0, norm("n5"),
          attention1, norm("n6"), experts1]


def audio_tower_kernel(nc, x, cst, ew1, ew2, out):
    with ExitStack() as ctx:
        m = Memory()
        m.x, m.ended, m.raised, m.ahead_of_stores = x, [], [], []
        m.cst = ctx.enter_context(nc.sbuf_tensor("cst", [P, NCOL], F32))
        m.h = ctx.enter_context(nc.sbuf_tensor("h", [P, S, C], F32))
        m.y = ctx.enter_context(nc.sbuf_tensor("y", [P, S, C], F32))
        m.stat = ctx.enter_context(nc.sbuf_tensor("stat", [P, S, 6], F32))
        m.eps = ctx.enter_context(nc.sbuf_tensor("eps", [P, 1], F32))
        m.ps = ctx.enter_context(nc.psum_tensor("ps", [P, 8, 512], F32))
        m.cst_sem = ctx.enter_context(nc.semaphore("constants_loaded"))
        m.cst2_sem = ctx.enter_context(nc.semaphore("layer_constants_loaded"))
        m.eps_sem = ctx.enter_context(nc.semaphore("eps_set"))
        m.waited = ctx.enter_context(nc.semaphore("waits_alone"))
        m.dve_pre = ctx.enter_context(nc.semaphore("dve_pre"))
        m.out, m.ew1, m.ew2 = out, ew1, ew2
        m.norm_tiles = [ctx.enter_context(nc.sbuf_tensor(f"norm_{n}", [P, S], F32)) for n in
                        ("diff", "m2", "dd", "var", "dev", "tmp", "mean", "rstd", "rstd2")]
        m.split = {n: Split(nc, ctx, n, AT[n][1]) for n in ("wkv2", "wq2", "wtok", "wm1", "gatew", "routw", "fw1")}
        m.ew1_hi = ctx.enter_context(nc.sbuf_tensor("ew1_hi", [P, EXPERTS0 * F0], F32R))
        m.ew1_lo = ctx.enter_context(nc.sbuf_tensor("ew1_lo", [P, EXPERTS0 * F0], F32R))
        m.ew1_f = ctx.enter_context(nc.sbuf_tensor("ew1_f", [P, EXPERTS0 * F0], F32))
        m.ew2_sb = ctx.enter_context(nc.sbuf_tensor("ew2_sb", [P, EXPERTS0 * C + C], F32))
        m.ew1_sem, m.ew2_sem, m.ew2_pad, m.ew_split = (
            ctx.enter_context(nc.semaphore(n)) for n in ("ew1_loaded", "ew2_loaded", "ew2_padded", "ew1_split"))

        def load_layers(eng):
            eng.dma_start(m.cst[:, TOK_END:NCOL], cst[:, TOK_END:NCOL]).then_inc(m.cst2_sem, 16)
            eng.dma_start(m.ew1_f[:, :], ew1).then_inc(m.ew1_sem, 16)
            eng.dma_start(m.ew2_sb[:, 0:EXPERTS0 * C], ew2).then_inc(m.ew2_sem, 16)

        m.load_layers = load_layers
        phases = []
        for make in PHASES:
            with ExitStack() as m.mem:
                m.steps = []
                phases.append(make(nc, ctx, m))
            m.ended += m.steps
        block = ctx.enter_context(nc.Block())

        @block.sync
        def _(eng):
            eng.dma_start(m.cst[:, 0:TOK_END], cst[:, 0:TOK_END]).then_inc(m.cst_sem, 16)
            for step in m.raised:
                eng.sem_inc(step.sem, step.start)
            for sem in m.ahead_of_stores:
                eng.sem_inc(sem, 16)
            for p in phases:
                if "sp" in p:
                    p["sp"](eng)

        @block.gpsimd
        def _(eng):
            eng.memset(m.ew2_sb[:, EXPERTS0 * C:], 0.0).then_inc(m.ew2_pad, 1)
            eng.memset(m.eps[:, :], EPS).then_inc(m.eps_sem, 1)
            for p in phases:
                if "pool" in p:
                    p["pool"](eng)

        @block.tensor
        def _(eng):
            for p in phases:
                if "pe" in p:
                    p["pe"](eng)

        @block.vector
        def _(eng):
            for p in phases:
                if "dve" in p:
                    p["dve"](eng)

        @block.scalar
        def _(eng):
            eng.wait_ge(m.cst_sem, 16)
            eng.wait_ge(m.eps_sem, 1)
            for p in phases:
                if "act" in p:
                    p["act"](eng)


def constants(i):
    import numpy as np

    c = np.zeros((P, NCOL), np.float32)

    def put(name, a, row=0):
        at, w = AT[name]
        a = np.asarray(a)
        a = a.reshape(a.shape[0], -1)
        c[row:row + a.shape[0], at:at + a.shape[1]] = a

    def rows(name, v):
        put(name, np.broadcast_to(np.asarray(v).reshape(1, -1), (P, np.asarray(v).size)))

    def tok(n):
        return np.asarray(i["L0_tok_" + n])

    put("ident", np.eye(P, dtype=np.float32))
    rows("g1r", np.tile(tok("g1"), 8)), rows("v1r", np.tile(tok("v1"), 8))
    rows("g2r", np.tile(tok("g2"), 2)), rows("v2r", np.tile(tok("v2"), 2))
    for n, reps in ((1, 8), (2, 2), (3, 1)):
        for k in ("b", "m", "g", "be", "v"):
            put(f"{k}{n}", np.tile(tok(f"{k}{n}"), reps)[:, None])
    w1, w2, w3 = (tok(n) for n in ("w1", "w2", "w3"))
    a = np.zeros((3, 8, 2, 8, 16), np.float32)
    for s in range(8):
        a[:, s, :, s, :] = w1.transpose(2, 1, 0)
    put("w1", a.reshape(48, P))
    a = np.zeros((3, 2, 16, 2, 64), np.float32)
    for s in range(2):
        a[:, s, :, s, :] = w2.transpose(2, 1, 0)
    put("w2", a.reshape(96, P))
    put("gamma", np.broadcast_to(tok("gamma"), (P, 1)))
    for s in range(2):
        put(f"wq{s}", np.pad(tok("wq").T, ((0, 0), (64 * s, 56 - 64 * s + 64))), 64 * s)
        put(f"bq{s}", tok("bq")[:, None], 64 * s)
        put("bk", tok("bk")[:, None], 64 * s)
    a = np.zeros((2, 64, 2, 64), np.float32)
    b = np.zeros((2, 64, 2, 64), np.float32)
    for s in range(2):
        a[s, :, s, :8] = tok("wk").T
        b[s, :, s, :] = tok("wv").T
    put("wk", a.reshape(P, P)), put("wv", b.reshape(P, P))
    rows("bvr", np.tile(tok("bv"), 2))
    a = np.zeros((2, 64, 2, 4, P), np.float32)
    for s in range(2):
        a[s, :, s] = w3.transpose(1, 2, 0)
    put("w3", a.reshape(P, 8 * P))
    more_constants(i, put, rows)
    return c


def kernel(**inputs):
    import numpy as np
    import concourse.bacc as bacc
    from concourse.bass_utils import run_bass_kernel_spmd as run

    nc = bacc.Bacc("TRN2", target_bir_lowering=False, num_devices=1)
    x = np.asarray(inputs["x"]).reshape(S, 2, L)
    ew1, ew2 = expert_layout(inputs)
    arrays = {"x_dram": np.pad(x, ((0, 0), (0, 0), (1, 1))), "cst_dram": constants(inputs),
              "ew1_dram": ew1, "ew2_dram": ew2}
    args = [nc.dram_tensor(n, a.shape, F32, kind="ExternalInput").ap() for n, a in arrays.items()]
    args.append(nc.dram_tensor("out_dram", (S, P, C), F32, kind="ExternalOutput").ap())
    audio_tower_kernel(nc, *args)
    r = run(nc, [arrays], core_ids=[0])
    return r.results[0]["out_dram"]


def more_constants(i, put, rows):
    import numpy as np

    def twice(name, a):
        put(name, np.concatenate([a, a]))

    def a0(n):
        return np.asarray(i["L0_attn_" + n])

    def f0(n):
        return np.asarray(i["L0_ffn_" + n])

    def a1(n):
        return np.asarray(i["L1_attn_" + n])

    def f1(n):
        return np.asarray(i["L1_ffn_" + n])

    twice("n1g", a0("norm1_g")[:, None]), twice("n1b", a0("norm1_b")[:, None])
    twice("n2g", a0("norm2_g")[:, None]), twice("n2b", a0("norm2_b")[:, None])
    wq, wkv = a0("Wq").T, a0("Wkv").T
    twice("wkv2", wkv), twice("wq2", wq[:, :8]), twice("wtok", np.concatenate([wkv, wq], 1))
    put("wproj", np.concatenate([a0("Wproj").T, a0("bproj")[None]]))
    head = np.arange(C) // 8
    put("headmask", ((head[:, None] == head[None]) & (head[:, None] > 0)).astype(np.float32))
    twice("wm1", a0("W1").T)
    put("bm1", a0("b1").reshape(2, P).T)
    put("wm2", a0("W2").T.reshape(2, P, C).transpose(1, 0, 2))
    rows("bm2r", a0("b2"))
    twice("gatew", f0("gate_w")), rows("gatebr", f0("gate_b"))
    rows("iota16", np.arange(EXPERTS0, dtype=np.float32))
    put("eb1", f0("b1").T), put("eb2", f0("b2"))
    rows("gamr", f0("gamma")), rows("betr", f0("beta"))

    def heads(w):
        w = w.reshape(C, HEADS, C).transpose(2, 1, 0)
        return np.stack([w, w], 2)

    put("wkT", heads(a1("WK"))), put("wvT", heads(a1("WV")))
    put("wqT", a1("WQ").reshape(C, HEADS, C).transpose(2, 1, 0))
    put("wout", a1("Wout").reshape(HEADS, C, C).transpose(1, 0, 2))
    rows("boutr", a1("bout"))
    twice("routw", f1("router_w").T), rows("routbr", f1("router_b"))
    rows("iota32", np.arange(EXPERTS1, dtype=np.float32))
    twice("fw1", f1("W1").transpose(1, 0, 2).reshape(C, HID1))
    put("fb1", f1("b1").reshape(4, P).T)
    put("fw2", f1("W2").reshape(4, P, C).transpose(1, 0, 2))
    put("fb2", f1("b2"))
    put("sel32", (np.arange(EXPERTS1)[:, None] == np.arange(HID1)[None] // F1).astype(np.float32))


def expert_layout(i):
    import numpy as np

    w1 = np.asarray(i["L0_ffn_w1"]).transpose(1, 0, 2).reshape(C, EXPERTS0 * F0)
    return np.concatenate([w1, w1]), np.asarray(i["L0_ffn_w2"]).transpose(1, 0, 2).reshape(F0, EXPERTS0 * C)
```
